# Optimizing a Trainium2 kernel written in Bass

```python
import numpy as np
import jax
import jax.numpy as jnp

def _softmax(x, axis=-1):
    return jax.nn.softmax(x, axis=axis)

def _gelu(x):
    return jax.nn.gelu(x, approximate=True)

def _silu(x):
    return jax.nn.silu(x)

def _sigmoid(x):
    return jax.nn.sigmoid(x)

def _layernorm(x, axis=-1, eps=1e-05):
    m = jnp.mean(x, axis=axis, keepdims=True)
    v = jnp.var(x, axis=axis, keepdims=True)
    return (x - m) / jnp.sqrt(v + eps)

def _scatter_add(tgt, idx, src, axis=0):
    return tgt.at[idx].add(src)

def _segment_sum(src, seg, n):
    return jax.ops.segment_sum(src, seg, n)
kernel_name = 'mk_flamingo_gated_d2_seqx_r4_811605'

def setup_inputs(seed: int=0):
    np.random.seed(seed)
    _w = jnp.asarray

    def _rec_inputs():
        import jax
        import jax.numpy as jnp
        _rk = jax.random.key(seed)
        x = -0.0002928 + 1 * jax.random.normal(jax.random.fold_in(_rk, 1), (2, 1024, 256), jnp.float32)
        _lenS = 1024 - jax.random.randint(jax.random.fold_in(_rk, 7), (2,), 0, max(1, 1024 // 4) + 1, jnp.int32)
        _lenS2 = 77 - jax.random.randint(jax.random.fold_in(_rk, 8), (2,), 0, max(1, 77 // 4) + 1, jnp.int32)
        _ctx_1024P = jax.random.normal(jax.random.fold_in(_rk, 11), (2, 16, 256), jnp.float32)
        _ctx_1024c = jax.random.dirichlet(jax.random.fold_in(_rk, 511), 0.3 * jnp.ones((16,), jnp.float32), (2, 77))
        _ctx_1024t = jnp.einsum('bsk,bkd->bsd', _ctx_1024c, _ctx_1024P)
        _ctx_1024t = _ctx_1024t * jax.lax.rsqrt(jnp.mean(jnp.square(_ctx_1024t)) + 1e-12) * 0.953939
        ctx_1024 = -1.39393e-06 + 0.999914 * (_ctx_1024t + 0.3 * jax.random.normal(jax.random.fold_in(_rk, 611), (2, 77, 256), jnp.float32))
        _g = jax.random.normal(jax.random.fold_in(_rk, 9001), (2, 2), jnp.float32)
        _g = jnp.sign(_g) * jnp.maximum(jnp.abs(_g), 1.0) + (_g == 0) * 1.0
        g_xattn = _g[0]
        g_ffn = _g[1]
        return (x, ctx_1024, g_xattn, g_ffn)
    x, ctx_1024, g_xattn, g_ffn = _rec_inputs()

    def _L0_xattn_setup():
        import jax, jax.numpy as jnp
        import numpy as np
        EMBED_DIM = 256
        NUM_HEADS = 16
        DEPTH = EMBED_DIM // NUM_HEADS

        def _split_heads(x):
            B, S, _ = x.shape
            return x.reshape(B, S, NUM_HEADS, DEPTH).transpose(0, 2, 1, 3)
        key = jax.random.key(seed)
        ks = jax.random.split(key, 11)
        B, S, D = (2, 512, EMBED_DIM)
        scale = 1.0 / np.sqrt(D)
        inp = {'q': jax.random.normal(ks[0], (B, S, D), jnp.float32), 'k': jax.random.normal(ks[1], (B, S, D), jnp.float32), 'v': jax.random.normal(ks[2], (B, S, D), jnp.float32), 'Wq': jax.random.normal(ks[3], (D, D), jnp.float32) * scale, 'bq': jnp.zeros((D,), jnp.float32), 'Wk': jax.random.normal(ks[4], (D, D), jnp.float32) * scale, 'bk': jnp.zeros((D,), jnp.float32), 'Wv': jax.random.normal(ks[5], (D, D), jnp.float32) * scale, 'bv': jnp.zeros((D,), jnp.float32), 'Wo': jax.random.normal(ks[6], (D, D), jnp.float32) * scale, 'bo': jnp.zeros((D,), jnp.float32)}
        return inp
    _L0_xattn_all = _L0_xattn_setup()
    _L0_xattn_in = {k: v for k, v in _L0_xattn_all.items() if k in ('Wq', 'bq', 'Wk', 'bk', 'Wv', 'bv', 'Wo', 'bo')}
    del _L0_xattn_all

    def _L0_ffn_setup():
        import jax, jax.numpy as jnp
        import numpy as np
        NUM_EXPERTS = 8
        TOP_K = 2
        key = jax.random.key(seed)
        ks = jax.random.split(key, 4)
        B, S, H, F = (4, 1024, 256, 1024)
        x = jax.random.normal(ks[0], (B, S, H), dtype=jnp.float32)
        router_w = jax.random.normal(ks[1], (H, NUM_EXPERTS), dtype=jnp.float32) * 0.02
        w1 = jax.random.normal(ks[2], (H, F), dtype=jnp.float32) * 0.02
        b1 = jnp.zeros((F,), dtype=jnp.float32)
        w2 = jax.random.normal(ks[3], (F, H), dtype=jnp.float32) * 0.02
        b2 = jnp.zeros((H,), dtype=jnp.float32)
        return {'x': x, 'router_w': router_w, 'w1': w1, 'b1': b1, 'w2': w2, 'b2': b2}
    _L0_ffn_all = _L0_ffn_setup()
    _L0_ffn_in = {k: v for k, v in _L0_ffn_all.items() if k in ('router_w', 'w1', 'b1', 'w2', 'b2')}
    del _L0_ffn_all

    def _L1_xattn_setup():
        import jax, jax.numpy as jnp
        import numpy as np
        EMBED_DIM = 256
        NUM_HEADS = 16
        HEAD_DIM = EMBED_DIM // NUM_HEADS
        N, S = (4, 512)
        key = jax.random.key(seed)
        ks = jax.random.split(key, 11)
        s = 1.0 / np.sqrt(EMBED_DIM)
        inp = {'query': jax.random.normal(ks[0], (N, S, EMBED_DIM), jnp.float32), 'key': jax.random.normal(ks[1], (N, S, EMBED_DIM), jnp.float32), 'value': jax.random.normal(ks[2], (N, S, EMBED_DIM), jnp.float32), 'wq': jax.random.normal(ks[3], (EMBED_DIM, EMBED_DIM), jnp.float32) * s, 'bq': jnp.zeros((EMBED_DIM,), jnp.float32), 'wk': jax.random.normal(ks[4], (EMBED_DIM, EMBED_DIM), jnp.float32) * s, 'bk': jnp.zeros((EMBED_DIM,), jnp.float32), 'wv': jax.random.normal(ks[5], (EMBED_DIM, EMBED_DIM), jnp.float32) * s, 'bv': jnp.zeros((EMBED_DIM,), jnp.float32), 'wo': jax.random.normal(ks[6], (EMBED_DIM, EMBED_DIM), jnp.float32) * s, 'bo': jnp.zeros((EMBED_DIM,), jnp.float32)}
        return inp
    _L1_xattn_all = _L1_xattn_setup()
    _L1_xattn_in = {k: v for k, v in _L1_xattn_all.items() if k in ('wq', 'bq', 'wk', 'bk', 'wv', 'bv', 'wo', 'bo')}
    del _L1_xattn_all

    def _L1_ffn_setup():
        import jax, jax.numpy as jnp
        import numpy as np
        E = 8
        H = 256
        M = 512
        K = 2
        SE = 1
        BSZ, SEQ = (2, 256)
        W_SCALE = 0.02
        key = jax.random.key(seed)
        ks = jax.random.split(key, 9)
        return {'x': jax.random.normal(ks[0], (BSZ, SEQ, H), jnp.float32), 'gate_w': jax.random.normal(ks[1], (E, H), jnp.float32) * W_SCALE, 'beta': jnp.zeros((E,), jnp.float32), 'gate_proj_w': jax.random.normal(ks[2], (E, H, M), jnp.float32) * W_SCALE, 'up_proj_w': jax.random.normal(ks[3], (E, H, M), jnp.float32) * W_SCALE, 'down_proj_w': jax.random.normal(ks[4], (E, M, H), jnp.float32) * W_SCALE, 'shared_gate_w': jax.random.normal(ks[5], (SE, H, M), jnp.float32) * W_SCALE, 'shared_up_w': jax.random.normal(ks[6], (SE, H, M), jnp.float32) * W_SCALE, 'shared_down_w': jax.random.normal(ks[7], (SE, M, H), jnp.float32) * W_SCALE}
    _L1_ffn_all = _L1_ffn_setup()
    _L1_ffn_in = {k: v for k, v in _L1_ffn_all.items() if k in ('gate_w', 'beta', 'gate_proj_w', 'up_proj_w', 'down_proj_w', 'shared_gate_w', 'shared_up_w', 'shared_down_w')}
    del _L1_ffn_all
    return {'x': x, 'ctx_1024': ctx_1024, 'g_xattn': g_xattn, 'g_ffn': g_ffn, 'L0_xattn_Wq': _L0_xattn_in['Wq'], 'L0_xattn_bq': _L0_xattn_in['bq'], 'L0_xattn_Wk': _L0_xattn_in['Wk'], 'L0_xattn_bk': _L0_xattn_in['bk'], 'L0_xattn_Wv': _L0_xattn_in['Wv'], 'L0_xattn_bv': _L0_xattn_in['bv'], 'L0_xattn_Wo': _L0_xattn_in['Wo'], 'L0_xattn_bo': _L0_xattn_in['bo'], 'L0_ffn_router_w': _L0_ffn_in['router_w'], 'L0_ffn_w1': _L0_ffn_in['w1'], 'L0_ffn_b1': _L0_ffn_in['b1'], 'L0_ffn_w2': _L0_ffn_in['w2'], 'L0_ffn_b2': _L0_ffn_in['b2'], 'L1_xattn_wq': _L1_xattn_in['wq'], 'L1_xattn_bq': _L1_xattn_in['bq'], 'L1_xattn_wk': _L1_xattn_in['wk'], 'L1_xattn_bk': _L1_xattn_in['bk'], 'L1_xattn_wv': _L1_xattn_in['wv'], 'L1_xattn_bv': _L1_xattn_in['bv'], 'L1_xattn_wo': _L1_xattn_in['wo'], 'L1_xattn_bo': _L1_xattn_in['bo'], 'L1_ffn_gate_w': _L1_ffn_in['gate_w'], 'L1_ffn_beta': _L1_ffn_in['beta'], 'L1_ffn_gate_proj_w': _L1_ffn_in['gate_proj_w'], 'L1_ffn_up_proj_w': _L1_ffn_in['up_proj_w'], 'L1_ffn_down_proj_w': _L1_ffn_in['down_proj_w'], 'L1_ffn_shared_gate_w': _L1_ffn_in['shared_gate_w'], 'L1_ffn_shared_up_w': _L1_ffn_in['shared_up_w'], 'L1_ffn_shared_down_w': _L1_ffn_in['shared_down_w']}

def reference(x, ctx_1024, g_xattn, g_ffn, L0_xattn_Wq, L0_xattn_bq, L0_xattn_Wk, L0_xattn_bk, L0_xattn_Wv, L0_xattn_bv, L0_xattn_Wo, L0_xattn_bo, L0_ffn_router_w, L0_ffn_w1, L0_ffn_b1, L0_ffn_w2, L0_ffn_b2, L1_xattn_wq, L1_xattn_bq, L1_xattn_wk, L1_xattn_bk, L1_xattn_wv, L1_xattn_bv, L1_xattn_wo, L1_xattn_bo, L1_ffn_gate_w, L1_ffn_beta, L1_ffn_gate_proj_w, L1_ffn_up_proj_w, L1_ffn_down_proj_w, L1_ffn_shared_gate_w, L1_ffn_shared_up_w, L1_ffn_shared_down_w):
    import jax
    import jax.numpy as jnp

    def _L0_xattn_ref(q, k, v, Wq, bq, Wk, bk, Wv, bv, Wo, bo):
        import jax, jax.numpy as jnp
        import numpy as np
        EMBED_DIM = 256
        NUM_HEADS = 16
        DEPTH = EMBED_DIM // NUM_HEADS

        def _split_heads(x):
            B, S, _ = x.shape
            return x.reshape(B, S, NUM_HEADS, DEPTH).transpose(0, 2, 1, 3)
        query = _split_heads(q @ Wq + bq)
        key_ = _split_heads(k @ Wk + bk)
        value = _split_heads(v @ Wv + bv)
        logits = jnp.einsum('bhqd,bhkd->bhqk', query, key_) / jnp.sqrt(jnp.asarray(DEPTH, query.dtype))
        attn = jax.nn.softmax(logits, axis=-1)
        out = jnp.einsum('bhqk,bhkd->bhqd', attn, value)
        B, H, S, d = out.shape
        concat = out.transpose(0, 2, 1, 3).reshape(B, S, H * d)
        return concat @ Wo + bo

    def _L0_ffn_ref(x, router_w, w1, b1, w2, b2):
        import jax, jax.numpy as jnp
        import numpy as np
        NUM_EXPERTS = 8
        TOP_K = 2
        B, S, H = x.shape
        xt = x.reshape(-1, H)
        router_logits = jnp.matmul(xt, router_w)
        router_probs = jax.nn.softmax(router_logits, axis=-1)
        top_k_probs, top_k_indices = jax.lax.top_k(router_probs, TOP_K)
        top_k_probs = top_k_probs / jnp.sum(top_k_probs, axis=-1, keepdims=True)
        one_hot = jax.nn.one_hot(top_k_indices, NUM_EXPERTS, dtype=xt.dtype)
        combine = jnp.einsum('tk,tke->te', top_k_probs, one_hot)
        expert_out = jnp.matmul(jax.nn.gelu(jnp.matmul(xt, w1) + b1), w2) + b2
        out = expert_out * jnp.sum(combine, axis=-1, keepdims=True)
        return out.reshape(B, S, H)

    def _L1_xattn_ref(query, key, value, wq, bq, wk, bk, wv, bv, wo, bo):
        import jax, jax.numpy as jnp
        import numpy as np
        EMBED_DIM = 256
        NUM_HEADS = 16
        HEAD_DIM = EMBED_DIM // NUM_HEADS
        N, S = (4, 512)
        n = query.shape[0]
        Q = query @ wq.T + bq
        K = key @ wk.T + bk
        V = value @ wv.T + bv
        Q = Q.reshape(n, -1, NUM_HEADS, HEAD_DIM).transpose(0, 2, 1, 3)
        K = K.reshape(n, -1, NUM_HEADS, HEAD_DIM).transpose(0, 2, 1, 3)
        V = V.reshape(n, -1, NUM_HEADS, HEAD_DIM).transpose(0, 2, 1, 3)
        energy = jnp.einsum('nhqd,nhkd->nhqk', Q, K)
        attn = jax.nn.softmax(energy / jnp.sqrt(jnp.float32(HEAD_DIM)), axis=-1)
        out = jnp.einsum('nhqk,nhkd->nhqd', attn, V)
        out = out.transpose(0, 2, 1, 3).reshape(n, -1, NUM_HEADS * HEAD_DIM)
        return out @ wo.T + bo

    def _L1_ffn_ref(x, gate_w, beta, gate_proj_w, up_proj_w, down_proj_w, shared_gate_w, shared_up_w, shared_down_w):
        import jax, jax.numpy as jnp
        import numpy as np
        E = 8
        H = 256
        M = 512
        K = 2
        SE = 1
        BSZ, SEQ = (2, 256)
        W_SCALE = 0.02
        B0, S0, H0 = x.shape
        xt = x.reshape(-1, H0)
        B = xt.shape[0]
        logits = xt @ gate_w.T
        _, idx = jax.lax.top_k(logits + beta, K)
        probs = jax.nn.sigmoid(jnp.take_along_axis(logits, idx, axis=-1))
        c = jnp.zeros((B, E), xt.dtype).at[jnp.arange(B)[:, None], idx].add(probs)
        g = jnp.einsum('bh,ehm->bem', xt, gate_proj_w)
        u = jnp.einsum('bh,ehm->bem', xt, up_proj_w)
        h = jax.nn.silu(g) * u
        eo = jnp.einsum('bem,emh->beh', h, down_proj_w)
        combined = jnp.einsum('beh,be->bh', eo, c)
        sg = jnp.einsum('bh,ehm->bem', xt, shared_gate_w)
        su = jnp.einsum('bh,ehm->bem', xt, shared_up_w)
        sh = jax.nn.silu(sg) * su
        shared_out = jnp.einsum('bem,emh->beh', sh, shared_down_w).sum(axis=1)
        return (combined + shared_out).reshape(B0, S0, H0)
    x = x + jnp.tanh(g_xattn[0]) * _L0_xattn_ref(_layernorm(x, axis=-1), ctx_1024, ctx_1024, L0_xattn_Wq, L0_xattn_bq, L0_xattn_Wk, L0_xattn_bk, L0_xattn_Wv, L0_xattn_bv, L0_xattn_Wo, L0_xattn_bo)
    x = x + jnp.tanh(g_ffn[0]) * _L0_ffn_ref(_layernorm(x, axis=-1), L0_ffn_router_w, L0_ffn_w1, L0_ffn_b1, L0_ffn_w2, L0_ffn_b2)
    x = x + jnp.tanh(g_xattn[1]) * _L1_xattn_ref(_layernorm(x, axis=-1), ctx_1024, ctx_1024, L1_xattn_wq, L1_xattn_bq, L1_xattn_wk, L1_xattn_bk, L1_xattn_wv, L1_xattn_bv, L1_xattn_wo, L1_xattn_bo)
    x = x + jnp.tanh(g_ffn[1]) * _L1_ffn_ref(_layernorm(x, axis=-1), L1_ffn_gate_w, L1_ffn_beta, L1_ffn_gate_proj_w, L1_ffn_up_proj_w, L1_ffn_down_proj_w, L1_ffn_shared_gate_w, L1_ffn_shared_up_w, L1_ffn_shared_down_w)
    return x

_drawn_inputs = setup_inputs


def setup_inputs(seed=0):
    import zlib

    import numpy as np

    out = dict(_drawn_inputs(seed))
    spreads = {'g_ffn': (-1.0, 0.6),
     'L0_xattn_bq': (0.0, 0.496),
     'L0_xattn_bk': (0.0, 0.8),
     'L0_xattn_bv': (0.0, 0.1),
     'L0_xattn_bo': (0.0, 0.1),
     'L0_ffn_b1': (0.0, 0.366),
     'L0_ffn_b2': (0.0, 0.1),
     'L1_xattn_bq': (0.0, 0.435),
     'L1_xattn_bk': (0.0, 0.8),
     'L1_xattn_bv': (0.0, 0.1),
     'L1_xattn_bo': (0.0, 0.1),
     'L1_ffn_beta': (0.0, 0.8)}
    factors = {'L0_ffn_router_w': 8.0,
     'L1_ffn_gate_w': 4.879,
     'L1_ffn_gate_proj_w': 4.442,
     'L1_ffn_up_proj_w': 4.406,
     'L1_ffn_down_proj_w': 4.379,
     'L1_ffn_shared_gate_w': 3.618,
     'L1_ffn_shared_up_w': 3.595,
     'L1_ffn_shared_down_w': 3.618}
    for name, (base, spread) in spreads.items():
        noise = np.random.default_rng([zlib.crc32(name.encode()), seed]).standard_normal(out[name].shape)
        drawn = base * np.exp(spread * noise) if base else spread * noise
        out[name] = jnp.asarray(drawn.astype(out[name].dtype))
    for name, factor in factors.items():
        out[name] = (out[name] * factor).astype(out[name].dtype)
    return out
```

```python
from contextlib import ExitStack

import concourse.bass as bass
from concourse import mybir

F32 = mybir.dt.float32
F32R = mybir.dt.float32r
F16 = mybir.dt.float16
BF16 = mybir.dt.bfloat16
ALU = mybir.AluOpType
ACT = mybir.ActivationFunctionType
AX = mybir.AxisListType

P = 128
D = 256
KD = D // P
B = 2
SEQ = 1024
SC = 77
T = B * SEQ
NT = T // P
BLK = 512
NB = T // BLK
TPB = BLK // P
H = 16
HD = D // H
HG = 8
G = H // HG
SW = HG * SC
SH = SW // 2
VW = HD + 1
NU = NT * G
UPB = TPB * G
F0 = 1024
M0 = F0 // P
E = 8
M1W = 512
M1 = M1W // P
EPS = 1e-5
KV_AFTER = 1
SCALE = 0.25

WA = 4 * KD * D
WF = KD * F0
WE = 2 * KD * M1W + M1 * D

COLS = {"bq0": 2, "bk0": 2, "b1": M0, "bq1": 2, "bk1": 2, "wr0": KD * E, "wr1": KD * E}
ROWS = {"bv0": D, "bo0": D, "b2": D, "bv1": D, "bo1": D}
EVERY = {"gates": 4, "beta": E}


def offsets(widths):
    at, n = {}, 0
    for name, w in widths.items():
        at[name] = (n, n + w)
        n += w
    return at, n


def flamingo(nc, x, ctx_t, cols, rows, every, wa0, w1, w2, wa1, w_in, w_down, out):
    col_at, n_cols = offsets(COLS)
    row_at, n_rows = offsets(ROWS)
    ev_at, n_every = offsets(EVERY)
    with ExitStack() as ctx:
        def sb(name, shape, dt, where=ctx):
            return where.enter_context(nc.sbuf_tensor(name, shape, dt))

        def sem(name):
            return ctx.enter_context(nc.semaphore(name))

        x_res = sb("x_res", [P, NT, D], F32)
        xnt_hi = sb("xnt_hi", [P, KD, T], F32R)
        xnt_lo = sb("xnt_lo", [P, KD, T], F32R)
        arena = sb("arena", [P, 4 * WE], F32R)
        raw = [sb(f"raw{i}", [P, WE], F32) for i in range(2)]
        kb_hi = sb("kb_hi", [P, G, B, HG, SC], F32R)
        kb_lo = sb("kb_lo", [P, G, B, HG, SC], F32R)
        v3 = sb("v3", [SC, B, 3, H, VW], BF16)
        ct_hi = sb("ct_hi", [P, KD, B * SC], F32R)
        ct_lo = sb("ct_lo", [P, KD, B * SC], F32R)
        colp = sb("colp", [P, n_cols], F32)
        ev = sb("ev", [P, n_every], F32)
        gate_t = sb("gate_t", [P, 4], F32)
        row_hi = sb("row_hi", [1, n_rows], F32R)
        row_lo = sb("row_lo", [1, n_rows], F32R)
        ones_row = sb("ones_row", [1, P], F32R)
        wr_hi = sb("wr_hi", [P, 2, KD, E], F32R)
        wr_lo = sb("wr_lo", [P, 2, KD, E], F32R)
        ident = sb("ident", [P, P], F32)
        head_mask = sb("head_mask", [P, HG], F32)
        xn = sb("xn", [P, TPB, D], F32)
        vrest = sb("vrest", [SC, B * D], F32)
        stats = sb("stats", [P, 2, 6], F32)
        mv = sb("mv", [P, NT, 2], F32)
        std = sb("std", [P, NT], F32)
        rstd = sb("rstd", [P, NT], F32)
        lg = sb("lg", [P, NT, E], F32)
        rt = [sb(f"rt{i}", [P, NT, E], F32) for i in range(3)]
        rs = [sb(f"rs{i}", [P, NT], F32) for i in range(4)]
        cw = sb("cw", [P, NT, E], F32)

        att = ExitStack()
        qt_hi = sb("qt_hi", [P, G, BLK], F32R, att)
        qt_lo = sb("qt_lo", [P, G, BLK], F32R, att)
        prob = sb("prob", [P, 2, HG, SC], F32, att)
        smax = sb("smax", [P, 2, HG], F32, att)
        pt_hi = sb("pt_hi", [SC, 2, 2, 4, P], F16, att)
        pt_lo = sb("pt_lo", [SC, 2, 2, 4, P], F16, att)
        o_n = sb("o_n", [P, 2, H, HD], F32, att)
        rsum = sb("rsum", [P, 2, H], F32, att)
        ot_hi = sb("ot_hi", [P, 2, KD, P], F32R, att)
        ot_lo = sb("ot_lo", [P, 2, KD, P], F32R, att)
        att.close()
        ffn = ExitStack()
        hf = sb("hf", [P, 2, BLK], F32, ffn)
        ht_hi = sb("ht_hi", [P, M0, BLK], F32R, ffn)
        ht_lo = sb("ht_lo", [P, M0, BLK], F32R, ffn)
        ffn.close()
        rts = ExitStack()
        sb("hf_again", [P, 2, BLK], F32, rts)
        rank = sb("rank", [P, NT, E, E], F32, rts)[:]
        cmp = sb("cmp", [P, NT, E, E], F32, rts)[:]
        rts.close()
        key_words = KD * B * SC
        key_space = xn[:].rearrange("p t d -> p (t d)")
        kf, kx_hi, kx_lo = (key_space[:, n * key_words:(n + 1) * key_words].rearrange("p (k n) -> p k n", k=KD)
                            for n in range(3))
        cst = ExitStack()
        ct_raw = sb("ct_raw", [P, KD, B * SC], F32, cst)
        row_raw = sb("row_raw", [1, n_rows], F32, cst)
        cst.close()

        bank = [ctx.enter_context(nc.psum_tensor(f"bank{i}", [P, BLK], F32)) for i in range(8)]

        wq = {}
        for layer, buf, at in ((0, arena, 0), (1, arena, 0)):
            for part, o in (("hi", 0), ("lo", WA)):
                wq[layer, part] = buf[:, at + o:at + o + WA].rearrange("p (w k n) -> p w k n", w=4, k=KD)
        w1_p = {part: arena[:, 2 * WA + o:2 * WA + o + WF].rearrange("p (k n) -> p k n", k=KD)
                for part, o in (("hi", 0), ("lo", WF))}
        w2_p = {part: arena[:, 2 * WA + 2 * WF + o:2 * WA + 2 * WF + o + WF].rearrange("p (k n) -> p k n", k=M0)
                for part, o in (("hi", 0), ("lo", WF))}

        def expert(buf, part):
            o = buf * 2 * WE + (WE if part == "lo" else 0)
            w = arena[:, o:o + WE]
            return (w[:, 0:2 * KD * M1W].rearrange("p (w k n) -> p w k n", w=2, k=KD),
                    w[:, 2 * KD * M1W:WE].rearrange("p (k n) -> p k n", k=M1))

        small_in = sem("small_in")
        x_in = [sem(f"x_in{i}") for i in range(NB)]
        raw_in = [sem(f"raw_in{i}") for i in range(2)]
        first_split = sem("first_split")
        split_done = sem("split_done")
        consts = sem("consts")
        pool_chain = sem("pool_chain")
        setup_dve = sem("setup_dve")
        gates_done = sem("gates_done")
        k_ready, v_ready = sem("k_ready"), sem("v_ready")
        k_biased = sem("k_biased")
        kx_done, kb_done, v_done = sem("kx_done"), sem("kb_done"), sem("v_done")
        v_chain = sem("v_chain")
        stats_done, var_done, std_done, rstd_done = sem("stats_done"), sem("var_done"), sem("std_done"), sem("rstd_done")
        xn_ready, xt_ready, xt_hi, xt_lo = sem("xn_ready"), sem("xt_ready"), sem("xt_hi"), sem("xt_lo")
        q_ready, q_hi, q_lo = sem("q_ready"), sem("q_hi"), sem("q_lo")
        s_ready, max_done, sub_done, exp_done = sem("s_ready"), sem("max_done"), sem("sub_done"), sem("exp_done")
        pt_ready, pt_hi_done, pt_lo_done = sem("pt_ready"), sem("pt_hi_done"), sem("pt_lo_done")
        pv_ready, rsum_done, o_done = sem("pv_ready"), sem("rsum_done"), sem("o_done")
        ot_ready, ot_hi_done, ot_lo_done = sem("ot_ready"), sem("ot_hi_done"), sem("ot_lo_done")
        op_ready, x_new = sem("op_ready"), sem("x_new")
        lg_ready, lg_copied, r_chain, r_act, c_done = (sem("lg_ready"), sem("lg_copied"), sem("r_chain"),
                                                       sem("r_act"), sem("c_done"))
        up_ready, act_done, h_done, hi_done, lo_done = (sem("up_ready"), sem("act_done"), sem("h_done"),
                                                        sem("hi_done"), sem("lo_done"))
        dn_ready, y_done = sem("dn_ready"), sem("y_done")
        stored = sem("stored")

        block = ctx.enter_context(nc.Block())

        PIECES = 4 + 1 + E

        def split_dst(p):
            if p == 0:
                return wq[0, "hi"], wq[0, "lo"], WA
            if p == 1:
                return w1_p["hi"], w1_p["lo"], WF
            if p == 2:
                return w2_p["hi"], w2_p["lo"], WF
            if p == 3:
                return wq[1, "hi"], wq[1, "lo"], WA
            o = (p + 1) % 2 * 2 * WE
            return arena[:, o:o + WE], arena[:, o + WE:o + 2 * WE], WE

        @block.sync
        def _(sp):
            sp.dma_start(colp[:], cols).then_inc(small_in, 16)
            sp.dma_start(ct_raw[:], ctx_t.rearrange("(k p) n -> p k n", p=P)).then_inc(small_in, 16)
            sp.dma_start(row_raw[:], rows).then_inc(small_in, 16)
            sp.dma_start(ev[:], every.partition_broadcast(P)).then_inc(small_in, 16)
            for i in range(NB):
                sp.dma_start(x_res[:, TPB * i:TPB * (i + 1), :],
                             x[BLK * i:BLK * (i + 1), :].rearrange("(t p) d -> p t d", p=P)).then_inc(x_in[i], 16)
                if i == 0:
                    sp.dma_start(raw[0][:, 0:WA].rearrange("p (w k n) -> p w k n", w=4, k=KD),
                                 wa0.rearrange("w (k p) n -> p w k n", p=P)).then_inc(raw_in[0], 16)
            for p in range(1, PIECES):
                if p == 2:
                    sp.wait_ge(first_split, 1)
                if p > 2:
                    sp.wait_ge(split_done, p - 2)
                to = raw[p % 2]
                if p == 1:
                    sp.dma_start(to[:, 0:WF].rearrange("p (k n) -> p k n", k=KD),
                                 w1.rearrange("(k p) n -> p k n", p=P)).then_inc(raw_in[p % 2], 16)
                elif p == 2:
                    sp.dma_start(to[:, 0:WF].rearrange("p (k n) -> p k n", k=M0),
                                 w2.rearrange("(k p) n -> p k n", p=P)).then_inc(raw_in[p % 2], 16)
                elif p == 3:
                    sp.dma_start(to[:, 0:WA].rearrange("p (w k n) -> p w k n", w=4, k=KD),
                                 wa1.rearrange("w (k p) n -> p w k n", p=P)).then_inc(raw_in[p % 2], 16)
                else:
                    sp.dma_start(to[:, 0:2 * KD * M1W].rearrange("p (w k n) -> p w k n", w=2, k=KD),
                                 w_in[p - 4].rearrange("w (k p) n -> p w k n", p=P)).then_inc(raw_in[p % 2], 16)
                    sp.dma_start(to[:, 2 * KD * M1W:WE].rearrange("p (k n) -> p k n", k=M1),
                                 w_down[p - 4].rearrange("(k p) n -> p k n", p=P)).then_inc(raw_in[p % 2], 16)
            for i in range(NB):
                sp.wait_ge(y_done, NT + NT * E + TPB * (i + 1))
                sp.dma_start(out[BLK * i:BLK * (i + 1), :].rearrange("(t p) d -> p t d", p=P),
                             x_res[:, TPB * i:TPB * (i + 1), :]).then_inc(stored, 16)
            sp.wait_ge(stored, 16 * NB)

        def raw_value(p):
            return 16 * sum(1 if q < 4 else 2 for q in range(p % 2, p + 1, 2))

        @block.gpsimd
        def _(pool):
            nc.gpsimd.memset(ident[:], 0.0).then_inc(pool_chain, 1)
            nc.gpsimd.memset(head_mask[:], 1.0).then_inc(pool_chain, 1)
            pool.wait_ge(pool_chain, 2)
            nc.gpsimd.affine_select(out=ident[:], in_=ident[:], compare_op=ALU.not_equal, fill=1.0, base=0,
                                    pattern=[[-1, P]], channel_multiplier=1).then_inc(consts, 1)
            nc.gpsimd.affine_select(out=head_mask[:], in_=head_mask[:], compare_op=ALU.is_ge, fill=0.0, base=0,
                                    pattern=[[-HD, HG]], channel_multiplier=1).then_inc(pool_chain, 1)
            pool.wait_ge(pool_chain, 3)
            nc.gpsimd.affine_select(out=head_mask[:], in_=head_mask[:], compare_op=ALU.is_ge, fill=0.0, base=HD - 1,
                                    pattern=[[HD, HG]], channel_multiplier=-1).then_inc(consts, 1)
            done = 3
            for p in range(1, PIECES):
                hi, lo, n = split_dst(p)
                pool.wait_ge(raw_in[p % 2], raw_value(p))
                if p == 3:
                    pool.wait_ge(op_ready, NT)
                if p == 4:
                    pool.wait_ge(dn_ready, NT)
                if p == 5:
                    pool.wait_ge(op_ready, 2 * NT)
                if p > 5:
                    pool.wait_ge(dn_ready, NT + NT * (p - 5))
                src = raw[p % 2][:, 0:n]
                if len(hi.shape) == 3:
                    src = src.rearrange("p (k n) -> p k n", k=hi.shape[1])
                if len(hi.shape) == 4:
                    src = src.rearrange("p (w k n) -> p w k n", w=4, k=KD)
                nc.gpsimd.tensor_copy(hi, src).then_inc(pool_chain, 1)
                done += 1
                pool.wait_ge(pool_chain, done)
                nc.gpsimd.tensor_tensor(lo, src, hi.bitcast(F32), ALU.subtract).then_inc(split_done, 1)

        @block.tensor
        def _(pe):
            def three(ps, w_hi, w_lo, m_hi, m_lo, start, stop, inc=None):
                nc.tensor.matmul(ps, w_lo, m_hi, start=start, stop=False)
                nc.tensor.matmul(ps, w_hi, m_lo, start=False, stop=False)
                return nc.tensor.matmul(ps, w_hi, m_hi, start=False, stop=stop)

            def kv(layer, k_bank, v_bank):
                w_hi, w_lo = wq[layer, "hi"], wq[layer, "lo"]
                for m in range(G):
                    for k in range(KD):
                        mm = three(k_bank[:, m * B * SC:(m + 1) * B * SC],
                                   w_hi[:, 1, k, m * P:(m + 1) * P], w_lo[:, 1, k, m * P:(m + 1) * P],
                                   ct_hi[:, k, :], ct_lo[:, k, :], k == 0, k == KD - 1)
                mm.then_inc(k_ready, 1)
                a, z = row_at[f"bv{layer}"]
                for b in range(B):
                    ps = v_bank[0:SC, b * D:(b + 1) * D]
                    for k in range(KD):
                        three(ps, ct_hi[:, k, b * SC:(b + 1) * SC], ct_lo[:, k, b * SC:(b + 1) * SC],
                              w_hi[:, 2, k, :], w_lo[:, 2, k, :], k == 0, False)
                    nc.tensor.matmul(ps, ones_row[:, 0:SC], row_lo[:, a:z], start=False, stop=False)
                    mm = nc.tensor.matmul(ps, ones_row[:, 0:SC], row_hi[:, a:z], start=False, stop=True)
                mm.then_inc(v_ready, 1)

            def attention(layer):
                w_hi, w_lo = wq[layer, "hi"], wq[layer, "lo"]
                bo = row_at[f"bo{layer}"]
                phase = 2 * layer
                work = bank[7]
                last_use = []

                def take_work():
                    if last_use:
                        pe.wait_ge(*last_use[-1])

                def x_transposed(i, c):
                    take_work()
                    for j in range(TPB):
                        if c == 0:
                            pe.wait_ge(xn_ready, NT * phase + TPB * i + j + 1)
                        mm = nc.tensor.transpose(work[:, j * P:(j + 1) * P], xn[:, j, c * P:(c + 1) * P], ident[:])
                    mm.then_inc(xt_ready, 1)
                    last_use.append((xt_lo, 2 * NB * phase + 2 * i + c + 1))

                def queries(i, m):
                    take_work()
                    pe.wait_ge(xt_lo, 2 * NB * phase + 2 * i + 2)
                    for k in range(KD):
                        mm = three(work[:], w_hi[:, 0, k, m * P:(m + 1) * P], w_lo[:, 0, k, m * P:(m + 1) * P],
                                   xnt_hi[:, k, i * BLK:(i + 1) * BLK], xnt_lo[:, k, i * BLK:(i + 1) * BLK],
                                   k == 0, k == KD - 1)
                    mm.then_inc(q_ready, 1)
                    last_use.append((q_lo, 2 * (NB * layer + i) + m + 1))

                def scores(n):
                    gn, i, g, b = NU * layer + n, n // UPB, n % G, n // (NU // B)
                    j = n % UPB // G
                    pe.wait_ge(q_lo, 2 * (NB * layer + i) + g + 1)
                    if gn >= 2:
                        pe.wait_ge(sub_done, gn - 1)
                    for half in range(2):
                        ps = bank[2 * (n % 2) + half][:, 0:SH].rearrange("p (h c) -> p h c", c=SC)
                        heads = slice(half * HG // 2, (half + 1) * HG // 2)
                        mm = three(ps, qt_hi[:, g, j * P:(j + 1) * P], qt_lo[:, g, j * P:(j + 1) * P],
                                   kb_hi[:, g, b, heads, :], kb_lo[:, g, b, heads, :], True, True)
                    mm.then_inc(s_ready, 1)

                def probs_transposed(n):
                    gn = NU * layer + n
                    pe.wait_ge(exp_done, gn + 1)
                    for q in range(2):
                        if gn >= 1:
                            pe.wait_ge(pt_lo_done, 2 * (gn - 1) + q + 1)
                        for h in range(4):
                            mm = nc.tensor.transpose(bank[4 + q][0:SC, h * P:(h + 1) * P],
                                                     prob[:, n % 2, 4 * q + h, :], ident[:])
                        mm.then_inc(pt_ready, 1)

                def values(n):
                    gn, b, g = NU * layer + n, n // (NU // B), n % G
                    if g == 0 and gn >= 2:
                        pe.wait_ge(o_done, gn // 2)
                    for q in range(2):
                        pe.wait_ge(pt_lo_done, 2 * gn + q + 1)
                        for h in range(4):
                            head = g * HG + 4 * q + h
                            ps = bank[6][:, head * VW:(head + 1) * VW]
                            hi, lo = pt_hi[:, n % 2, q, h, :], pt_lo[:, n % 2, q, h, :]
                            nc.tensor.matmul(ps, hi, v3[:, b, 2, head, :], start=True, stop=False)
                            nc.tensor.matmul(ps, hi, v3[:, b, 1, head, :], start=False, stop=False)
                            nc.tensor.matmul(ps, hi, v3[:, b, 0, head, :], start=False, stop=False)
                            nc.tensor.matmul(ps, lo, v3[:, b, 1, head, :], start=False, stop=False)
                            mm = nc.tensor.matmul(ps, lo, v3[:, b, 0, head, :], start=False, stop=True)
                    mm.then_inc(pv_ready, 1)

                def out_transposed(t):
                    gt = NT * layer + t
                    take_work()
                    pe.wait_ge(o_done, gt + 1)
                    flat = o_n[:, t % 2].rearrange("p h d -> p (h d)")
                    for c in range(KD):
                        mm = nc.tensor.transpose(work[:, c * P:(c + 1) * P], flat[:, c * P:(c + 1) * P], ident[:])
                    mm.then_inc(ot_ready, 1)
                    last_use.append((ot_lo_done, gt + 1))

                def out_projected(t):
                    gt = NT * layer + t
                    take_work()
                    ps = work[:, 0:D]
                    for k in range(KD):
                        three(ps, ot_hi[:, t % 2, k, :], ot_lo[:, t % 2, k, :],
                              w_hi[:, 3, k, :], w_lo[:, 3, k, :], k == 0, False)
                    nc.tensor.matmul(ps, ones_row[:], row_lo[:, bo[0]:bo[1]], start=False, stop=False)
                    nc.tensor.matmul(ps, ones_row[:], row_hi[:, bo[0]:bo[1]], start=False, stop=True)\
                        .then_inc(op_ready, 1)
                    last_use.append((x_new, gt + 1))

                x_transposed(0, 0)
                x_transposed(0, 1)
                queries(0, 0)
                queries(0, 1)
                pe.wait_ge(kb_done, 4 * (layer + 1))
                pe.wait_ge(v_done, layer + 1)
                for n in range(NU + 4):
                    i, u = n // UPB, n % UPB
                    if u == 7 and i + 1 < NB:
                        queries(i + 1, 0)
                    if n < NU:
                        scores(n)
                    if 1 <= n <= NU:
                        probs_transposed(n - 1)
                    if 2 <= n < NU + 2:
                        values(n - 2)
                    if n % 2 == 0 and 4 <= n < NU + 4:
                        out_transposed((n - 4) // 2)
                    if n % 2 == 1 and 5 <= n:
                        out_projected((n - 5) // 2)
                    if u == 6 and i + 1 < NB:
                        x_transposed(i + 1, 0)
                        x_transposed(i + 1, 1)
                    if u == 7 and i + 1 < NB:
                        queries(i + 1, 1)

            def prepare(which):
                phase = 2 * which + 1
                for i in range(NB):
                    for c in range(KD):
                        n = 2 * i + c
                        if n >= 4:
                            pe.wait_ge(xt_lo, 2 * NB * phase + n - 3)
                        for j in range(TPB):
                            if c == 0:
                                pe.wait_ge(xn_ready, NT * phase + TPB * i + j + 1)
                            mm = nc.tensor.transpose(bank[n % 4][:, j * P:(j + 1) * P], xn[:, j, c * P:(c + 1) * P],
                                                     ident[:])
                        mm.then_inc(xt_ready, 1)
                for t in range(NT):
                    if t % TPB == 0:
                        pe.wait_ge(xt_lo, 2 * NB * phase + 2 * (t // TPB) + 2)
                    for k in range(KD):
                        mm = three(bank[6][:, t * E:(t + 1) * E], xnt_hi[:, k, t * P:(t + 1) * P],
                                   xnt_lo[:, k, t * P:(t + 1) * P], wr_hi[:, which, k, :], wr_lo[:, which, k, :],
                                   k == 0, k == KD - 1)
                mm.then_inc(lg_ready, 1)

            def down(ps, hh, hl, w_hi, w_lo, ks, j, waits, bias=None):
                for k in range(ks):
                    if waits:
                        pe.wait_ge(lo_done, waits + k + 1)
                    mm = three(ps, hh[:, k, j * P:(j + 1) * P], hl[:, k, j * P:(j + 1) * P],
                               w_hi[:, k, :], w_lo[:, k, :], k == 0, k == ks - 1 and bias is None)
                if bias is not None:
                    nc.tensor.matmul(ps, ones_row[:], row_lo[:, bias[0]:bias[1]], start=False, stop=False)
                    mm = nc.tensor.matmul(ps, ones_row[:], row_hi[:, bias[0]:bias[1]], start=False, stop=True)
                return mm

            pe.wait_ge(setup_dve, 1)
            pe.wait_ge(consts, 2)
            kv(0, bank[4], bank[5])
            attention(0)
            prepare(0)
            pe.wait_ge(split_done, 2)
            for i in range(NB):
                for m in range(M0):
                    n = M0 * i + m
                    if n >= 4:
                        pe.wait_ge(act_done, n - 3)
                    for k in range(KD):
                        mm = three(bank[n % 4][:], w1_p["hi"][:, k, m * P:(m + 1) * P],
                                   w1_p["lo"][:, k, m * P:(m + 1) * P],
                                   xnt_hi[:, k, i * BLK:(i + 1) * BLK], xnt_lo[:, k, i * BLK:(i + 1) * BLK],
                                   k == 0, k == KD - 1)
                    mm.then_inc(up_ready, 1)
                if i == KV_AFTER:
                    pe.wait_ge(split_done, 3)
                    pe.wait_ge(lg_copied, 1)
                    kv(1, bank[7], bank[6])
                for j in range(TPB):
                    t = TPB * i + j
                    if t >= 2:
                        pe.wait_ge(y_done, t - 1)
                    for k in range(M0):
                        if j == 0:
                            pe.wait_ge(lo_done, M0 * i + k + 1)
                        three(bank[4 + t % 2][:, 0:D], ht_hi[:, k, j * P:(j + 1) * P], ht_lo[:, k, j * P:(j + 1) * P],
                              w2_p["hi"][:, k, :], w2_p["lo"][:, k, :], k == 0, False)
                    a, z = row_at["b2"]
                    nc.tensor.matmul(bank[4 + t % 2][:, 0:D], ones_row[:], row_lo[:, a:z], start=False, stop=False)
                    nc.tensor.matmul(bank[4 + t % 2][:, 0:D], ones_row[:], row_hi[:, a:z], start=False, stop=True)\
                        .then_inc(dn_ready, 1)

            attention(1)
            prepare(1)

            def expert_up(v):
                x, i = v // NB, v % NB
                (w_hi, _), (w_lo, _) = expert((x + 1) % 2, "hi"), expert((x + 1) % 2, "lo")
                if i == 0:
                    pe.wait_ge(split_done, 4 + x)
                for m in range(M1):
                    n = M1 * v + m
                    for w in range(2):
                        if n >= 2:
                            if w == 0:
                                pe.wait_ge(act_done, NB * M0 + n - 1)
                            else:
                                pe.wait_ge(h_done, n - 1)
                        for k in range(KD):
                            mm = three(bank[2 * w + n % 2][:], w_hi[:, w, k, m * P:(m + 1) * P],
                                       w_lo[:, w, k, m * P:(m + 1) * P], xnt_hi[:, k, i * BLK:(i + 1) * BLK],
                                       xnt_lo[:, k, i * BLK:(i + 1) * BLK], k == 0, k == KD - 1)
                        mm.then_inc(up_ready, 1)

            def expert_down(v):
                x = v // NB
                (_, w_hi), (_, w_lo) = expert((x + 1) % 2, "hi"), expert((x + 1) % 2, "lo")
                for j in range(TPB):
                    t = TPB * v + j
                    pe.wait_ge(y_done, NT + t - 1)
                    for k in range(M1):
                        if j == 0:
                            pe.wait_ge(lo_done, NB * M0 + M1 * v + k + 1)
                        slot = v % 2 * M1 + k
                        mm = three(bank[4 + t % 2][:, 0:D], ht_hi[:, slot, j * P:(j + 1) * P],
                                   ht_lo[:, slot, j * P:(j + 1) * P], w_hi[:, k, :], w_lo[:, k, :],
                                   k == 0, k == M1 - 1)
                    mm.then_inc(dn_ready, 1)

            for v in range(NB * (E + 1)):
                expert_up(v)
                if v >= 1:
                    expert_down(v - 1)
            expert_down(NB * (E + 1) - 1)

        @block.scalar
        def _(act):
            a, z = ev_at["gates"]
            act.wait_ge(small_in, 64)
            nc.scalar.activation(gate_t[:], ev[:, a:z], ACT.Tanh).then_inc(gates_done, 1)

            def bias_keys(layer):
                src = bank[4] if layer == 0 else bank[7]
                act.wait_ge(k_ready, layer + 1)
                for m in range(G):
                    c = col_at[f"bk{layer}"][0] + m
                    nc.scalar.activation(kf[:, m, :], src[:, m * B * SC:(m + 1) * B * SC], ACT.Identity,
                                         bias=colp[:, c:c + 1]).then_inc(k_biased, 1)

            def norm_std(phase):
                act.wait_ge(var_done, phase + 1)
                nc.scalar.activation(std[:], std[:], ACT.Sqrt).then_inc(std_done, 1)

            def xt_high(phase, i, c, src):
                n = 2 * NB * phase + 2 * i + c
                act.wait_ge(xt_ready, n + 1)
                nc.scalar.copy(xnt_hi[:, c, i * BLK:(i + 1) * BLK], src[:]).then_inc(xt_hi, 1)

            def attention(layer):
                def q_high(i, m):
                    n = 2 * (NB * layer + i) + m
                    act.wait_ge(q_ready, n + 1)
                    if i >= 1:
                        act.wait_ge(s_ready, NU * layer + UPB * i - 1 + m)
                    c = col_at[f"bq{layer}"][0] + m
                    nc.scalar.activation(qt_hi[:, m, :], bank[7][:], ACT.Identity, bias=colp[:, c:c + 1])\
                        .then_inc(q_hi, 1)

                xt_high(2 * layer, 0, 0, bank[7])
                xt_high(2 * layer, 0, 1, bank[7])
                q_high(0, 0)
                q_high(0, 1)
                for n in range(NU + 4):
                    i, u, gn = n // UPB, n % UPB, NU * layer + n
                    if u == 7 and i + 1 < NB:
                        q_high(i + 1, 0)
                    if n < NU:
                        act.wait_ge(sub_done, gn + 1)
                        nc.scalar.activation(prob[:, n % 2], prob[:, n % 2], ACT.Exp, scale=SCALE)\
                            .then_inc(exp_done, 1)
                    if 1 <= n <= NU:
                        for q in range(2):
                            act.wait_ge(pt_ready, 2 * (gn - 1) + q + 1)
                            if gn - 1 >= 2:
                                act.wait_ge(pv_ready, gn - 2)
                            nc.scalar.copy(pt_hi[:, (n - 1) % 2, q].rearrange("p h c -> p (h c)"),
                                           bank[4 + q][0:SC, :]).then_inc(pt_hi_done, 1)
                    if n % 2 == 0 and 4 <= n < NU + 4:
                        t = (n - 4) // 2
                        gt = NT * layer + t
                        act.wait_ge(ot_ready, gt + 1)
                        if gt >= 2:
                            act.wait_ge(op_ready, gt - 1)
                        nc.scalar.copy(ot_hi[:, t % 2].rearrange("p k c -> p (k c)"), bank[7][:, 0:D])\
                            .then_inc(ot_hi_done, 1)
                    if u == 6 and i + 1 < NB:
                        xt_high(2 * layer, i + 1, 0, bank[7])
                        xt_high(2 * layer, i + 1, 1, bank[7])
                    if u == 7 and i + 1 < NB:
                        q_high(i + 1, 1)

            def prepare(which):
                for i in range(NB):
                    for c in range(KD):
                        xt_high(2 * which + 1, i, c, bank[(2 * i + c) % 4])

            bias_keys(0)
            norm_std(0)
            attention(0)
            norm_std(1)
            prepare(0)
            act.wait_ge(r_chain, 2)
            nc.scalar.activation(rt[1][:], rt[0][:], ACT.Exp).then_inc(r_act, 1)
            for n in range(NB * M0):
                m = n % M0
                if n == (KV_AFTER + 1) * M0:
                    bias_keys(1)
                act.wait_ge(up_ready, n + 1)
                if n >= 2:
                    act.wait_ge(lo_done, n - 1)
                c = col_at["b1"][0] + m
                nc.scalar.activation(hf[:, n % 2, :], bank[n % 4][:], ACT.Gelu_apprx_tanh, bias=colp[:, c:c + 1])\
                    .then_inc(act_done, 1)
            norm_std(2)
            attention(1)
            norm_std(3)
            prepare(1)
            act.wait_ge(lg_copied, 2)
            nc.scalar.activation(rt[2][:], lg[:], ACT.Sigmoid).then_inc(r_act, 1)
            for n in range(NB * (E + 1) * M1):
                act.wait_ge(up_ready, NB * M0 + 2 * n + 1)
                if n >= 2:
                    act.wait_ge(lo_done, NB * M0 + n - 1)
                nc.scalar.activation(hf[:, n % 2, :], bank[n % 2][:], ACT.Silu).then_inc(act_done, 1)

        @block.vector
        def _(dve):
            v = nc.vector

            v.memset(v3[:], 0.0).then_inc(v_chain, 1)
            v.memset(ones_row[:].bitcast(F32), 1.0)
            dve.wait_ge(v_chain, 1)
            v.memset(v3[:, :, 0, :, HD:VW], 1.0).then_inc(v_chain, 1)
            dve.wait_ge(small_in, 64)
            v.tensor_copy(ct_hi[:], ct_raw[:]).then_inc(v_chain, 1)
            v.tensor_copy(row_hi[:], row_raw[:]).then_inc(v_chain, 1)
            a = col_at["wr0"][0]
            wr_raw = colp[:, a:a + 2 * KD * E].rearrange("p (w k e) -> p w k e", w=2, k=KD)
            v.tensor_copy(wr_hi[:], wr_raw).then_inc(v_chain, 1)
            dve.wait_ge(raw_in[0], 16)
            src = raw[0][:, 0:WA].rearrange("p (w k n) -> p w k n", w=4, k=KD)
            v.tensor_copy(wq[0, "hi"], src).then_inc(v_chain, 1)
            dve.wait_ge(v_chain, 6)
            v.tensor_tensor(ct_lo[:], ct_raw[:], ct_hi[:].bitcast(F32), ALU.subtract)
            v.tensor_tensor(row_lo[:], row_raw[:], row_hi[:].bitcast(F32), ALU.subtract)
            v.tensor_tensor(wr_lo[:], wr_raw, wr_hi[:].bitcast(F32), ALU.subtract)
            v.tensor_tensor(wq[0, "lo"], src, wq[0, "hi"].bitcast(F32), ALU.subtract).then_inc(first_split, 1)
            v.memset(ones_row[:].bitcast(F32), 1.0).then_inc(setup_dve, 1)

            def tile_stats(phase, t):
                n = NT * phase + t
                v.bn_stats(stats[:, t % 2, :], x_res[:, t, :]).then_inc(stats_done, 1)
                dve.wait_ge(stats_done, n + 1)
                return v.bn_aggr(mv[:, t, :], stats[:, t % 2, :])

            def norm_scale(phase, aggr):
                aggr.then_inc(rstd_done, 1)
                dve.wait_ge(rstd_done, 2 * phase + 1)
                v.tensor_scalar(std[:], mv[:, :, 1], EPS, None, ALU.add).then_inc(var_done, 1)
                dve.wait_ge(std_done, phase + 1)
                v.reciprocal(rstd[:], std[:]).then_inc(rstd_done, 1)
                dve.wait_ge(rstd_done, 2 * phase + 2)

            def normalise(phase, t):
                i, j = t // TPB, t % TPB
                if NB * phase + i >= 1:
                    dve.wait_ge(xt_ready, 2 * (NB * phase + i))
                v.tensor_scalar(xn[:, j, :], x_res[:, t, :], mv[:, t, 0:1], rstd[:, t:t + 1],
                                ALU.subtract, ALU.mult).then_inc(xn_ready, 1)

            def xt_low(phase, i, c, src):
                n = 2 * NB * phase + 2 * i + c
                dve.wait_ge(xt_hi, n + 1)
                v.tensor_tensor(xnt_lo[:, c, i * BLK:(i + 1) * BLK], src[:],
                                xnt_hi[:, c, i * BLK:(i + 1) * BLK].bitcast(F32), ALU.subtract).then_inc(xt_lo, 1)

            def keys_values(layer):
                vr = vrest[:]
                ps = bank[5 + layer][0:SC, :]
                dve.wait_ge(k_biased, 2 * layer + 2)
                v.tensor_copy(kx_hi.bitcast(F32R), kf).then_inc(kx_done, 1)
                dve.wait_ge(kx_done, 2 * layer + 1)
                v.tensor_tensor(kx_lo.bitcast(F32R), kf, kx_hi, ALU.subtract).then_inc(kx_done, 1)
                dve.wait_ge(kx_done, 2 * layer + 2)
                dve.wait_ge(consts, 2)
                mask = head_mask[:].unsqueeze(2).to_broadcast([P, HG, SC])
                for g in range(G):
                    for b in range(B):
                        for part, (to, k) in enumerate(((kb_hi, kx_hi), (kb_lo, kx_lo))):
                            one = k[:, g, b * SC:(b + 1) * SC].unsqueeze(1).to_broadcast([P, HG, SC])
                            ins = v.tensor_tensor(to[:, g, b], one, mask, ALU.mult)
                        ins.then_inc(kb_done, 1)
                dve.wait_ge(v_ready, layer + 1)
                heads = "p (b h d) -> p b h d"
                psv = ps.rearrange(heads, b=B, h=H)
                vrv = vr.rearrange(heads, b=B, h=H)
                base = 6 + 4 * layer
                v.tensor_copy(v3[:, :, 0, :, 0:HD], psv).then_inc(v_chain, 1)
                dve.wait_ge(v_chain, base + 1)
                v.tensor_tensor(vrv, psv, v3[:, :, 0, :, 0:HD], ALU.subtract).then_inc(v_chain, 1)
                dve.wait_ge(v_chain, base + 2)
                v.tensor_copy(v3[:, :, 1, :, 0:HD], vrv).then_inc(v_chain, 1)
                dve.wait_ge(v_chain, base + 3)
                v.tensor_tensor(vrv, vrv, v3[:, :, 1, :, 0:HD], ALU.subtract).then_inc(v_chain, 1)
                dve.wait_ge(v_chain, base + 4)
                v.tensor_copy(v3[:, :, 2, :, 0:HD], vrv).then_inc(v_done, 1)

            def attention(layer):
                phase = 2 * layer

                def q_low(i, m):
                    c = col_at[f"bq{layer}"][0] + m
                    dve.wait_ge(q_hi, 2 * (NB * layer + i) + m + 1)
                    v.scalar_tensor_tensor(out=qt_lo[:, m, :], in0=bank[7][:], scalar=colp[:, c:c + 1],
                                           in1=qt_hi[:, m, :].bitcast(F32), op0=ALU.add, op1=ALU.subtract)\
                        .then_inc(q_lo, 1)

                for t in range(TPB):
                    normalise(phase, t)
                xt_low(phase, 0, 0, bank[7])
                xt_low(phase, 0, 1, bank[7])
                q_low(0, 0)
                q_low(0, 1)
                aggr = None
                for n in range(NU + 4):
                    i, u, gn = n // UPB, n % UPB, NU * layer + n
                    if u in (4, 5) and i + 1 < NB:
                        normalise(phase, TPB * (i + 1) + 2 * (u - 4))
                        normalise(phase, TPB * (i + 1) + 2 * (u - 4) + 1)
                    if u == 7 and i + 1 < NB:
                        q_low(i + 1, 0)
                    if n < NU:
                        dve.wait_ge(s_ready, gn + 1)
                        for half in range(2):
                            s = bank[2 * (n % 2) + half][:, 0:SH].rearrange("p (h c) -> p h c", c=SC)
                            ins = v.tensor_reduce(smax[:, n % 2, 4 * half:4 * half + 4], s, AX.X, ALU.max)
                        ins.then_inc(max_done, 1)
                        dve.wait_ge(max_done, gn + 1)
                        if gn >= 2:
                            dve.wait_ge(pt_ready, 2 * (gn - 1))
                        for half in range(2):
                            s = bank[2 * (n % 2) + half][:, 0:SH].rearrange("p (h c) -> p h c", c=SC)
                            m = smax[:, n % 2, 4 * half:4 * half + 4].unsqueeze(2).to_broadcast([P, 4, SC])
                            ins = v.tensor_tensor(prob[:, n % 2, 4 * half:4 * half + 4, :], s, m, ALU.subtract)
                        ins.then_inc(sub_done, 1)
                    if 1 <= n <= NU:
                        for q in range(2):
                            dve.wait_ge(pt_hi_done, 2 * (gn - 1) + q + 1)
                            v.tensor_tensor(pt_lo[:, (n - 1) % 2, q].rearrange("p h c -> p (h c)"),
                                            bank[4 + q][0:SC, :],
                                            pt_hi[:, (n - 1) % 2, q].rearrange("p h c -> p (h c)"),
                                            ALU.subtract).then_inc(pt_lo_done, 1)
                    if n % 2 == 1 and 3 <= n < NU + 3:
                        t = (n - 3) // 2
                        gt = NT * layer + t
                        o = bank[6][:, 0:H * VW].rearrange("p (h d) -> p h d", h=H)
                        dve.wait_ge(pv_ready, 2 * gt + 2)
                        v.reciprocal(rsum[:, t % 2, :], o[:, :, HD]).then_inc(rsum_done, 1)
                        dve.wait_ge(rsum_done, gt + 1)
                        if gt >= 2:
                            dve.wait_ge(ot_ready, gt - 1)
                        v.tensor_tensor(o_n[:, t % 2], o[:, :, 0:HD],
                                        rsum[:, t % 2, :].unsqueeze(2).to_broadcast([P, H, HD]), ALU.mult)\
                            .then_inc(o_done, 1)
                    if n % 2 == 0 and 4 <= n < NU + 4:
                        t = (n - 4) // 2
                        gt = NT * layer + t
                        dve.wait_ge(ot_hi_done, gt + 1)
                        v.tensor_tensor(ot_lo[:, t % 2].rearrange("p k c -> p (k c)"), bank[7][:, 0:D],
                                        ot_hi[:, t % 2].rearrange("p k c -> p (k c)").bitcast(F32),
                                        ALU.subtract).then_inc(ot_lo_done, 1)
                    if n % 2 == 1 and 5 <= n:
                        t = (n - 5) // 2
                        gt = NT * layer + t
                        dve.wait_ge(op_ready, gt + 1)
                        v.scalar_tensor_tensor(out=x_res[:, t, :], in0=bank[7][:, 0:D],
                                               scalar=gate_t[:, layer:layer + 1], in1=x_res[:, t, :],
                                               op0=ALU.mult, op1=ALU.add).then_inc(x_new, 1)
                        dve.wait_ge(x_new, gt + 1)
                        aggr = tile_stats(phase + 1, t)
                    if u == 6 and i + 1 < NB:
                        xt_low(phase, i + 1, 0, bank[7])
                        xt_low(phase, i + 1, 1, bank[7])
                    if u == 7 and i + 1 < NB:
                        q_low(i + 1, 1)
                return aggr

            def prepare(which):
                phase = 2 * which + 1
                for i in range(NB):
                    for t in range(TPB * i, TPB * (i + 1)):
                        normalise(phase, t)
                    for c in range(KD):
                        xt_low(phase, i, c, bank[(2 * i + c) % 4])
                dve.wait_ge(lg_ready, which + 1)
                v.tensor_copy(lg[:], bank[6][:, 0:NT * E].rearrange("p (t e) -> p t e", e=E)).then_inc(lg_copied, 1)
                dve.wait_ge(lg_copied, which + 1)

            chain = [0]

            def link(ins):
                chain[0] += 1
                ins.then_inc(r_chain, 1)
                dve.wait_ge(r_chain, chain[0])

            for i in range(NB):
                dve.wait_ge(x_in[i], 16)
                for t in range(TPB * i, TPB * (i + 1)):
                    aggr = tile_stats(0, t)
            norm_scale(0, aggr)
            keys_values(0)
            dve.wait_ge(gates_done, 1)
            aggr = attention(0)
            norm_scale(1, aggr)
            prepare(0)

            def over_e(a):
                return a.unsqueeze(2).to_broadcast([P, NT, E])
            link(v.tensor_reduce(rs[0][:], lg[:], AX.X, ALU.max))
            link(v.tensor_tensor(rt[0][:], lg[:], over_e(rs[0][:]), ALU.subtract))
            dve.wait_ge(r_act, 1)
            link(v.tensor_reduce(rs[0][:], rt[1][:], AX.X, ALU.add))
            link(v.reciprocal(rs[1][:], rs[0][:]))
            link(v.tensor_tensor(rt[0][:], rt[1][:], over_e(rs[1][:]), ALU.mult))
            for t in range(NT):
                ins = v.max(rt[2][:, t, :], rt[0][:, t, :])
            link(ins)
            link(v.tensor_tensor(rs[0][:], rt[2][:, :, 0], rt[2][:, :, 1], ALU.add))
            link(v.reciprocal(rs[1][:], rs[0][:]))
            link(v.tensor_tensor(rs[2][:], rt[2][:, :, 0], rs[1][:], ALU.mult))
            link(v.tensor_tensor(rs[3][:], rt[2][:, :, 1], rs[1][:], ALU.mult))
            link(v.tensor_tensor(rs[0][:], rs[2][:], rs[3][:], ALU.add))
            link(v.tensor_scalar(rs[1][:], rs[0][:], gate_t[:, 2:3], None, ALU.mult))

            for i in range(NB):
                for m in range(M0):
                    n = M0 * i + m
                    dve.wait_ge(act_done, n + 1)
                    v.tensor_copy(ht_hi[:, m, :], hf[:, n % 2, :]).then_inc(hi_done, 1)
                    dve.wait_ge(hi_done, n + 1)
                    v.tensor_tensor(ht_lo[:, m, :], hf[:, n % 2, :], ht_hi[:, m, :].bitcast(F32), ALU.subtract)\
                        .then_inc(lo_done, 1)
                for j in range(TPB):
                    t = TPB * i + j
                    dve.wait_ge(dn_ready, t + 1)
                    v.scalar_tensor_tensor(out=x_res[:, t, :], in0=bank[4 + t % 2][:, 0:D], scalar=rs[1][:, t:t + 1],
                                           in1=x_res[:, t, :], op0=ALU.mult, op1=ALU.add).then_inc(y_done, 1)
                    dve.wait_ge(y_done, t + 1)
                    aggr = tile_stats(2, t)
                if i == KV_AFTER:
                    keys_values(1)
            norm_scale(2, aggr)
            aggr = attention(1)
            norm_scale(3, aggr)
            prepare(1)

            sel = rt[0][:]
            a, z = ev_at["beta"]
            link(v.tensor_tensor(sel, lg[:], ev[:, a:z].unsqueeze(1).to_broadcast([P, NT, E]), ALU.add))
            mine = sel.unsqueeze(3).to_broadcast([P, NT, E, E])
            other = sel.unsqueeze(2).to_broadcast([P, NT, E, E])
            link(v.tensor_tensor(cmp, other, mine, ALU.is_gt))
            link(v.tensor_tensor(rank, other, mine, ALU.is_equal))
            for j in range(E):
                ins = v.memset(rank[:, :, j, j:E], 0.0)
            link(ins)
            link(v.tensor_tensor(rank, rank, cmp, ALU.add))
            link(v.tensor_reduce(rt[1][:], rank, AX.X, ALU.add))
            dve.wait_ge(r_act, 2)
            link(v.scalar_tensor_tensor(out=cw[:], in0=rt[1][:], scalar=1.5, in1=rt[2][:], op0=ALU.is_lt, op1=ALU.mult))
            link(v.tensor_scalar(cw[:], cw[:], gate_t[:, 3:4], None, ALU.mult))

            def add_tiles(u):
                x = u // NB
                for j in range(TPB):
                    n = TPB * u + j
                    t = n % NT
                    dve.wait_ge(dn_ready, NT + n + 1)
                    if x >= 1:
                        dve.wait_ge(y_done, NT + n + 1 - NT)
                    s = gate_t[:, 3:4] if x == 0 else cw[:, t, x - 1:x]
                    v.scalar_tensor_tensor(out=x_res[:, t, :], in0=bank[4 + n % 2][:, 0:D], scalar=s,
                                           in1=x_res[:, t, :], op0=ALU.mult, op1=ALU.add).then_inc(y_done, 1)

            for u in range(NB * (E + 1)):
                for m in range(M1):
                    n = M1 * u + m
                    slot = u % 2 * M1 + m
                    dve.wait_ge(act_done, NB * M0 + n + 1)
                    dve.wait_ge(up_ready, NB * M0 + 2 * n + 2)
                    v.tensor_tensor(hf[:, n % 2, :], hf[:, n % 2, :], bank[2 + n % 2][:], ALU.mult).then_inc(h_done, 1)
                    dve.wait_ge(h_done, n + 1)
                    v.tensor_copy(ht_hi[:, slot, :], hf[:, n % 2, :]).then_inc(hi_done, 1)
                    dve.wait_ge(hi_done, NB * M0 + n + 1)
                    v.tensor_tensor(ht_lo[:, slot, :], hf[:, n % 2, :], ht_hi[:, slot, :].bitcast(F32), ALU.subtract)\
                        .then_inc(lo_done, 1)
                if u >= 1:
                    add_tiles(u - 1)
            add_tiles(NB * (E + 1) - 1)


def kernel(**inputs):
    import numpy as np
    import concourse.bacc as bacc
    from concourse.bass_utils import run_bass_kernel_spmd

    i = {k: np.asarray(v) for k, v in inputs.items()}

    def per_partition(a):
        return a.reshape(-1, P).T

    def rows_per_partition(a):
        return a.reshape(KD, P, -1).transpose(1, 0, 2).reshape(P, -1)

    arrays = {
        "x": i["x"].reshape(T, D),
        "ctx_t": i["ctx_1024"].reshape(B * SC, D).T,
        "cols": np.concatenate([
            per_partition(i["L0_xattn_bq"]), per_partition(i["L0_xattn_bk"]), per_partition(i["L0_ffn_b1"]),
            per_partition(i["L1_xattn_bq"]), per_partition(i["L1_xattn_bk"]),
            rows_per_partition(i["L0_ffn_router_w"]), rows_per_partition(i["L1_ffn_gate_w"].T)], axis=1),
        "rows": np.concatenate([i["L0_xattn_bv"], i["L0_xattn_bo"], i["L0_ffn_b2"], i["L1_xattn_bv"],
                                i["L1_xattn_bo"]])[None, :],
        "every": np.concatenate([i["g_xattn"], i["g_ffn"], i["L1_ffn_beta"]]),
        "wa0": np.stack([i["L0_xattn_Wq"], i["L0_xattn_Wk"], i["L0_xattn_Wv"], i["L0_xattn_Wo"]]),
        "w1": i["L0_ffn_w1"],
        "w2": i["L0_ffn_w2"],
        "wa1": np.stack([i["L1_xattn_wq"].T, i["L1_xattn_wk"].T, i["L1_xattn_wv"].T, i["L1_xattn_wo"].T]),
        "w_in": np.stack([np.concatenate([i["L1_ffn_shared_gate_w"], i["L1_ffn_gate_proj_w"]]),
                          np.concatenate([i["L1_ffn_shared_up_w"], i["L1_ffn_up_proj_w"]])], axis=1),
        "w_down": np.concatenate([i["L1_ffn_shared_down_w"], i["L1_ffn_down_proj_w"]]),
    }
    arrays = {k: np.ascontiguousarray(a) for k, a in arrays.items()}
    nc = bacc.Bacc("TRN2", target_bir_lowering=False, num_devices=1)
    aps = [nc.dram_tensor("in_" + k, a.shape, F32, kind="ExternalInput").ap() for k, a in arrays.items()]
    out = nc.dram_tensor("out_x", (T, D), F32, kind="ExternalOutput").ap()
    flamingo(nc, *aps, out)
    r = run_bass_kernel_spmd(nc, [{"in_" + k: a for k, a in arrays.items()}], core_ids=[0])
    return r.results[0]["out_x"].reshape(B, SEQ, D)
```

```python
from contextlib import ExitStack

import concourse.bass as bass
from concourse import mybir

F32 = mybir.dt.float32
F32R = mybir.dt.float32r
I32 = mybir.dt.int32
F16 = mybir.dt.float16
BF16 = mybir.dt.bfloat16
ALU = mybir.AluOpType
ACT = mybir.ActivationFunctionType
AX = mybir.AxisListType

P = 128
D = 256
KD = D // P
B = 2
SEQ = 1024
SC = 77
T = B * SEQ
NT = T // P
BLK = 512
NB = T // BLK
TPB = BLK // P
H = 16
HD = D // H
HG = 8
G = H // HG
SW = HG * SC
SH = SW // 2
VW = HD + 1
NU = NT * G
UPB = TPB * G
F0 = 1024
M0 = F0 // P
E = 8
M1W = 512
M1 = M1W // P
R = 256
KS = R // P
MAX_PER_EXPERT = T // R
NSLOT = (2 * T + E * (R - 1)) // R
BEFORE = 2
EPS = 1e-5
KV_AFTER = 1
SCALE = 0.25

WA = 4 * KD * D
WF = KD * F0
WI = 2 * KD * M1W
WE = WI + M1 * D

COLS = {"bq0": 2, "bk0": 2, "b1": M0, "bq1": 2, "bk1": 2, "wr0": KD * E, "wr1": KD * E}
ROWS = {"bv0": D, "bo0": D, "b2": D, "bv1": D, "bo1": D}
EVERY = {"gates": 4, "beta": E}


def offsets(widths):
    at, n = {}, 0
    for name, w in widths.items():
        at[name] = (n, n + w)
        n += w
    return at, n


def flamingo(nc, x, ctx_t, cols, rows, every, wa0, w1, w2, wa1, w_shared, w_experts, out):
    col_at, n_cols = offsets(COLS)
    row_at, n_rows = offsets(ROWS)
    ev_at, n_every = offsets(EVERY)
    with ExitStack() as ctx:
        def sb(name, shape, dt, where=ctx):
            return where.enter_context(nc.sbuf_tensor(name, shape, dt))

        def sem(name):
            return ctx.enter_context(nc.semaphore(name))

        x_res = sb("x_res", [P, NT, D], F32)
        xnt_hi = sb("xnt_hi", [P, KD, T], F32R)
        xnt_lo = sb("xnt_lo", [P, KD, T], F32R)
        arena = sb("arena", [P, 4 * WE], F32R)
        work = ExitStack()
        slot_cmp = sb("slot_cmp", [1, NSLOT, E], F32, work)
        slot_e = sb("slot_e", [1, NSLOT], F32, work)
        filled = sb("filled", [P, E, MAX_PER_EXPERT], F32, work)
        cum = [sb(f"cum{i}", [P, NT, E], F32, work) for i in range(2)]
        es = [sb(f"es{i}", [P, E], F32, work) for i in range(4)]
        chosen = sb("chosen", [P, 3, NT, E], F32, work)
        dest_f = sb("dest_f", [P, 2, NT], F32, work)
        work.close()
        raw = [sb(f"raw{i}", [P, WE], F32) for i in range(2)]
        keys = ExitStack()
        kb_hi = sb("kb_hi", [P, G, B, HG, SC], F32R, keys)
        kb_lo = sb("kb_lo", [P, G, B, HG, SC], F32R, keys)
        v3 = sb("v3", [SC, B, 3, H, VW], BF16, keys)
        ct_hi = sb("ct_hi", [P, KD, B * SC], F32R, keys)
        ct_lo = sb("ct_lo", [P, KD, B * SC], F32R, keys)
        keys.close()
        routing = ExitStack()
        xn_all = sb("xn_all", [P, NT, D], F32, routing)
        rank = sb("rank", [P, NT, E, E], F32, routing)
        cmp = sb("cmp", [P, NT, E, E], F32, routing)
        routing.close()
        odd = ExitStack()
        w_odd = sb("w_odd", [P, 2 * WE], F32R, odd)
        odd.close()
        sb("keys_space", [P, max(G * B * HG * SC * 2 + 2 * KD * B * SC + B * 3 * H * VW // 2 + 16, 2 * WE)], F32)
        colp = sb("colp", [P, n_cols], F32)
        ev = sb("ev", [P, n_every], F32)
        gate_t = sb("gate_t", [P, 4], F32)
        biases = ExitStack()
        row_hi = sb("row_hi", [1, n_rows], F32R, biases)
        row_lo = sb("row_lo", [1, n_rows], F32R, biases)
        vrest = sb("vrest", [SC, B * D], F32, biases)
        biases.close()
        slot = ExitStack()
        xs = sb("xs", [P, 2, KS, D], F32, slot)
        xst_hi = sb("xst_hi", [P, 2, KD, R], F32R, slot)
        xst_lo = sb("xst_lo", [P, 2, KD, R], F32R, slot)
        slot.close()
        back = ExitStack()
        RING = 6
        y_back = sb("y_back", [P, RING, 2, D], F32, back)
        back.close()
        sb("biases_space", [P, 2 * n_rows + B * D], F32)
        zero_row = sb("zero_row", [P, D], F32)
        before = sb("before", [P, P], F32)
        all_ones = sb("all_ones", [P, P], F32)
        slot_limit = sb("slot_limit", [P, E, MAX_PER_EXPERT], F32)
        slot_id = sb("slot_id", [1, NSLOT, E], F32)
        slot_expert = sb("slot_expert", [1, NSLOT], I32)
        dest = sb("dest", [P, 2, NT], I32)
        weight = sb("weight", [P, 2, NT], F32)
        ones_row = sb("ones_row", [1, P], F32R)
        wr_hi = sb("wr_hi", [P, 2, KD, E], F32R)
        wr_lo = sb("wr_lo", [P, 2, KD, E], F32R)
        ident = sb("ident", [P, P], F32)
        head_mask = sb("head_mask", [P, HG], F32)
        slot_y = ExitStack()
        y_out = sb("y_out", [P, 2, KS, D], F32, slot_y)
        slot_y.close()
        xn = sb("xn", [P, TPB, D], F32)
        stats = sb("stats", [P, 2, 6], F32)
        mv = sb("mv", [P, NT, 2], F32)
        std = sb("std", [P, NT], F32)
        rstd = sb("rstd", [P, NT], F32)
        lg = sb("lg", [P, NT, E], F32)
        rt = [sb(f"rt{i}", [P, NT, E], F32) for i in range(3)]
        rs = [sb(f"rs{i}", [P, NT], F32) for i in range(4)]
        cw = sb("cw", [P, NT, E], F32)

        att = ExitStack()
        qt_hi = sb("qt_hi", [P, G, BLK], F32R, att)
        qt_lo = sb("qt_lo", [P, G, BLK], F32R, att)
        prob = sb("prob", [P, 2, HG, SC], F32, att)
        smax = sb("smax", [P, 2, HG], F32, att)
        pt_hi = sb("pt_hi", [SC, 2, 2, 4, P], F16, att)
        pt_lo = sb("pt_lo", [SC, 2, 2, 4, P], F16, att)
        o_n = sb("o_n", [P, 2, H, HD], F32, att)
        rsum = sb("rsum", [P, 2, H], F32, att)
        ot_hi = sb("ot_hi", [P, 2, KD, P], F32R, att)
        ot_lo = sb("ot_lo", [P, 2, KD, P], F32R, att)
        att.close()
        ffn = ExitStack()
        hf = sb("hf", [P, 2, BLK], F32, ffn)
        ht_hi = sb("ht_hi", [P, M0, BLK], F32R, ffn)
        ht_lo = sb("ht_lo", [P, M0, BLK], F32R, ffn)
        ffn.close()
        key_words = KD * B * SC
        key_space = xn[:].rearrange("p t d -> p (t d)")
        kf, kx_hi, kx_lo = (key_space[:, n * key_words:(n + 1) * key_words].rearrange("p (k n) -> p k n", k=KD)
                            for n in range(3))
        cst = ExitStack()
        ct_raw = sb("ct_raw", [P, KD, B * SC], F32, cst)
        row_raw = sb("row_raw", [1, n_rows], F32, cst)
        cst.close()

        bank = [ctx.enter_context(nc.psum_tensor(f"bank{i}", [P, BLK], F32)) for i in range(8)]

        wq = {}
        for layer, buf, at in ((0, arena, 0), (1, arena, 0)):
            for part, o in (("hi", 0), ("lo", WA)):
                wq[layer, part] = buf[:, at + o:at + o + WA].rearrange("p (w k n) -> p w k n", w=4, k=KD)
        w1_p = {part: arena[:, 2 * WA + o:2 * WA + o + WF].rearrange("p (k n) -> p k n", k=KD)
                for part, o in (("hi", 0), ("lo", WF))}
        w2_p = {part: arena[:, 2 * WA + 2 * WF + o:2 * WA + 2 * WF + o + WF].rearrange("p (k n) -> p k n", k=M0)
                for part, o in (("hi", 0), ("lo", WF))}

        def expert(buf, part):
            w = {"shared": arena[:, 2 * WE:4 * WE], 0: arena[:, 0:2 * WE], 1: w_odd[:]}[buf]
            w = w[:, WE:2 * WE] if part == "lo" else w[:, 0:WE]
            return (w[:, 0:WI].rearrange("p (w k n) -> p w k n", w=2, k=KD),
                    w[:, WI:WE].rearrange("p (k n) -> p k n", k=M1))

        x_rows = nc.dram_tensor("x_rows", (NSLOT * R, D), F32, kind="Internal").ap()
        y_rows = nc.dram_tensor("y_rows", (NSLOT * R, D), F32, kind="Internal").ap()

        small_in = sem("small_in")
        x_in = [sem(f"x_in{i}") for i in range(NB)]
        raw_in = [sem(f"raw_in{i}") for i in range(2)]
        first_split = sem("first_split")
        split_done = sem("split_done")
        consts = sem("consts")
        pool_chain = sem("pool_chain")
        setup_dve = sem("setup_dve")
        gates_done = sem("gates_done")
        k_ready, v_ready = sem("k_ready"), sem("v_ready")
        k_biased = sem("k_biased")
        kx_done, kb_done, v_done = sem("kx_done"), sem("kb_done"), sem("v_done")
        v_chain = sem("v_chain")
        stats_done, var_done, std_done, rstd_done = sem("stats_done"), sem("var_done"), sem("std_done"), sem("rstd_done")
        xn_ready, xt_ready, xt_hi, xt_lo = sem("xn_ready"), sem("xt_ready"), sem("xt_hi"), sem("xt_lo")
        q_ready, q_hi, q_lo = sem("q_ready"), sem("q_hi"), sem("q_lo")
        s_ready, max_done, sub_done, exp_done = sem("s_ready"), sem("max_done"), sem("sub_done"), sem("exp_done")
        pt_ready, pt_hi_done, pt_lo_done = sem("pt_ready"), sem("pt_hi_done"), sem("pt_lo_done")
        pv_ready, rsum_done, o_done = sem("pv_ready"), sem("rsum_done"), sem("o_done")
        ot_ready, ot_hi_done, ot_lo_done = sem("ot_ready"), sem("ot_hi_done"), sem("ot_lo_done")
        op_ready, x_new = sem("op_ready"), sem("x_new")
        lg_ready, lg_copied, r_chain, r_act, c_done = (sem("lg_ready"), sem("lg_copied"), sem("r_chain"),
                                                       sem("r_act"), sem("c_done"))
        up_ready, act_done, h_done, hi_done, lo_done = (sem("up_ready"), sem("act_done"), sem("h_done"),
                                                        sem("hi_done"), sem("lo_done"))
        dn_ready, y_done = sem("dn_ready"), sem("y_done")
        stored = sem("stored")
        zeroed, routed_pe, rank_ready, route_done = sem("zeroed"), sem("routed_pe"), sem("rank_ready"), sem("route_done")
        scattered = sem("scattered")
        rows_in = [sem(f"rows_in{i}") for i in range(2)]
        y_stored = [sem(f"y_stored{i}") for i in range(2)]
        gathered = [sem(f"gathered{i}") for i in range(RING)]
        win_in = [sem(f"win_in{i}") for i in range(2)]
        wdn_in = [sem(f"wdn_in{i}") for i in range(2)]
        in_hi, in_lo, dn_hi, dn_lo = sem("in_hi"), sem("in_lo"), sem("dn_hi"), sem("dn_lo")
        st_ready, st_hi, st_lo = sem("st_ready"), sem("st_hi"), sem("st_lo")
        sg_ready, su_ready, s_silu, s_h, s_hhi, s_hlo = (sem("sg_ready"), sem("su_ready"), sem("s_silu"), sem("s_h"),
                                                         sem("s_hhi"), sem("s_hlo"))
        sd_ready, sy_done = sem("sd_ready"), sem("sy_done")
        added, combined = sem("added"), sem("combined")

        block = ctx.enter_context(nc.Block())

        PIECES = 4 + 1

        def split_dst(p):
            if p == 0:
                return wq[0, "hi"], wq[0, "lo"], WA
            if p == 1:
                return w1_p["hi"], w1_p["lo"], WF
            if p == 2:
                return w2_p["hi"], w2_p["lo"], WF
            if p == 3:
                return wq[1, "hi"], wq[1, "lo"], WA
            return arena[:, 2 * WE:3 * WE], arena[:, 3 * WE:4 * WE], WE

        @block.sync
        def _(sp):
            sp.dma_start(colp[:], cols).then_inc(small_in, 16)
            sp.dma_start(ct_raw[:], ctx_t.rearrange("(k p) n -> p k n", p=P)).then_inc(small_in, 16)
            sp.dma_start(row_raw[:], rows).then_inc(small_in, 16)
            sp.dma_start(ev[:], every.partition_broadcast(P)).then_inc(small_in, 16)
            for i in range(NB):
                sp.dma_start(x_res[:, TPB * i:TPB * (i + 1), :],
                             x[BLK * i:BLK * (i + 1), :].rearrange("(t p) d -> p t d", p=P)).then_inc(x_in[i], 16)
                if i == 0:
                    sp.dma_start(raw[0][:, 0:WA].rearrange("p (w k n) -> p w k n", w=4, k=KD),
                                 wa0.rearrange("w (k p) n -> p w k n", p=P)).then_inc(raw_in[0], 16)
            for p in range(1, PIECES):
                if p == 2:
                    sp.wait_ge(first_split, 1)
                if p > 2:
                    sp.wait_ge(split_done, p - 2)
                to = raw[p % 2]
                if p == 1:
                    sp.dma_start(to[:, 0:WF].rearrange("p (k n) -> p k n", k=KD),
                                 w1.rearrange("(k p) n -> p k n", p=P)).then_inc(raw_in[p % 2], 16)
                elif p == 2:
                    sp.dma_start(to[:, 0:WF].rearrange("p (k n) -> p k n", k=M0),
                                 w2.rearrange("(k p) n -> p k n", p=P)).then_inc(raw_in[p % 2], 16)
                elif p == 3:
                    sp.dma_start(to[:, 0:WA].rearrange("p (w k n) -> p w k n", w=4, k=KD),
                                 wa1.rearrange("w (k p) n -> p w k n", p=P)).then_inc(raw_in[p % 2], 16)
                else:
                    sp.dma_start(to[:], w_shared).then_inc(raw_in[p % 2], 16)
                if p == 3:
                    sp.wait_ge(setup_dve, 1)
                    sp.dma_start(x_rows.rearrange("(p n) d -> p n d", p=P),
                                 zero_row[:].unsqueeze(1).to_broadcast([P, NSLOT * R // P, D])).then_inc(zeroed, 16)

            def load_in(s):
                if s >= 2:
                    sp.wait_ge(in_lo, s - 1)
                e = sp.value_load(slot_expert[0:1, s:s + 1], min_val=0, max_val=E - 1)
                sp.dma_start(raw[s % 2][:, 0:WI], w_experts[bass.ds(e, 1), :, 0:WI].rearrange("e p n -> p (e n)"))\
                    .then_inc(win_in[s % 2], 16)
                return e

            def load_down(s, e):
                if s >= 2:
                    sp.wait_ge(dn_lo, s - 1)
                sp.dma_start(raw[s % 2][:, WI:WE], w_experts[bass.ds(e, 1), :, WI:WE].rearrange("e p n -> p (e n)"))\
                    .then_inc(wdn_in[s % 2], 16)

            def load_rows(s):
                if s >= 2:
                    sp.wait_ge(st_ready, s - 1)
                sp.dma_start(xs[:, s % 2], x_rows[s * R:(s + 1) * R, :].rearrange("(a p) d -> p a d", p=P))\
                    .then_inc(rows_in[s % 2], 16)

            def store_rows(s):
                sp.wait_ge(sy_done, s + 1)
                sp.dma_start(y_rows[s * R:(s + 1) * R, :].rearrange("(a p) d -> p a d", p=P), y_out[:, s % 2])\
                    .then_inc(y_stored[s % 2], 16)

            sp.wait_ge(route_done, 1)
            sp.wait_ge(split_done, 4)
            for s in range(2):
                load_down(s, load_in(s))
            sp.wait_ge(scattered, 16 * 2 * NT)
            load_rows(0)
            load_rows(1)
            for s in range(NSLOT):
                if s + 2 < NSLOT:
                    e = load_in(s + 2)
                    load_rows(s + 2)
                    load_down(s + 2, e)
                if s >= 1:
                    store_rows(s - 1)
            store_rows(NSLOT - 1)

            for i in range(NB):
                sp.wait_ge(combined, 2 * TPB * (i + 1))
                sp.dma_start(out[BLK * i:BLK * (i + 1), :].rearrange("(t p) d -> p t d", p=P),
                             x_res[:, TPB * i:TPB * (i + 1), :]).then_inc(stored, 16)
            sp.wait_ge(stored, 16 * NB)

        def raw_value(p):
            return 16 * (p // 2 + 1)

        @block.gpsimd
        def _(pool):
            nc.gpsimd.memset(ident[:], 0.0).then_inc(pool_chain, 1)
            nc.gpsimd.memset(head_mask[:], 1.0).then_inc(pool_chain, 1)
            pool.wait_ge(pool_chain, 2)
            nc.gpsimd.affine_select(out=ident[:], in_=ident[:], compare_op=ALU.not_equal, fill=1.0, base=0,
                                    pattern=[[-1, P]], channel_multiplier=1).then_inc(consts, 1)
            nc.gpsimd.affine_select(out=head_mask[:], in_=head_mask[:], compare_op=ALU.is_ge, fill=0.0, base=0,
                                    pattern=[[-HD, HG]], channel_multiplier=1).then_inc(pool_chain, 1)
            pool.wait_ge(pool_chain, 3)
            nc.gpsimd.affine_select(out=head_mask[:], in_=head_mask[:], compare_op=ALU.is_ge, fill=0.0, base=HD - 1,
                                    pattern=[[HD, HG]], channel_multiplier=-1).then_inc(consts, 1)
            nc.gpsimd.memset(before[:], 1.0).then_inc(pool_chain, 1)
            pool.wait_ge(pool_chain, 4)
            nc.gpsimd.affine_select(out=before[:], in_=before[:], compare_op=ALU.is_gt, fill=0.0, base=0,
                                    pattern=[[1, P]], channel_multiplier=-1).then_inc(consts, 1)
            nc.gpsimd.memset(all_ones[:], 1.0).then_inc(consts, 1)
            nc.gpsimd.iota(slot_limit[:], [[0, E], [R, MAX_PER_EXPERT]], base=0, channel_multiplier=0,
                           allow_small_or_imprecise_dtypes=True).then_inc(consts, 1)
            nc.gpsimd.iota(slot_id[:], [[1, NSLOT], [0, E]], base=0, channel_multiplier=0,
                           allow_small_or_imprecise_dtypes=True).then_inc(consts, 1)
            done = 4
            for p in range(1, PIECES):
                hi, lo, n = split_dst(p)
                pool.wait_ge(raw_in[p % 2], raw_value(p))
                if p == 3:
                    pool.wait_ge(op_ready, NT)
                if p == 4:
                    pool.wait_ge(dn_ready, NT)
                src = raw[p % 2][:, 0:n]
                if len(hi.shape) == 3:
                    src = src.rearrange("p (k n) -> p k n", k=hi.shape[1])
                if len(hi.shape) == 4:
                    src = src.rearrange("p (w k n) -> p w k n", w=4, k=KD)
                nc.gpsimd.tensor_copy(hi, src).then_inc(pool_chain, 1)
                done += 1
                pool.wait_ge(pool_chain, done)
                nc.gpsimd.tensor_tensor(lo, src, hi.bitcast(F32), ALU.subtract).then_inc(split_done, 1)

            pool.wait_ge(route_done, 1)
            pool.wait_ge(zeroed, 16)
            for t in range(NT):
                for c in range(2):
                    pool.indirect_dma_start(x_rows, bass.IndirectOffsetOnAxis(ap=dest[:, c, t:t + 1], axis=0),
                                            xn_all[:, t, :], None).then_inc(scattered, 16)

            for s in range(NSLOT):
                pool.wait_ge(in_hi, s + 1)
                if s >= 2:
                    pool.wait_ge(su_ready, 2 * (s - 1))
                (hi, _), (lo, _) = expert(s % 2, "hi"), expert(s % 2, "lo")
                src = raw[s % 2][:, 0:WI].rearrange("p (w k n) -> p w k n", w=2, k=KD)
                nc.gpsimd.tensor_tensor(lo, src, hi.bitcast(F32), ALU.subtract).then_inc(in_lo, 1)

            pool.wait_ge(y_stored[0], 16 * ((NSLOT + 1) // 2))
            pool.wait_ge(y_stored[1], 16 * (NSLOT // 2))
            pool.wait_ge(st_lo, NSLOT)
            for t in range(NT):
                if t >= RING:
                    pool.wait_ge(combined, 2 * (t - RING) + 2)
                for c in range(2):
                    pool.indirect_dma_start(y_back[:, t % RING, c, :], None, y_rows,
                                            bass.IndirectOffsetOnAxis(ap=dest[:, c, t:t + 1], axis=0))\
                        .then_inc(gathered[t % RING], 16)

        @block.tensor
        def _(pe):
            def three(ps, w_hi, w_lo, m_hi, m_lo, start, stop, inc=None):
                nc.tensor.matmul(ps, w_lo, m_hi, start=start, stop=False)
                nc.tensor.matmul(ps, w_hi, m_lo, start=False, stop=False)
                return nc.tensor.matmul(ps, w_hi, m_hi, start=False, stop=stop)

            def kv(layer, k_bank, v_bank):
                w_hi, w_lo = wq[layer, "hi"], wq[layer, "lo"]
                for m in range(G):
                    for k in range(KD):
                        mm = three(k_bank[:, m * B * SC:(m + 1) * B * SC],
                                   w_hi[:, 1, k, m * P:(m + 1) * P], w_lo[:, 1, k, m * P:(m + 1) * P],
                                   ct_hi[:, k, :], ct_lo[:, k, :], k == 0, k == KD - 1)
                mm.then_inc(k_ready, 1)
                a, z = row_at[f"bv{layer}"]
                for b in range(B):
                    ps = v_bank[0:SC, b * D:(b + 1) * D]
                    for k in range(KD):
                        three(ps, ct_hi[:, k, b * SC:(b + 1) * SC], ct_lo[:, k, b * SC:(b + 1) * SC],
                              w_hi[:, 2, k, :], w_lo[:, 2, k, :], k == 0, False)
                    nc.tensor.matmul(ps, ones_row[:, 0:SC], row_lo[:, a:z], start=False, stop=False)
                    mm = nc.tensor.matmul(ps, ones_row[:, 0:SC], row_hi[:, a:z], start=False, stop=True)
                mm.then_inc(v_ready, 1)

            def attention(layer):
                w_hi, w_lo = wq[layer, "hi"], wq[layer, "lo"]
                bo = row_at[f"bo{layer}"]
                phase = 2 * layer
                work = bank[7]
                last_use = []

                def take_work():
                    if last_use:
                        pe.wait_ge(*last_use[-1])

                def x_transposed(i, c):
                    take_work()
                    for j in range(TPB):
                        if c == 0:
                            pe.wait_ge(xn_ready, NT * phase + TPB * i + j + 1)
                        mm = nc.tensor.transpose(work[:, j * P:(j + 1) * P], xn[:, j, c * P:(c + 1) * P], ident[:])
                    mm.then_inc(xt_ready, 1)
                    last_use.append((xt_lo, 2 * NB * phase + 2 * i + c + 1))

                def queries(i, m):
                    take_work()
                    pe.wait_ge(xt_lo, 2 * NB * phase + 2 * i + 2)
                    for k in range(KD):
                        mm = three(work[:], w_hi[:, 0, k, m * P:(m + 1) * P], w_lo[:, 0, k, m * P:(m + 1) * P],
                                   xnt_hi[:, k, i * BLK:(i + 1) * BLK], xnt_lo[:, k, i * BLK:(i + 1) * BLK],
                                   k == 0, k == KD - 1)
                    mm.then_inc(q_ready, 1)
                    last_use.append((q_lo, 2 * (NB * layer + i) + m + 1))

                def scores(n):
                    gn, i, g, b = NU * layer + n, n // UPB, n % G, n // (NU // B)
                    j = n % UPB // G
                    pe.wait_ge(q_lo, 2 * (NB * layer + i) + g + 1)
                    if gn >= 2:
                        pe.wait_ge(sub_done, gn - 1)
                    for half in range(2):
                        ps = bank[2 * (n % 2) + half][:, 0:SH].rearrange("p (h c) -> p h c", c=SC)
                        heads = slice(half * HG // 2, (half + 1) * HG // 2)
                        mm = three(ps, qt_hi[:, g, j * P:(j + 1) * P], qt_lo[:, g, j * P:(j + 1) * P],
                                   kb_hi[:, g, b, heads, :], kb_lo[:, g, b, heads, :], True, True)
                    mm.then_inc(s_ready, 1)

                def probs_transposed(n):
                    gn = NU * layer + n
                    pe.wait_ge(exp_done, gn + 1)
                    for q in range(2):
                        if gn >= 1:
                            pe.wait_ge(pt_lo_done, 2 * (gn - 1) + q + 1)
                        for h in range(4):
                            mm = nc.tensor.transpose(bank[4 + q][0:SC, h * P:(h + 1) * P],
                                                     prob[:, n % 2, 4 * q + h, :], ident[:])
                        mm.then_inc(pt_ready, 1)

                def values(n):
                    gn, b, g = NU * layer + n, n // (NU // B), n % G
                    if g == 0 and gn >= 2:
                        pe.wait_ge(o_done, gn // 2)
                    for q in range(2):
                        pe.wait_ge(pt_lo_done, 2 * gn + q + 1)
                        for h in range(4):
                            head = g * HG + 4 * q + h
                            ps = bank[6][:, head * VW:(head + 1) * VW]
                            hi, lo = pt_hi[:, n % 2, q, h, :], pt_lo[:, n % 2, q, h, :]
                            nc.tensor.matmul(ps, hi, v3[:, b, 2, head, :], start=True, stop=False)
                            nc.tensor.matmul(ps, hi, v3[:, b, 1, head, :], start=False, stop=False)
                            nc.tensor.matmul(ps, hi, v3[:, b, 0, head, :], start=False, stop=False)
                            nc.tensor.matmul(ps, lo, v3[:, b, 1, head, :], start=False, stop=False)
                            mm = nc.tensor.matmul(ps, lo, v3[:, b, 0, head, :], start=False, stop=True)
                    mm.then_inc(pv_ready, 1)

                def out_transposed(t):
                    gt = NT * layer + t
                    take_work()
                    pe.wait_ge(o_done, gt + 1)
                    flat = o_n[:, t % 2].rearrange("p h d -> p (h d)")
                    for c in range(KD):
                        mm = nc.tensor.transpose(work[:, c * P:(c + 1) * P], flat[:, c * P:(c + 1) * P], ident[:])
                    mm.then_inc(ot_ready, 1)
                    last_use.append((ot_lo_done, gt + 1))

                def out_projected(t):
                    gt = NT * layer + t
                    take_work()
                    ps = work[:, 0:D]
                    for k in range(KD):
                        three(ps, ot_hi[:, t % 2, k, :], ot_lo[:, t % 2, k, :],
                              w_hi[:, 3, k, :], w_lo[:, 3, k, :], k == 0, False)
                    nc.tensor.matmul(ps, ones_row[:], row_lo[:, bo[0]:bo[1]], start=False, stop=False)
                    nc.tensor.matmul(ps, ones_row[:], row_hi[:, bo[0]:bo[1]], start=False, stop=True)\
                        .then_inc(op_ready, 1)
                    last_use.append((x_new, gt + 1))

                x_transposed(0, 0)
                x_transposed(0, 1)
                queries(0, 0)
                queries(0, 1)
                pe.wait_ge(kb_done, 4 * (layer + 1))
                pe.wait_ge(v_done, layer + 1)
                for n in range(NU + 4):
                    i, u = n // UPB, n % UPB
                    if u == 7 and i + 1 < NB:
                        queries(i + 1, 0)
                    if n < NU:
                        scores(n)
                    if 1 <= n <= NU:
                        probs_transposed(n - 1)
                    if 2 <= n < NU + 2:
                        values(n - 2)
                    if n % 2 == 0 and 4 <= n < NU + 4:
                        out_transposed((n - 4) // 2)
                    if n % 2 == 1 and 5 <= n:
                        out_projected((n - 5) // 2)
                    if u == 6 and i + 1 < NB:
                        x_transposed(i + 1, 0)
                        x_transposed(i + 1, 1)
                    if u == 7 and i + 1 < NB:
                        queries(i + 1, 1)

            def prepare(which):
                phase = 2 * which + 1
                for i in range(NB):
                    for c in range(KD):
                        n = 2 * i + c
                        if n >= 4:
                            pe.wait_ge(xt_lo, 2 * NB * phase + n - 3)
                        src = xn[:] if which == 0 else xn_all[:, TPB * i:TPB * (i + 1), :]
                        for j in range(TPB):
                            if c == 0:
                                pe.wait_ge(xn_ready, NT * phase + TPB * i + j + 1)
                            mm = nc.tensor.transpose(bank[n % 4][:, j * P:(j + 1) * P], src[:, j, c * P:(c + 1) * P],
                                                     ident[:])
                        mm.then_inc(xt_ready, 1)
                for t in range(NT):
                    if t % TPB == 0:
                        pe.wait_ge(xt_lo, 2 * NB * phase + 2 * (t // TPB) + 2)
                    for k in range(KD):
                        mm = three(bank[6][:, t * E:(t + 1) * E], xnt_hi[:, k, t * P:(t + 1) * P],
                                   xnt_lo[:, k, t * P:(t + 1) * P], wr_hi[:, which, k, :], wr_lo[:, which, k, :],
                                   k == 0, k == KD - 1)
                mm.then_inc(lg_ready, 1)

            def down(ps, hh, hl, w_hi, w_lo, ks, j, waits, bias=None):
                for k in range(ks):
                    if waits:
                        pe.wait_ge(lo_done, waits + k + 1)
                    mm = three(ps, hh[:, k, j * P:(j + 1) * P], hl[:, k, j * P:(j + 1) * P],
                               w_hi[:, k, :], w_lo[:, k, :], k == 0, k == ks - 1 and bias is None)
                if bias is not None:
                    nc.tensor.matmul(ps, ones_row[:], row_lo[:, bias[0]:bias[1]], start=False, stop=False)
                    mm = nc.tensor.matmul(ps, ones_row[:], row_hi[:, bias[0]:bias[1]], start=False, stop=True)
                return mm

            pe.wait_ge(setup_dve, 1)
            pe.wait_ge(consts, 2)
            kv(0, bank[4], bank[5])
            attention(0)
            prepare(0)
            pe.wait_ge(split_done, 2)
            for i in range(NB):
                for m in range(M0):
                    n = M0 * i + m
                    if n >= 4:
                        pe.wait_ge(act_done, n - 3)
                    for k in range(KD):
                        mm = three(bank[n % 4][:], w1_p["hi"][:, k, m * P:(m + 1) * P],
                                   w1_p["lo"][:, k, m * P:(m + 1) * P],
                                   xnt_hi[:, k, i * BLK:(i + 1) * BLK], xnt_lo[:, k, i * BLK:(i + 1) * BLK],
                                   k == 0, k == KD - 1)
                    mm.then_inc(up_ready, 1)
                if i == KV_AFTER:
                    pe.wait_ge(split_done, 3)
                    pe.wait_ge(lg_copied, 1)
                    kv(1, bank[7], bank[6])
                for j in range(TPB):
                    t = TPB * i + j
                    if t >= 2:
                        pe.wait_ge(y_done, t - 1)
                    for k in range(M0):
                        if j == 0:
                            pe.wait_ge(lo_done, M0 * i + k + 1)
                        three(bank[4 + t % 2][:, 0:D], ht_hi[:, k, j * P:(j + 1) * P], ht_lo[:, k, j * P:(j + 1) * P],
                              w2_p["hi"][:, k, :], w2_p["lo"][:, k, :], k == 0, False)
                    a, z = row_at["b2"]
                    nc.tensor.matmul(bank[4 + t % 2][:, 0:D], ones_row[:], row_lo[:, a:z], start=False, stop=False)
                    nc.tensor.matmul(bank[4 + t % 2][:, 0:D], ones_row[:], row_hi[:, a:z], start=False, stop=True)\
                        .then_inc(dn_ready, 1)

            attention(1)
            prepare(1)

            pe.wait_ge(rank_ready, 1)
            pe.wait_ge(consts, 6)
            picked = chosen[:, 2].rearrange("p t e -> p (t e)")
            nc.tensor.matmul(bank[7][:, 0:NT * E], before[:], picked, start=True, stop=True)
            nc.tensor.matmul(bank[7][:, NT * E:2 * NT * E], all_ones[:], picked, start=True, stop=True)\
                .then_inc(routed_pe, 1)

            def shared_up(v):
                (w_hi, _), (w_lo, _) = expert("shared", "hi"), expert("shared", "lo")
                for m in range(M1):
                    n = M1 * v + m
                    for w in range(2):
                        if n % (M1 * BEFORE) >= 2:
                            if w == 0:
                                pe.wait_ge(act_done, NB * M0 + n - 1)
                            else:
                                pe.wait_ge(h_done, n - 1)
                        for k in range(KD):
                            mm = three(bank[2 * w + n % 2][:], w_hi[:, w, k, m * P:(m + 1) * P],
                                       w_lo[:, w, k, m * P:(m + 1) * P], xnt_hi[:, k, v * BLK:(v + 1) * BLK],
                                       xnt_lo[:, k, v * BLK:(v + 1) * BLK], k == 0, k == KD - 1)
                        mm.then_inc(up_ready, 1)

            def shared_down(v):
                (_, w_hi), (_, w_lo) = expert("shared", "hi"), expert("shared", "lo")
                for j in range(TPB):
                    t = TPB * v + j
                    pe.wait_ge(y_done, NT + t - 1)
                    for k in range(M1):
                        if j == 0:
                            pe.wait_ge(lo_done, NB * M0 + M1 * v + k + 1)
                        at = v % 2 * M1 + k
                        mm = three(bank[4 + t % 2][:, 0:D], ht_hi[:, at, j * P:(j + 1) * P],
                                   ht_lo[:, at, j * P:(j + 1) * P], w_hi[:, k, :], w_lo[:, k, :],
                                   k == 0, k == M1 - 1)
                    mm.then_inc(dn_ready, 1)

            pe.wait_ge(split_done, 4)
            for v in range(BEFORE):
                shared_up(v)
                if v >= 1:
                    shared_down(v - 1)
            shared_down(BEFORE - 1)

            def rows_transposed(s):
                pe.wait_ge(rows_in[s % 2], 16 * (s // 2 + 1))
                if s >= 2:
                    pe.wait_ge(st_lo, s - 1)
                for k in range(KD):
                    for a in range(KS):
                        mm = nc.tensor.transpose(bank[6 + s % 2][:, (k * KS + a) * P:(k * KS + a + 1) * P],
                                                 xs[:, s % 2, a, k * P:(k + 1) * P], ident[:])
                mm.then_inc(st_ready, 1)

            def slot_up(s):
                (w_hi, _), (w_lo, _) = expert(s % 2, "hi"), expert(s % 2, "lo")
                pe.wait_ge(in_lo, s + 1)
                pe.wait_ge(st_lo, s + 1)
                for pair in range(2):
                    n = 2 * s + pair
                    for w in range(2):
                        if n >= 2:
                            if w == 0:
                                pe.wait_ge(s_silu, n - 1)
                            else:
                                pe.wait_ge(s_h, n - 1)
                        for c in range(2):
                            m = 2 * pair + c
                            for k in range(KD):
                                mm = three(bank[2 * w + pair][:, c * R:(c + 1) * R],
                                           w_hi[:, w, k, m * P:(m + 1) * P], w_lo[:, w, k, m * P:(m + 1) * P],
                                           xst_hi[:, s % 2, k, :], xst_lo[:, s % 2, k, :], k == 0, k == KD - 1)
                        mm.then_inc(sg_ready if w == 0 else su_ready, 1)

            def slot_down(s):
                (_, w_hi), (_, w_lo) = expert(s % 2, "hi"), expert(s % 2, "lo")
                pe.wait_ge(dn_lo, s + 1)
                if s >= 2:
                    pe.wait_ge(sy_done, s - 1)
                for a in range(KS):
                    for k in range(M1):
                        if a == 0 and k % 2 == 0:
                            pe.wait_ge(s_hlo, 2 * s + k // 2 + 1)
                        at, o = 2 * (s % 2) + k // 2, k % 2 * R + a * P
                        mm = three(bank[4 + s % 2][:, a * D:(a + 1) * D], ht_hi[:, at, o:o + P], ht_lo[:, at, o:o + P],
                                   w_hi[:, k, :], w_lo[:, k, :], k == 0, k == M1 - 1)
                mm.then_inc(sd_ready, 1)

            pe.wait_ge(act_done, NB * M0 + M1 * BEFORE)
            pe.wait_ge(h_done, M1 * BEFORE)
            pe.wait_ge(y_done, NT + TPB * BEFORE)
            rows_transposed(0)
            for s in range(NSLOT):
                slot_up(s)
                if s + 1 < NSLOT:
                    rows_transposed(s + 1)
                if s >= 1:
                    slot_down(s - 1)
            slot_down(NSLOT - 1)

            pe.wait_ge(s_silu, 2 * NSLOT)
            pe.wait_ge(s_h, 2 * NSLOT)
            pe.wait_ge(sy_done, NSLOT)
            for v in range(BEFORE, NB):
                shared_up(v)
                if v > BEFORE:
                    shared_down(v - 1)
            shared_down(NB - 1)

        @block.scalar
        def _(act):
            a, z = ev_at["gates"]
            act.wait_ge(small_in, 64)
            nc.scalar.activation(gate_t[:], ev[:, a:z], ACT.Tanh).then_inc(gates_done, 1)

            def bias_keys(layer):
                src = bank[4] if layer == 0 else bank[7]
                act.wait_ge(k_ready, layer + 1)
                for m in range(G):
                    c = col_at[f"bk{layer}"][0] + m
                    nc.scalar.activation(kf[:, m, :], src[:, m * B * SC:(m + 1) * B * SC], ACT.Identity,
                                         bias=colp[:, c:c + 1]).then_inc(k_biased, 1)

            def norm_std(phase):
                act.wait_ge(var_done, phase + 1)
                nc.scalar.activation(std[:], std[:], ACT.Sqrt).then_inc(std_done, 1)

            def xt_high(phase, i, c, src):
                n = 2 * NB * phase + 2 * i + c
                act.wait_ge(xt_ready, n + 1)
                nc.scalar.copy(xnt_hi[:, c, i * BLK:(i + 1) * BLK], src[:]).then_inc(xt_hi, 1)

            def attention(layer):
                def q_high(i, m):
                    n = 2 * (NB * layer + i) + m
                    act.wait_ge(q_ready, n + 1)
                    if i >= 1:
                        act.wait_ge(s_ready, NU * layer + UPB * i - 1 + m)
                    c = col_at[f"bq{layer}"][0] + m
                    nc.scalar.activation(qt_hi[:, m, :], bank[7][:], ACT.Identity, bias=colp[:, c:c + 1])\
                        .then_inc(q_hi, 1)

                xt_high(2 * layer, 0, 0, bank[7])
                xt_high(2 * layer, 0, 1, bank[7])
                q_high(0, 0)
                q_high(0, 1)
                for n in range(NU + 4):
                    i, u, gn = n // UPB, n % UPB, NU * layer + n
                    if u == 7 and i + 1 < NB:
                        q_high(i + 1, 0)
                    if 1 <= n <= NU:
                        for q in range(2):
                            act.wait_ge(pt_ready, 2 * (gn - 1) + q + 1)
                            if gn - 1 >= 2:
                                act.wait_ge(pv_ready, gn - 2)
                            nc.scalar.copy(pt_hi[:, (n - 1) % 2, q].rearrange("p h c -> p (h c)"),
                                           bank[4 + q][0:SC, :]).then_inc(pt_hi_done, 1)
                    if n < NU:
                        act.wait_ge(sub_done, gn + 1)
                        nc.scalar.activation(prob[:, n % 2], prob[:, n % 2], ACT.Exp, scale=SCALE)\
                            .then_inc(exp_done, 1)
                    if n % 2 == 0 and 4 <= n < NU + 4:
                        t = (n - 4) // 2
                        gt = NT * layer + t
                        act.wait_ge(ot_ready, gt + 1)
                        if gt >= 2:
                            act.wait_ge(op_ready, gt - 1)
                        nc.scalar.copy(ot_hi[:, t % 2].rearrange("p k c -> p (k c)"), bank[7][:, 0:D])\
                            .then_inc(ot_hi_done, 1)
                    if u == 6 and i + 1 < NB:
                        xt_high(2 * layer, i + 1, 0, bank[7])
                        xt_high(2 * layer, i + 1, 1, bank[7])
                    if u == 7 and i + 1 < NB:
                        q_high(i + 1, 1)

            def prepare(which):
                for i in range(NB):
                    for c in range(KD):
                        xt_high(2 * which + 1, i, c, bank[(2 * i + c) % 4])

            bias_keys(0)
            norm_std(0)
            attention(0)
            norm_std(1)
            prepare(0)
            act.wait_ge(r_chain, 2)
            nc.scalar.activation(rt[1][:], rt[0][:], ACT.Exp).then_inc(r_act, 1)
            for n in range(NB * M0):
                m = n % M0
                if n == (KV_AFTER + 1) * M0:
                    bias_keys(1)
                act.wait_ge(up_ready, n + 1)
                if n >= 2:
                    act.wait_ge(lo_done, n - 1)
                c = col_at["b1"][0] + m
                nc.scalar.activation(hf[:, n % 2, :], bank[n % 4][:], ACT.Gelu_apprx_tanh, bias=colp[:, c:c + 1])\
                    .then_inc(act_done, 1)
            norm_std(2)
            attention(1)
            norm_std(3)
            prepare(1)
            act.wait_ge(lg_copied, 2)
            nc.scalar.activation(rt[2][:], lg[:], ACT.Sigmoid).then_inc(r_act, 1)

            def shared(v):
                for n in range(M1 * v, M1 * (v + 1)):
                    act.wait_ge(up_ready, NB * M0 + 2 * n + 1)
                    if n >= 2:
                        act.wait_ge(lo_done, NB * M0 + n - 1)
                    nc.scalar.activation(hf[:, n % 2, :], bank[n % 2][:], ACT.Silu).then_inc(act_done, 1)

            def in_high(s):
                act.wait_ge(win_in[s % 2], 16 * (s // 2 + 1))
                if s >= 2:
                    act.wait_ge(su_ready, 2 * (s - 1))
                (hi, _) = expert(s % 2, "hi")
                nc.scalar.copy(hi, raw[s % 2][:, 0:WI].rearrange("p (w k n) -> p w k n", w=2, k=KD)).then_inc(in_hi, 1)

            def down_high(s):
                act.wait_ge(wdn_in[s % 2], 16 * (s // 2 + 1))
                if s >= 2:
                    act.wait_ge(sd_ready, s - 1)
                (_, hi) = expert(s % 2, "hi")
                nc.scalar.copy(hi, raw[s % 2][:, WI:WE].rearrange("p (k n) -> p k n", k=M1)).then_inc(dn_hi, 1)

            def rows_high(s):
                act.wait_ge(st_ready, s + 1)
                if s >= 2:
                    act.wait_ge(su_ready, 2 * (s - 1))
                nc.scalar.copy(xst_hi[:, s % 2].rearrange("p k r -> p (k r)"), bank[6 + s % 2][:]).then_inc(st_hi, 1)

            def slot_silu(s):
                for n in (2 * s, 2 * s + 1):
                    act.wait_ge(sg_ready, n + 1)
                    if n >= 2:
                        act.wait_ge(s_hlo, n - 1)
                    nc.scalar.activation(hf[:, n % 2, :], bank[n % 2][:], ACT.Silu).then_inc(s_silu, 1)

            def slot_out(s):
                act.wait_ge(sd_ready, s + 1)
                if s >= 2:
                    act.wait_ge(y_stored[s % 2], 16 * (s // 2))
                nc.scalar.copy(y_out[:, s % 2].rearrange("p a d -> p (a d)"), bank[4 + s % 2][:]).then_inc(sy_done, 1)

            for v in range(BEFORE):
                shared(v)
            in_high(0)
            rows_high(0)
            for s in range(NSLOT):
                if s + 1 < NSLOT:
                    in_high(s + 1)
                down_high(s)
                slot_silu(s)
                if s + 1 < NSLOT:
                    rows_high(s + 1)
                if s >= 1:
                    slot_out(s - 1)
            slot_out(NSLOT - 1)
            for v in range(BEFORE, NB):
                shared(v)

        @block.vector
        def _(dve):
            v = nc.vector

            v.memset(v3[:], 0.0).then_inc(v_chain, 1)
            v.memset(zero_row[:], 0.0)
            v.memset(ones_row[:].bitcast(F32), 1.0)
            dve.wait_ge(v_chain, 1)
            v.memset(v3[:, :, 0, :, HD:VW], 1.0).then_inc(v_chain, 1)
            dve.wait_ge(small_in, 64)
            v.tensor_copy(ct_hi[:], ct_raw[:]).then_inc(v_chain, 1)
            v.tensor_copy(row_hi[:], row_raw[:]).then_inc(v_chain, 1)
            a = col_at["wr0"][0]
            wr_raw = colp[:, a:a + 2 * KD * E].rearrange("p (w k e) -> p w k e", w=2, k=KD)
            v.tensor_copy(wr_hi[:], wr_raw).then_inc(v_chain, 1)
            dve.wait_ge(raw_in[0], 16)
            src = raw[0][:, 0:WA].rearrange("p (w k n) -> p w k n", w=4, k=KD)
            v.tensor_copy(wq[0, "hi"], src).then_inc(v_chain, 1)
            dve.wait_ge(v_chain, 6)
            v.tensor_tensor(ct_lo[:], ct_raw[:], ct_hi[:].bitcast(F32), ALU.subtract)
            v.tensor_tensor(row_lo[:], row_raw[:], row_hi[:].bitcast(F32), ALU.subtract)
            v.tensor_tensor(wr_lo[:], wr_raw, wr_hi[:].bitcast(F32), ALU.subtract)
            v.tensor_tensor(wq[0, "lo"], src, wq[0, "hi"].bitcast(F32), ALU.subtract).then_inc(first_split, 1)
            v.memset(ones_row[:].bitcast(F32), 1.0).then_inc(setup_dve, 1)

            def tile_stats(phase, t):
                n = NT * phase + t
                v.bn_stats(stats[:, t % 2, :], x_res[:, t, :]).then_inc(stats_done, 1)
                dve.wait_ge(stats_done, n + 1)
                return v.bn_aggr(mv[:, t, :], stats[:, t % 2, :])

            def norm_scale(phase, aggr):
                aggr.then_inc(rstd_done, 1)
                dve.wait_ge(rstd_done, 2 * phase + 1)
                v.tensor_scalar(std[:], mv[:, :, 1], EPS, None, ALU.add).then_inc(var_done, 1)
                dve.wait_ge(std_done, phase + 1)
                v.reciprocal(rstd[:], std[:]).then_inc(rstd_done, 1)
                dve.wait_ge(rstd_done, 2 * phase + 2)

            def normalise(phase, t):
                i, j = t // TPB, t % TPB
                to = xn[:, j, :] if phase < 3 else xn_all[:, t, :]
                if NB * phase + i >= 1 and phase < 3:
                    dve.wait_ge(xt_ready, 2 * (NB * phase + i))
                v.tensor_scalar(to, x_res[:, t, :], mv[:, t, 0:1], rstd[:, t:t + 1],
                                ALU.subtract, ALU.mult).then_inc(xn_ready, 1)

            def xt_low(phase, i, c, src):
                n = 2 * NB * phase + 2 * i + c
                dve.wait_ge(xt_hi, n + 1)
                v.tensor_tensor(xnt_lo[:, c, i * BLK:(i + 1) * BLK], src[:],
                                xnt_hi[:, c, i * BLK:(i + 1) * BLK].bitcast(F32), ALU.subtract).then_inc(xt_lo, 1)

            def keys_values(layer):
                vr = vrest[:]
                ps = bank[5 + layer][0:SC, :]
                dve.wait_ge(k_biased, 2 * layer + 2)
                v.tensor_copy(kx_hi.bitcast(F32R), kf).then_inc(kx_done, 1)
                dve.wait_ge(kx_done, 2 * layer + 1)
                v.tensor_tensor(kx_lo.bitcast(F32R), kf, kx_hi, ALU.subtract).then_inc(kx_done, 1)
                dve.wait_ge(kx_done, 2 * layer + 2)
                dve.wait_ge(consts, 2)
                mask = head_mask[:].unsqueeze(2).to_broadcast([P, HG, SC])
                for g in range(G):
                    for b in range(B):
                        for part, (to, k) in enumerate(((kb_hi, kx_hi), (kb_lo, kx_lo))):
                            one = k[:, g, b * SC:(b + 1) * SC].unsqueeze(1).to_broadcast([P, HG, SC])
                            ins = v.tensor_tensor(to[:, g, b], one, mask, ALU.mult)
                        ins.then_inc(kb_done, 1)
                dve.wait_ge(v_ready, layer + 1)
                heads = "p (b h d) -> p b h d"
                psv = ps.rearrange(heads, b=B, h=H)
                vrv = vr.rearrange(heads, b=B, h=H)
                base = 6 + 4 * layer
                v.tensor_copy(v3[:, :, 0, :, 0:HD], psv).then_inc(v_chain, 1)
                dve.wait_ge(v_chain, base + 1)
                v.tensor_tensor(vrv, psv, v3[:, :, 0, :, 0:HD], ALU.subtract).then_inc(v_chain, 1)
                dve.wait_ge(v_chain, base + 2)
                v.tensor_copy(v3[:, :, 1, :, 0:HD], vrv).then_inc(v_chain, 1)
                dve.wait_ge(v_chain, base + 3)
                v.tensor_tensor(vrv, vrv, v3[:, :, 1, :, 0:HD], ALU.subtract).then_inc(v_chain, 1)
                dve.wait_ge(v_chain, base + 4)
                v.tensor_copy(v3[:, :, 2, :, 0:HD], vrv).then_inc(v_done, 1)

            def attention(layer):
                phase = 2 * layer

                def q_low(i, m):
                    c = col_at[f"bq{layer}"][0] + m
                    dve.wait_ge(q_hi, 2 * (NB * layer + i) + m + 1)
                    v.scalar_tensor_tensor(out=qt_lo[:, m, :], in0=bank[7][:], scalar=colp[:, c:c + 1],
                                           in1=qt_hi[:, m, :].bitcast(F32), op0=ALU.add, op1=ALU.subtract)\
                        .then_inc(q_lo, 1)

                for t in range(TPB):
                    normalise(phase, t)
                xt_low(phase, 0, 0, bank[7])
                xt_low(phase, 0, 1, bank[7])
                q_low(0, 0)
                q_low(0, 1)
                aggr = None
                for n in range(NU + 4):
                    i, u, gn = n // UPB, n % UPB, NU * layer + n
                    if u in (4, 5) and i + 1 < NB:
                        normalise(phase, TPB * (i + 1) + 2 * (u - 4))
                        normalise(phase, TPB * (i + 1) + 2 * (u - 4) + 1)
                    if u == 7 and i + 1 < NB:
                        q_low(i + 1, 0)
                    if n < NU:
                        dve.wait_ge(s_ready, gn + 1)
                        for half in range(2):
                            s = bank[2 * (n % 2) + half][:, 0:SH].rearrange("p (h c) -> p h c", c=SC)
                            ins = v.tensor_reduce(smax[:, n % 2, 4 * half:4 * half + 4], s, AX.X, ALU.max)
                        ins.then_inc(max_done, 1)
                        dve.wait_ge(max_done, gn + 1)
                        if gn >= 2:
                            dve.wait_ge(pt_ready, 2 * (gn - 1))
                        for half in range(2):
                            s = bank[2 * (n % 2) + half][:, 0:SH].rearrange("p (h c) -> p h c", c=SC)
                            m = smax[:, n % 2, 4 * half:4 * half + 4].unsqueeze(2).to_broadcast([P, 4, SC])
                            ins = v.tensor_tensor(prob[:, n % 2, 4 * half:4 * half + 4, :], s, m, ALU.subtract)
                        ins.then_inc(sub_done, 1)
                    if 1 <= n <= NU:
                        for q in range(2):
                            dve.wait_ge(pt_hi_done, 2 * (gn - 1) + q + 1)
                            v.tensor_tensor(pt_lo[:, (n - 1) % 2, q].rearrange("p h c -> p (h c)"),
                                            bank[4 + q][0:SC, :],
                                            pt_hi[:, (n - 1) % 2, q].rearrange("p h c -> p (h c)"),
                                            ALU.subtract).then_inc(pt_lo_done, 1)
                    if n % 2 == 1 and 3 <= n < NU + 3:
                        t = (n - 3) // 2
                        gt = NT * layer + t
                        o = bank[6][:, 0:H * VW].rearrange("p (h d) -> p h d", h=H)
                        dve.wait_ge(pv_ready, 2 * gt + 2)
                        v.reciprocal(rsum[:, t % 2, :], o[:, :, HD]).then_inc(rsum_done, 1)
                        dve.wait_ge(rsum_done, gt + 1)
                        if gt >= 2:
                            dve.wait_ge(ot_ready, gt - 1)
                        v.tensor_tensor(o_n[:, t % 2], o[:, :, 0:HD],
                                        rsum[:, t % 2, :].unsqueeze(2).to_broadcast([P, H, HD]), ALU.mult)\
                            .then_inc(o_done, 1)
                    if n % 2 == 0 and 4 <= n < NU + 4:
                        t = (n - 4) // 2
                        gt = NT * layer + t
                        dve.wait_ge(ot_hi_done, gt + 1)
                        v.tensor_tensor(ot_lo[:, t % 2].rearrange("p k c -> p (k c)"), bank[7][:, 0:D],
                                        ot_hi[:, t % 2].rearrange("p k c -> p (k c)").bitcast(F32),
                                        ALU.subtract).then_inc(ot_lo_done, 1)
                    if n % 2 == 1 and 5 <= n:
                        t = (n - 5) // 2
                        gt = NT * layer + t
                        dve.wait_ge(op_ready, gt + 1)
                        v.scalar_tensor_tensor(out=x_res[:, t, :], in0=bank[7][:, 0:D],
                                               scalar=gate_t[:, layer:layer + 1], in1=x_res[:, t, :],
                                               op0=ALU.mult, op1=ALU.add).then_inc(x_new, 1)
                        dve.wait_ge(x_new, gt + 1)
                        aggr = tile_stats(phase + 1, t)
                    if u == 6 and i + 1 < NB:
                        xt_low(phase, i + 1, 0, bank[7])
                        xt_low(phase, i + 1, 1, bank[7])
                    if u == 7 and i + 1 < NB:
                        q_low(i + 1, 1)
                return aggr

            def prepare(which):
                phase = 2 * which + 1
                for i in range(NB):
                    for t in range(TPB * i, TPB * (i + 1)):
                        normalise(phase, t)
                    for c in range(KD):
                        xt_low(phase, i, c, bank[(2 * i + c) % 4])
                dve.wait_ge(lg_ready, which + 1)
                v.tensor_copy(lg[:], bank[6][:, 0:NT * E].rearrange("p (t e) -> p t e", e=E)).then_inc(lg_copied, 1)
                dve.wait_ge(lg_copied, which + 1)

            chain = [0]

            def link(ins):
                chain[0] += 1
                ins.then_inc(r_chain, 1)
                dve.wait_ge(r_chain, chain[0])

            for i in range(NB):
                dve.wait_ge(x_in[i], 16)
                for t in range(TPB * i, TPB * (i + 1)):
                    aggr = tile_stats(0, t)
            norm_scale(0, aggr)
            keys_values(0)
            dve.wait_ge(gates_done, 1)
            aggr = attention(0)
            norm_scale(1, aggr)
            prepare(0)

            def over_e(a):
                return a.unsqueeze(2).to_broadcast([P, NT, E])
            link(v.tensor_reduce(rs[0][:], lg[:], AX.X, ALU.max))
            link(v.tensor_tensor(rt[0][:], lg[:], over_e(rs[0][:]), ALU.subtract))
            dve.wait_ge(r_act, 1)
            link(v.tensor_reduce(rs[0][:], rt[1][:], AX.X, ALU.add))
            link(v.reciprocal(rs[1][:], rs[0][:]))
            link(v.tensor_tensor(rt[0][:], rt[1][:], over_e(rs[1][:]), ALU.mult))
            for t in range(NT):
                ins = v.max(rt[2][:, t, :], rt[0][:, t, :])
            link(ins)
            link(v.tensor_tensor(rs[0][:], rt[2][:, :, 0], rt[2][:, :, 1], ALU.add))
            link(v.reciprocal(rs[1][:], rs[0][:]))
            link(v.tensor_tensor(rs[2][:], rt[2][:, :, 0], rs[1][:], ALU.mult))
            link(v.tensor_tensor(rs[3][:], rt[2][:, :, 1], rs[1][:], ALU.mult))
            link(v.tensor_tensor(rs[0][:], rs[2][:], rs[3][:], ALU.add))
            link(v.tensor_scalar(rs[1][:], rs[0][:], gate_t[:, 2:3], None, ALU.mult))

            for i in range(NB):
                for m in range(M0):
                    n = M0 * i + m
                    dve.wait_ge(act_done, n + 1)
                    v.tensor_copy(ht_hi[:, m, :], hf[:, n % 2, :]).then_inc(hi_done, 1)
                    dve.wait_ge(hi_done, n + 1)
                    v.tensor_tensor(ht_lo[:, m, :], hf[:, n % 2, :], ht_hi[:, m, :].bitcast(F32), ALU.subtract)\
                        .then_inc(lo_done, 1)
                for j in range(TPB):
                    t = TPB * i + j
                    dve.wait_ge(dn_ready, t + 1)
                    v.scalar_tensor_tensor(out=x_res[:, t, :], in0=bank[4 + t % 2][:, 0:D], scalar=rs[1][:, t:t + 1],
                                           in1=x_res[:, t, :], op0=ALU.mult, op1=ALU.add).then_inc(y_done, 1)
                    dve.wait_ge(y_done, t + 1)
                    aggr = tile_stats(2, t)
                if i == KV_AFTER:
                    keys_values(1)
            norm_scale(2, aggr)
            aggr = attention(1)
            norm_scale(3, aggr)
            prepare(1)

            dve.wait_ge(split_done, 4)
            sel = rt[0][:]
            a, z = ev_at["beta"]
            link(v.tensor_tensor(sel, lg[:], ev[:, a:z].unsqueeze(1).to_broadcast([P, NT, E]), ALU.add))
            mine = sel.unsqueeze(3).to_broadcast([P, NT, E, E])
            other = sel.unsqueeze(2).to_broadcast([P, NT, E, E])
            link(v.tensor_tensor(cmp[:], other, mine, ALU.is_gt))
            link(v.tensor_tensor(rank[:], other, mine, ALU.is_equal))
            for j in range(E):
                ins = v.memset(rank[:, :, j, j:E], 0.0)
            link(ins)
            link(v.tensor_tensor(rank[:], rank[:], cmp[:], ALU.add))
            link(v.tensor_reduce(rt[1][:], rank[:], AX.X, ALU.add))
            link(v.tensor_scalar(chosen[:, 0], rt[1][:], 0.5, None, ALU.is_lt))
            v.tensor_scalar(chosen[:, 2], rt[1][:], 1.5, None, ALU.is_lt).then_inc(rank_ready, 1)
            dve.wait_ge(rank_ready, 1)
            link(v.tensor_tensor(chosen[:, 1], chosen[:, 2], chosen[:, 0], ALU.subtract))
            dve.wait_ge(r_act, 2)
            for c in range(2):
                link(v.tensor_tensor(rt[0][:], chosen[:, c], rt[2][:], ALU.mult))
                link(v.tensor_reduce(rs[c][:], rt[0][:], AX.X, ALU.add))
                link(v.tensor_scalar(weight[:, c, :], rs[c][:], gate_t[:, 3:4], None, ALU.mult))
            dve.wait_ge(routed_pe, 1)
            in_tile = bank[7][:, 0:NT * E].rearrange("p (t e) -> p t e", e=E)
            tile_total = bank[7][:, NT * E:2 * NT * E].rearrange("p (t e) -> p t e", e=E)
            link(v.tensor_copy(cum[0][:], tile_total))
            a, step = 0, 1
            while step < NT:
                link(v.tensor_copy(cum[1 - a][:, 0:step, :], cum[a][:, 0:step, :]))
                link(v.tensor_tensor(cum[1 - a][:, step:NT, :], cum[a][:, step:NT, :], cum[a][:, 0:NT - step, :], ALU.add))
                a, step = 1 - a, 2 * step
            count = cum[a][:, NT - 1, :]
            link(v.tensor_tensor(filled[:], count.unsqueeze(2).to_broadcast([P, E, MAX_PER_EXPERT]), slot_limit[:],
                                 ALU.is_gt))
            link(v.tensor_reduce(es[0][:], filled[:], AX.X, ALU.add))
            link(v.tensor_copy(es[1][:], es[0][:]))
            b, step = 1, 1
            while step < E:
                link(v.tensor_copy(es[3 - b][:, 0:step], es[b][:, 0:step]))
                link(v.tensor_tensor(es[3 - b][:, step:E], es[b][:, step:E], es[b][:, 0:E - step], ALU.add))
                b, step = 3 - b, 2 * step
            link(v.tensor_tensor(es[3][:], es[b][:], es[0][:], ALU.subtract))
            link(v.tensor_scalar(es[3][:], es[3][:], float(R), None, ALU.mult))
            link(v.tensor_tensor(cum[1 - a][:], cum[a][:], tile_total, ALU.subtract))
            link(v.tensor_tensor(cum[a][:], cum[1 - a][:], in_tile, ALU.add))
            link(v.tensor_tensor(cum[1 - a][:], cum[a][:], es[3][:].unsqueeze(1).to_broadcast([P, NT, E]), ALU.add))
            for c in range(2):
                link(v.tensor_tensor(rt[c][:], chosen[:, c], cum[1 - a][:], ALU.mult))
                link(v.tensor_reduce(dest_f[:, c, :], rt[c][:], AX.X, ALU.add))
            link(v.tensor_copy(dest[:], dest_f[:]))
            link(v.tensor_tensor(slot_cmp[:], es[b][0:1, :].unsqueeze(1).to_broadcast([1, NSLOT, E]), slot_id[:],
                                 ALU.is_le))
            link(v.tensor_reduce(slot_e[:], slot_cmp[:], AX.X, ALU.add))
            link(v.tensor_scalar(slot_e[:], slot_e[:], float(E - 1), None, ALU.min))
            v.tensor_copy(slot_expert[:], slot_e[:]).then_inc(route_done, 1)

            def shared_chunk(u, m):
                n = M1 * u + m
                at = u % 2 * M1 + m
                dve.wait_ge(act_done, NB * M0 + n + 1)
                dve.wait_ge(up_ready, NB * M0 + 2 * n + 2)
                v.tensor_tensor(hf[:, n % 2, :], hf[:, n % 2, :], bank[2 + n % 2][:], ALU.mult).then_inc(h_done, 1)
                dve.wait_ge(h_done, n + 1)
                v.tensor_copy(ht_hi[:, at, :], hf[:, n % 2, :]).then_inc(hi_done, 1)
                dve.wait_ge(hi_done, NB * M0 + n + 1)
                v.tensor_tensor(ht_lo[:, at, :], hf[:, n % 2, :], ht_hi[:, at, :].bitcast(F32), ALU.subtract)\
                    .then_inc(lo_done, 1)

            def add_shared(u):
                for t in range(TPB * u, TPB * (u + 1)):
                    dve.wait_ge(dn_ready, NT + t + 1)
                    v.scalar_tensor_tensor(out=x_res[:, t, :], in0=bank[4 + t % 2][:, 0:D], scalar=gate_t[:, 3:4],
                                           in1=x_res[:, t, :], op0=ALU.mult, op1=ALU.add).then_inc(y_done, 1)

            for u in range(BEFORE):
                for m in range(M1):
                    shared_chunk(u, m)
                if u >= 1:
                    add_shared(u - 1)
            add_shared(BEFORE - 1)

            def rows_low(s):
                dve.wait_ge(st_hi, s + 1)
                v.tensor_tensor(xst_lo[:, s % 2].rearrange("p k r -> p (k r)"), bank[6 + s % 2][:],
                                xst_hi[:, s % 2].rearrange("p k r -> p (k r)").bitcast(F32), ALU.subtract)\
                    .then_inc(st_lo, 1)

            def down_low(s):
                dve.wait_ge(dn_hi, s + 1)
                (_, hi), (_, lo) = expert(s % 2, "hi"), expert(s % 2, "lo")
                v.tensor_tensor(lo, raw[s % 2][:, WI:WE].rearrange("p (k n) -> p k n", k=M1), hi.bitcast(F32),
                                ALU.subtract).then_inc(dn_lo, 1)

            def slot_pair(s, pair):
                n, at = 2 * s + pair, 2 * (s % 2) + pair
                dve.wait_ge(s_silu, n + 1)
                dve.wait_ge(su_ready, n + 1)
                v.tensor_tensor(hf[:, n % 2, :], hf[:, n % 2, :], bank[2 + pair][:], ALU.mult).then_inc(s_h, 1)
                dve.wait_ge(s_h, n + 1)
                v.tensor_copy(ht_hi[:, at, :], hf[:, n % 2, :]).then_inc(s_hhi, 1)
                dve.wait_ge(s_hhi, n + 1)
                v.tensor_tensor(ht_lo[:, at, :], hf[:, n % 2, :], ht_hi[:, at, :].bitcast(F32), ALU.subtract)\
                    .then_inc(s_hlo, 1)

            rows_low(0)
            for s in range(NSLOT):
                down_low(s)
                slot_pair(s, 0)
                slot_pair(s, 1)
                if s + 1 < NSLOT:
                    rows_low(s + 1)

            def combine(t):
                for c in range(2):
                    if c == 0:
                        dve.wait_ge(y_done, NT + t + 1)
                        dve.wait_ge(gathered[t % RING], 32 * (t // RING + 1))
                    else:
                        dve.wait_ge(combined, 2 * t + 1)
                    v.scalar_tensor_tensor(out=x_res[:, t, :], in0=y_back[:, t % RING, c, :],
                                           scalar=weight[:, c, t:t + 1], in1=x_res[:, t, :],
                                           op0=ALU.mult, op1=ALU.add).then_inc(combined, 1)

            for u in range(BEFORE, NB):
                for m in range(M1):
                    shared_chunk(u, m)
                    combine(M1 * (u - BEFORE) + m)
                if u > BEFORE:
                    add_shared(u - 1)
            add_shared(NB - 1)
            for t in range(M1 * (NB - BEFORE), NT):
                combine(t)


def kernel(**inputs):
    import numpy as np
    import concourse.bacc as bacc
    from concourse.bass_utils import run_bass_kernel_spmd

    i = {k: np.asarray(v) for k, v in inputs.items()}

    def per_partition(a):
        return a.reshape(-1, P).T

    def rows_per_partition(a):
        return a.reshape(KD, P, -1).transpose(1, 0, 2).reshape(P, -1)

    def pack(gate, up, down):
        def chunks(w):
            e, rows, n = w.shape
            return w.reshape(e, rows // P, P, n).transpose(0, 2, 1, 3).reshape(e, P, -1)
        return np.concatenate([chunks(gate), chunks(up), chunks(down)], axis=2)

    arrays = {
        "x": i["x"].reshape(T, D),
        "ctx_t": i["ctx_1024"].reshape(B * SC, D).T,
        "cols": np.concatenate([
            per_partition(i["L0_xattn_bq"]), per_partition(i["L0_xattn_bk"]), per_partition(i["L0_ffn_b1"]),
            per_partition(i["L1_xattn_bq"]), per_partition(i["L1_xattn_bk"]),
            rows_per_partition(i["L0_ffn_router_w"]), rows_per_partition(i["L1_ffn_gate_w"].T)], axis=1),
        "rows": np.concatenate([i["L0_xattn_bv"], i["L0_xattn_bo"], i["L0_ffn_b2"], i["L1_xattn_bv"],
                                i["L1_xattn_bo"]])[None, :],
        "every": np.concatenate([i["g_xattn"], i["g_ffn"], i["L1_ffn_beta"]]),
        "wa0": np.stack([i["L0_xattn_Wq"], i["L0_xattn_Wk"], i["L0_xattn_Wv"], i["L0_xattn_Wo"]]),
        "w1": i["L0_ffn_w1"],
        "w2": i["L0_ffn_w2"],
        "wa1": np.stack([i["L1_xattn_wq"].T, i["L1_xattn_wk"].T, i["L1_xattn_wv"].T, i["L1_xattn_wo"].T]),
        "w_shared": pack(i["L1_ffn_shared_gate_w"], i["L1_ffn_shared_up_w"], i["L1_ffn_shared_down_w"])[0],
        "w_experts": pack(i["L1_ffn_gate_proj_w"], i["L1_ffn_up_proj_w"], i["L1_ffn_down_proj_w"]),
    }
    arrays = {k: np.ascontiguousarray(a) for k, a in arrays.items()}
    nc = bacc.Bacc("TRN2", target_bir_lowering=False, num_devices=1)
    aps = [nc.dram_tensor("in_" + k, a.shape, F32, kind="ExternalInput").ap() for k, a in arrays.items()]
    out = nc.dram_tensor("out_x", (T, D), F32, kind="ExternalOutput").ap()
    flamingo(nc, *aps, out)
    r = run_bass_kernel_spmd(nc, [{"in_" + k: a for k, a in arrays.items()}], core_ids=[0])
    return r.results[0]["out_x"].reshape(B, SEQ, D)
```

```python
from contextlib import ExitStack

import concourse.bass as bass
from concourse import mybir

F32 = mybir.dt.float32
F32R = mybir.dt.float32r
F16 = mybir.dt.float16
BF16 = mybir.dt.bfloat16
I32 = mybir.dt.int32
ALU = mybir.AluOpType
ACT = mybir.ActivationFunctionType
AX = mybir.AxisListType

P = 128
D = 256
KD = D // P
B = 2
SEQ = 1024
SC = 77
T = B * SEQ
NT = T // P
BLK = 512
NB = T // BLK
TPB = BLK // P
AHEAD = 4
H = 16
HD = D // H
HG = 8
G = H // HG
SW = HG * SC
SH = SW // 2
VW = HD + 1
NU = NT * G
UPB = TPB * G
F0 = 1024
M0 = F0 // P
E = 8
M1W = 512
M1 = M1W // P
R = 256
KS = R // P
ASIDE = 2 * KS
MAX_PER_EXPERT = T // R
XW = D + 1
NSLOT = (2 * T + E * (R - 1)) // R
FILLS = -(-NSLOT * R // (P * ASIDE))
EPS = 1e-5
SLICES = 16
KV_AFTER = 1
SCALE = 0.25

WA = 4 * KD * D
WF = KD * F0
WI = 2 * KD * M1W
WE = WI + M1 * D

COLS = {"bq0": 2, "bk0": 2, "b1": M0, "bq1": 2, "bk1": 2, "wr0": KD * E, "wr1": KD * E}
ROWS = {"bv0": D, "bo0": D, "b2": D, "bv1": D, "bo1": D}
EVERY = {"gates": 4, "beta": E}


def offsets(widths):
    at, n = {}, 0
    for name, w in widths.items():
        at[name] = (n, n + w)
        n += w
    return at, n


def flamingo(nc, x, ctx_t, cols, rows, every, wa0, w1, w2, wa1, w_shared, w_experts, out):
    col_at, n_cols = offsets(COLS)
    row_at, n_rows = offsets(ROWS)
    ev_at, n_every = offsets(EVERY)
    with ExitStack() as ctx:
        def sb(name, shape, dt, where=ctx):
            return where.enter_context(nc.sbuf_tensor(name, shape, dt))

        def sem(name):
            return ctx.enter_context(nc.semaphore(name))

        x_res = sb("x_res", [P, NT, D], F32)
        xnt_hi = sb("xnt_hi", [P, KD, T], F32R)
        xnt_lo = sb("xnt_lo", [P, KD, T], F32R)
        arena = sb("arena", [P, 4 * WE], F32R)
        work = ExitStack()
        slot_cmp = sb("slot_cmp", [1, NSLOT, E], F32, work)
        slot_e = sb("slot_e", [1, NSLOT], F32, work)
        filled = sb("filled", [P, E, MAX_PER_EXPERT], F32, work)
        cum = [sb(f"cum{i}", [P, NT, E], F32, work) for i in range(2)]
        es = [sb(f"es{i}", [P, E], F32, work) for i in range(4)]
        chosen = sb("chosen", [P, 3, NT, E], F32, work)
        dest_f = sb("dest_f", [P, 2, NT], F32, work)
        work.close()
        raw = [sb(f"raw{i}", [P, WE], F32) for i in range(2)]
        keys = ExitStack()
        kb_hi = sb("kb_hi", [P, G, B, HG, SC], F32R, keys)
        kb_lo = sb("kb_lo", [P, G, B, HG, SC], F32R, keys)
        vals = sb("vals", [SC, B, 3, H, VW], BF16, keys)
        ct_hi = sb("ct_hi", [P, KD, B * SC], F32R, keys)
        ct_lo = sb("ct_lo", [P, KD, B * SC], F32R, keys)
        keys.close()
        routing = ExitStack()
        xn_all = sb("xn_all", [P, NT, XW], F32, routing)
        rank = sb("rank", [P, NT, E, E], BF16, routing)
        cmp = sb("cmp", [P, NT, E, E], BF16, routing)
        routing.close()
        odd = ExitStack()
        w_odd = sb("w_odd", [P, 2 * WE], F32R, odd)
        odd.close()
        sb("keys_space", [P, max(G * B * HG * SC * 2 + 2 * KD * B * SC + B * 3 * H * VW // 2 + 16, 2 * WE, NT * XW + 2 * NT * E * E)], F32)
        colp = sb("colp", [P, n_cols], F32)
        ev = sb("ev", [P, n_every], F32)
        gate_t = sb("gate_t", [P, 4], F32)
        biases = ExitStack()
        row_pair = sb("row_pair", [2, n_rows], F32R, biases)
        qt_hi = sb("qt_hi", [P, G, BLK], F32R, biases)
        qt_lo = sb("qt_lo", [P, G, BLK], F32R, biases)
        pt_copy = sb("pt_copy", [SC, 4 * P], F32, biases)
        biases.close()
        slot = ExitStack()
        xs = sb("xs", [P, 2, KS, XW], F32, slot)
        xst_hi = sb("xst_hi", [P, 2, KD, R], F32R, slot)
        xst_lo = sb("xst_lo", [P, 2, KD, R], F32R, slot)
        slot.close()
        back = ExitStack()
        RING = 8
        y_back = sb("y_back", [P, RING, 2, D], F32, back)
        back.close()
        sb("biases_space", [P, max(n_rows + 2 * G * BLK + 4 * P, RING * 2 * D, 2 * KS * XW + 4 * KD * R)], F32)
        back_to = sb("back_to", [P, 4, KS], I32)
        before = sb("before", [P, P], F32)
        all_ones = sb("all_ones", [P, P], F32)
        slot_limit = sb("slot_limit", [P, E, MAX_PER_EXPERT], F32)
        slot_id = sb("slot_id", [1, NSLOT, E], F32)
        slot_expert = sb("slot_expert", [1, NSLOT], I32)
        dest = sb("dest", [P, 2, NT], I32)
        weight = sb("weight", [P, 2, NT], F32)
        ones_pair = sb("ones_pair", [2, P], F32R)
        low_row = sb("low_row", [2, 1], F32)
        wr_pair = sb("wr_pair", [P, 2, KD, 2 * E], F32R)
        ident = sb("ident", [P, P], F32)
        head_mask = sb("head_mask", [P, HG], F32)
        slot_y = ExitStack()
        y_out = sb("y_out", [P, 2, KS, D], F32, slot_y)
        slot_y.close()
        xn = sb("xn", [P, TPB, D], F32)
        stats = sb("stats", [P, 2, 6], F32)
        mv = sb("mv", [P, NT, 2], F32)
        std = sb("std", [P, NT], F32)
        rstd = sb("rstd", [P, NT], F32)
        xm = sb("xm", [P, NT], F32)
        lg = sb("lg", [P, NT, E], F32)
        rt = [sb(f"rt{i}", [P, NT, E], F32) for i in range(3)]
        rs = [sb(f"rs{i}", [P, NT], F32) for i in range(4)]

        att = ExitStack()
        ot_hi = sb("ot_hi", [P, 2, KD, P], F32R, att)
        ot_lo = sb("ot_lo", [P, 2, KD, P], F32R, att)
        o_n = sb("o_n", [P, 2, H, HD], F32, att)
        rsum = sb("rsum", [P, 2, H], F32, att)
        pt_hi = sb("pt_hi", [SC, 2, 2, 4, P], F16, att)
        pt_lo = sb("pt_lo", [SC, 2, 2, 4, P], F16, att)
        smax = sb("smax", [P, 2, HG], F32, att)
        prob = sb("prob", [P, 2, HG, SC], F32, att)
        att.close()
        ffn = ExitStack()
        ht_chunks = [sb(f"ht{m}", [P, 2, BLK], F32R, ffn) for m in reversed(range(M0))][::-1]
        hf = sb("hf", [P, 2, BLK], F32, ffn)
        ffn.close()
        cst = ExitStack()
        ct_raw = sb("ct_raw", [P, KD, B * SC], F32, cst)
        row_raw = sb("row_raw", [2, n_rows], F32, cst)
        row_hi = sb("row_hi", [2, n_rows], F32R, cst)
        key_words = KD * B * SC
        first_keys = sb("first_keys", [P, 3 * key_words], F32, cst)
        sb("att_space", [P, 5120 - 2 * n_rows - 4 * key_words], F32, cst)
        no_rows = sb("no_rows", [P, ASIDE, XW], F32, cst)
        cst.close()

        def key_parts(layer):
            space = first_keys[:] if layer == 0 else xn[:].rearrange("p t d -> p (t d)")
            return (space[:, n * key_words:(n + 1) * key_words].rearrange("p (k n) -> p k n", k=KD) for n in range(3))

        def spread_keys(engine, layer, b, done):
            _, hi, lo = key_parts(layer)
            mask = head_mask[:].unsqueeze(2).to_broadcast([P, HG, SC])
            for g in range(G):
                for to, k in ((kb_hi, hi), (kb_lo, lo)):
                    one = k[:, g, b * SC:(b + 1) * SC].unsqueeze(1).to_broadcast([P, HG, SC])
                    ins = engine.tensor_tensor(to[:, g, b], one, mask, ALU.mult)
                ins.then_inc(done, 1)

        ht_hi, ht_lo = ([h[:, part, :] for h in ht_chunks] for part in range(2))

        psum = ctx.enter_context(nc.psum_tensor("psum", [P, 8, BLK], F32))
        bank = [psum[:, i, :] for i in range(8)]

        wq = {}
        for layer, buf, at in ((0, arena, 0), (1, arena, 0)):
            for part, o in (("hi", 0), ("lo", WA)):
                wq[layer, part] = buf[:, at + o:at + o + WA].rearrange("p (w k n) -> p w k n", w=4, k=KD)
        w1_p = {part: arena[:, 2 * WA + o:2 * WA + o + WF].rearrange("p (k n) -> p k n", k=KD)
                for part, o in (("hi", 0), ("lo", WF))}
        w2_p = {part: arena[:, 2 * WA + 2 * WF + o:2 * WA + 2 * WF + o + WF].rearrange("p (k n) -> p k n", k=M0)
                for part, o in (("hi", 0), ("lo", WF))}

        def expert(buf, part):
            w = {"shared": arena[:, 2 * WE:4 * WE], 0: arena[:, 0:2 * WE], 1: w_odd[:]}[buf]
            w = w[:, WE:2 * WE] if part == "lo" else w[:, 0:WE]
            return (w[:, 0:WI].rearrange("p (w k n) -> p w k n", w=2, k=KD),
                    w[:, WI:WE].rearrange("p (k n) -> p k n", k=M1))

        x_rows = nc.dram_tensor("x_rows", (NSLOT * R, XW), F32, kind="Internal").ap()
        y_rows = nc.dram_tensor("y_rows", (2 * T + ASIDE * P, D), F32, kind="Internal").ap()

        small_in = sem("small_in")
        x_in = [sem(f"x_in{i}") for i in range(NB)]
        raw_in = [sem(f"raw_in{i}") for i in range(2)]
        first_split = sem("first_split")
        split_done = sem("split_done")
        consts = sem("consts")
        pool_chain = sem("pool_chain")
        low_row_done = sem("low_row_done")
        kv_split = sem("kv_split")
        slice_hi = sem("slice_hi")
        pt_lo_pool = sem("pt_lo_pool")
        vals_cleared, vals_chain = sem("vals_cleared"), sem("vals_chain")
        setup_dve = sem("setup_dve")
        gates_done = sem("gates_done")
        k_ready, v_ready = sem("k_ready"), sem("v_ready")
        k_biased = sem("k_biased")
        kx_done, kb_first, kb_second, v_done = sem("kx_done"), sem("kb_first"), sem("kb_second"), sem("v_done")
        v_chain = sem("v_chain")
        stats_done, var_done, std_done, rstd_done = sem("stats_done"), sem("var_done"), sem("std_done"), sem("rstd_done")
        aggr_done = sem("aggr_done")
        xn_ready, xt_ready, xt_hi, xt_lo = sem("xn_ready"), sem("xt_ready"), sem("xt_hi"), sem("xt_lo")
        q_ready, q_hi, q_lo = sem("q_ready"), sem("q_hi"), sem("q_lo")
        s_ready, max_done, sub_done, exp_done = sem("s_ready"), sem("max_done"), sem("sub_done"), sem("exp_done")
        pt_ready, pt_hi_done, pt_lo_done = sem("pt_ready"), sem("pt_hi_done"), sem("pt_lo_done")
        pv_ready, rsum_done, o_done = sem("pv_ready"), sem("rsum_done"), sem("o_done")
        ot_ready, ot_hi_done, ot_lo_done = sem("ot_ready"), sem("ot_hi_done"), sem("ot_lo_done")
        op_ready, x_new = sem("op_ready"), sem("x_new")
        lg_ready, lg_copied, r_chain, r_act = sem("lg_ready"), sem("lg_copied"), sem("r_chain"), sem("r_act")
        up_ready, act_done, h_done, hi_done, lo_done = (sem("up_ready"), sem("act_done"), sem("h_done"),
                                                        sem("hi_done"), sem("lo_done"))
        dn_ready, y_done = sem("dn_ready"), sem("y_done")
        stored = sem("stored")
        zeroed, routed_pe, rank_ready, route_done = sem("zeroed"), sem("routed_pe"), sem("rank_ready"), sem("route_done")
        scattered = sem("scattered")
        rows_in = [sem(f"rows_in{i}") for i in range(2)]
        y_stored = [sem(f"y_stored{i}") for i in range(2)]
        aside_ready = sem("aside_ready")
        ids_ready, ids_read = sem("ids_ready"), sem("ids_read")
        gathered = [sem(f"gathered{i}") for i in range(RING)]
        win_in = [sem(f"win_in{i}") for i in range(2)]
        wdn_in = [sem(f"wdn_in{i}") for i in range(2)]
        in_hi, in_lo, dn_hi, dn_lo = sem("in_hi"), sem("in_lo"), sem("dn_hi"), sem("dn_lo")
        st_ready, st_hi, st_lo = sem("st_ready"), sem("st_hi"), sem("st_lo")
        sg_ready, su_ready, s_silu, s_h, s_hhi, s_hlo = (sem("sg_ready"), sem("su_ready"), sem("s_silu"), sem("s_h"),
                                                         sem("s_hhi"), sem("s_hlo"))
        sd_ready, sy_done = sem("sd_ready"), sem("sy_done")
        p_hi, p_lo = sem("p_hi"), sem("p_lo")
        qo_hi = sem("qo_hi")
        kvw_in, qo_in = sem("kvw_in"), sem("qo_in")
        xn_all_ready = sem("xn_all_ready")
        xm_done = sem("xm_done")
        weighted, weights_done = sem("weighted"), sem("weights_done")
        even_combined, odd_combined = sem("even_combined"), sem("odd_combined")

        block = ctx.enter_context(nc.Block())

        EARLY = NT - TPB

        def logits_at(t):
            at = H * VW + t * 2 * E if t < EARLY else (t - EARLY) * 2 * E
            return slice(at, at + 2 * E)

        def extras(layer, n):
            i, u = n // UPB, n % UPB
            if n < 0:
                return []
            if u == UPB - 1 and i + 1 < NB:
                return [("q", layer, i + 1, 0)]
            if u == 0 and 1 <= i < NB:
                return [("q", layer, i, 1)]
            if n == NU + 1:
                return [("x", layer, "ffn", i - 2, c) for c in range(KD)]
            if u in (1, 2) and 2 <= i < NB:
                return [("x", layer, "ffn", i - 2, u - 1)]
            if u in (5, 6) and i + 1 < NB:
                return [("x", layer, "queries", i + 1, u - 5)]
            return []

        def turn(layer, what, i):
            return 2 * NB * layer + {"queries": (0, 1, 2, 4), "ffn": (3, 5, 6, 7)}[what][i]

        work_bank = {}
        for layer in range(2):
            for n in range(-1, NU + 5):
                names = list(extras(layer, n))
                if n == -1:
                    names += [(kind, layer) + what + (c,) for kind, what in (("x", ("queries", 0)), ("q", (0,)))
                              for c in range(KD)]
                if n % 2 == 0 and 4 <= n < NU + 4:
                    names.append(("o", layer, (n - 4) // 2))
                if n % 2 == 1 and 5 <= n < NU + 4:
                    names.append(("y", layer, (n - 5) // 2))
                if n == NU + 4:
                    names += [("x", layer, "ffn", NB - 1, c) for c in range(KD)]
                for name in names:
                    if name[0] == "x" and n >= NU:
                        work_bank[name] = (7, 5)[name[-1]]
                        continue
                    work_bank[name] = (7, 3, 2)[len(work_bank) % 3] if n < NU and (layer, n) != (1, -1) else 7

        def by_pool(gn, q):
            return q == 1 and gn >= UPB

        def low_parts_of(gn, q):
            if by_pool(gn, q):
                return pt_lo_pool, gn - UPB + 1
            return pt_lo_done, 2 * gn + q + 1 if gn < UPB else gn + UPB + 1

        NORM_GROUPS = 2 + NB

        def norm_tiles(layer, group):
            if group >= 2:
                return TPB * (group - 2), TPB * (group - 1)
            first = TPB if layer == 0 else NT - TPB
            return (0, first) if group == 0 else (first, NT)

        def parts_of(n):
            return (p_lo, n + 1) if n < AHEAD else (lo_done, NB * M0 + n - AHEAD + 1)

        PIECES = 4 + 1

        def split_dst(p):
            if p == 0:
                return wq[0, "hi"], wq[0, "lo"], WA
            if p == 1:
                return w1_p["hi"], w1_p["lo"], WF
            if p == 2:
                return w2_p["hi"], w2_p["lo"], WF
            if p == 3:
                return wq[1, "hi"], wq[1, "lo"], WA
            return arena[:, 2 * WE:3 * WE], arena[:, 3 * WE:4 * WE], WE

        @block.sync
        def _(sp):
            sp.dma_start(raw[0][:, WA // 4:3 * WA // 4].rearrange("p (w k n) -> p w k n", w=2, k=KD),
                         wa0[1:3].rearrange("w (k p) n -> p w k n", p=P)).then_inc(kvw_in, 16)
            sp.dma_start(colp[:], cols).then_inc(small_in, 16)
            sp.dma_start(ct_raw[:], ctx_t.rearrange("(k p) n -> p k n", p=P)).then_inc(small_in, 16)
            sp.dma_start(row_raw[:], rows.partition_broadcast(2)).then_inc(small_in, 16)
            sp.dma_start(ev[:], every.partition_broadcast(P)).then_inc(small_in, 16)
            for i in range(NB):
                sp.dma_start(x_res[:, TPB * i:TPB * (i + 1), :],
                             x[BLK * i:BLK * (i + 1), :].rearrange("(t p) d -> p t d", p=P)).then_inc(x_in[i], 16)
                if i == 0:
                    for w in (0, 3):
                        sp.dma_start(raw[0][:, w * WA // 4:(w + 1) * WA // 4].rearrange("p (k n) -> p k n", k=KD),
                                     wa0[w].rearrange("(k p) n -> p k n", p=P)).then_inc(qo_in, 16)
            for p in range(1, PIECES):
                if p == 2:
                    sp.wait_ge(first_split, 1)
                    sp.wait_ge(setup_dve, 1)
                if p > 2:
                    sp.wait_ge(split_done, p - 2)
                to = raw[p % 2]
                if p == 1:
                    sp.dma_start(to[:, 0:WF].rearrange("p (k n) -> p k n", k=KD),
                                 w1.rearrange("(k p) n -> p k n", p=P)).then_inc(raw_in[p % 2], 16)
                elif p == 2:
                    sp.dma_start(to[:, 0:WF].rearrange("p (k n) -> p k n", k=M0),
                                 w2.rearrange("(k p) n -> p k n", p=P)).then_inc(raw_in[p % 2], 16)
                elif p == 3:
                    sp.dma_start(to[:, 0:WA].rearrange("p (w k n) -> p w k n", w=4, k=KD),
                                 wa1.rearrange("w (k p) n -> p w k n", p=P)).then_inc(raw_in[p % 2], 16)
                else:
                    sp.dma_start(to[:], w_shared).then_inc(raw_in[p % 2], 16)
                if p == 3:
                    sp.wait_ge(setup_dve, 1)
                    sp.wait_ge(aside_ready, 2)
                    for a in range(0, NSLOT * R // P, ASIDE):
                        z = min(a + ASIDE, NSLOT * R // P)
                        sp.dma_start(x_rows[a * P:z * P, :].rearrange("(n p) d -> p n d", p=P), no_rows[:, 0:z - a, :])\
                            .then_inc(zeroed, 16)

            def load_in(s):
                if s >= 2:
                    sp.wait_ge(in_lo, s - 1)
                e = sp.value_load(slot_expert[0:1, s:s + 1], min_val=0, max_val=E - 1)
                sp.dma_start(raw[s % 2][:, 0:WI], w_experts[bass.ds(e, 1), :, 0:WI].rearrange("e p n -> p (e n)"))\
                    .then_inc(win_in[s % 2], 16)
                return e

            def load_down(s, e):
                if s >= 2:
                    sp.wait_ge(dn_lo, s - 1)
                sp.dma_start(raw[s % 2][:, WI:WE], w_experts[bass.ds(e, 1), :, WI:WE].rearrange("e p n -> p (e n)"))\
                    .then_inc(wdn_in[s % 2], 16)

            def load_rows(s):
                if s >= 2:
                    sp.wait_ge(st_ready, s - 1)
                    sp.wait_ge(ids_read, s - 1)
                sp.dma_start(xs[:, s % 2], x_rows[s * R:(s + 1) * R, :].rearrange("(a p) d -> p a d", p=P))\
                    .then_inc(rows_in[s % 2], 16)

            sp.wait_ge(route_done, 1)
            sp.wait_ge(weights_done, 2)
            sp.wait_ge(split_done, 4)
            for s in range(2):
                load_down(s, load_in(s))
            sp.wait_ge(scattered, 16 * 2 * NT)
            load_rows(0)
            load_rows(1)
            for s in range(NSLOT):
                if s + 2 < NSLOT:
                    e = load_in(s + 2)
                    load_rows(s + 2)
                    load_down(s + 2, e)

            sp.wait_ge(y_stored[0], 16 * KS * ((NSLOT + 1) // 2))
            sp.wait_ge(y_stored[1], 16 * KS * (NSLOT // 2))
            sp.wait_ge(st_lo, NSLOT)
            by_tile = y_rows[0:2 * T, :].rearrange("(c t p) d -> t p c d", c=2, p=P)
            for t in range(NT):
                if t >= RING:
                    sp.wait_ge(odd_combined if t % 2 else even_combined, 2 * ((t - RING) // 2) + 2)
                sp.dma_start(y_back[:, t % RING], by_tile[t]).then_inc(gathered[t % RING], 16)

            for i in range(NB):
                sp.wait_ge(even_combined, TPB * (i + 1))
                sp.wait_ge(odd_combined, TPB * (i + 1))
                sp.dma_start(out[BLK * i:BLK * (i + 1), :].rearrange("(t p) d -> p t d", p=P),
                             x_res[:, TPB * i:TPB * (i + 1), :]).then_inc(stored, 16)
            sp.wait_ge(stored, 16 * NB)

        def raw_pieces(i):
            return raw[i][:, 0:WA].rearrange("p (w k n) -> p w k n", w=4, k=KD)

        def raw_value(p):
            return 16 * ((p + 1) // 2)

        @block.gpsimd
        def _(pool):
            nc.gpsimd.memset(ident[:], 0.0).then_inc(pool_chain, 1)
            nc.gpsimd.memset(head_mask[:], 1.0).then_inc(pool_chain, 1)
            pool.wait_ge(pool_chain, 2)
            nc.gpsimd.iota(low_row[:], [[0, 1]], base=0, channel_multiplier=-1,
                           allow_small_or_imprecise_dtypes=True).then_inc(low_row_done, 1)
            nc.gpsimd.affine_select(out=ident[:], in_=ident[:], compare_op=ALU.not_equal, fill=1.0, base=0,
                                    pattern=[[-1, P]], channel_multiplier=1).then_inc(consts, 1)
            nc.gpsimd.affine_select(out=head_mask[:], in_=head_mask[:], compare_op=ALU.is_ge, fill=0.0, base=0,
                                    pattern=[[-HD, HG]], channel_multiplier=1).then_inc(pool_chain, 1)
            pool.wait_ge(pool_chain, 3)
            nc.gpsimd.affine_select(out=head_mask[:], in_=head_mask[:], compare_op=ALU.is_ge, fill=0.0, base=HD - 1,
                                    pattern=[[HD, HG]], channel_multiplier=-1).then_inc(consts, 1)
            nc.gpsimd.iota(no_rows[:, :, D], [[P, ASIDE]], base=2 * T, channel_multiplier=1,
                           allow_small_or_imprecise_dtypes=True).then_inc(aside_ready, 1)
            nc.gpsimd.memset(before[:], 1.0).then_inc(pool_chain, 1)
            pool.wait_ge(pool_chain, 4)
            nc.gpsimd.affine_select(out=before[:], in_=before[:], compare_op=ALU.is_gt, fill=0.0, base=0,
                                    pattern=[[1, P]], channel_multiplier=-1).then_inc(consts, 1)
            nc.gpsimd.memset(all_ones[:], 1.0).then_inc(consts, 1)
            nc.gpsimd.iota(slot_limit[:], [[0, E], [R, MAX_PER_EXPERT]], base=0, channel_multiplier=0,
                           allow_small_or_imprecise_dtypes=True).then_inc(consts, 1)
            nc.gpsimd.iota(slot_id[:], [[1, NSLOT], [0, E]], base=0, channel_multiplier=0,
                           allow_small_or_imprecise_dtypes=True).then_inc(consts, 1)
            nc.gpsimd.memset(no_rows[:, :, 0:D], 0.0).then_inc(aside_ready, 1)
            pool.wait_ge(qo_hi, 1)
            nc.gpsimd.tensor_tensor(wq[0, "lo"][:, 0::3], raw_pieces(0)[:, 0::3], wq[0, "hi"][:, 0::3].bitcast(F32),
                                    ALU.subtract).then_inc(first_split, 1)
            pool.wait_ge(kx_done, 2)
            spread_keys(nc.gpsimd, 0, 1, kb_second)
            done = 4

            def low_probs(layer, between=lambda: None):
                for gn in range(NU * layer, NU * (layer + 1)):
                    if by_pool(gn, 1):
                        pool.wait_ge(pt_hi_done, 2 * gn + 2)
                        nc.gpsimd.tensor_tensor(pt_lo[:, gn % 2, 1].rearrange("p h c -> p (h c)"), pt_copy[:],
                                                pt_hi[:, gn % 2, 1].rearrange("p h c -> p (h c)"), ALU.subtract)\
                            .then_inc(pt_lo_pool, 1)
                        between()

            for p in range(1, PIECES - 1):
                hi, lo, n = split_dst(p)
                if p == 3:
                    low_probs(0)
                pool.wait_ge(raw_in[p % 2], raw_value(p))
                if p == 3:
                    pool.wait_ge(op_ready, NT)
                src = raw[p % 2][:, 0:n]
                if len(hi.shape) == 3:
                    src = src.rearrange("p (k n) -> p k n", k=hi.shape[1])
                if len(hi.shape) == 4:
                    src = src.rearrange("p (w k n) -> p w k n", w=4, k=KD)
                nc.gpsimd.tensor_copy(hi, src).then_inc(pool_chain, 1)
                done += 1
                pool.wait_ge(pool_chain, done)
                nc.gpsimd.tensor_tensor(lo, src, hi.bitcast(F32), ALU.subtract).then_inc(split_done, 1)

            slices = [slice(a, a + WE // SLICES) for a in range(0, WE, WE // SLICES)]
            hi, lo, _ = split_dst(PIECES - 1)
            parts = []

            def split_slice():
                if len(parts) == SLICES:
                    return
                part = slices[len(parts)]
                if not parts:
                    pool.wait_ge(raw_in[(PIECES - 1) % 2], raw_value(PIECES - 1))
                    pool.wait_ge(dn_ready, NT)
                src = raw[(PIECES - 1) % 2]
                nc.gpsimd.tensor_copy(hi[:, part], src[:, part]).then_inc(slice_hi, 1)
                parts.append(part)
                pool.wait_ge(slice_hi, len(parts))
                ins = nc.gpsimd.tensor_tensor(lo[:, part], src[:, part], hi[:, part].bitcast(F32), ALU.subtract)
                if len(parts) == SLICES:
                    ins.then_inc(split_done, 1)

            pool.wait_ge(kx_done, 4)
            spread_keys(nc.gpsimd, 1, 1, kb_second)
            low_probs(1, split_slice)

            def pooled_low(n):
                pool.wait_ge(p_hi, n + 1)
                nc.gpsimd.tensor_tensor(ht_lo[n], hf[:, n % 2, :], ht_hi[n].bitcast(F32), ALU.subtract).then_inc(p_lo, 1)

            for n in range(AHEAD):
                pooled_low(n)

            pool.wait_ge(lg_ready, 2)
            nc.gpsimd.iota(xn_all[:, :, D], [[P, NT]], base=0, channel_multiplier=1,
                           allow_small_or_imprecise_dtypes=True).then_inc(ids_ready, 1)
            pool.wait_ge(route_done, 1)
            pool.wait_ge(xn_all_ready, NT)
            pool.wait_ge(ids_ready, 1)
            for c in range(2):
                if c == 1:
                    pool.wait_ge(scattered, 16 * NT)
                    nc.gpsimd.tensor_scalar(xn_all[:, :, D], xn_all[:, :, D], float(T), None, ALU.add)\
                        .then_inc(ids_ready, 1)
                    pool.wait_ge(ids_ready, 2)
                for t in range(NT):
                    pool.indirect_dma_start(x_rows, bass.IndirectOffsetOnAxis(ap=dest[:, c, t:t + 1], axis=0),
                                            xn_all[:, t, :], None).then_inc(scattered, 16)

            def rows_back(s):
                pool.wait_ge(sy_done, s + 1)
                for a in range(KS):
                    pool.indirect_dma_start(y_rows, bass.IndirectOffsetOnAxis(ap=back_to[:, s % 4, a:a + 1], axis=0),
                                            y_out[:, s % 2, a, :], None).then_inc(y_stored[s % 2], 16)

            for s in range(NSLOT):
                pool.wait_ge(in_hi, s + 1)
                if s >= 2:
                    pool.wait_ge(su_ready, 2 * (s - 1))
                (hi, _), (lo, _) = expert(s % 2, "hi"), expert(s % 2, "lo")
                src = raw[s % 2][:, 0:WI].rearrange("p (w k n) -> p w k n", w=2, k=KD)
                nc.gpsimd.tensor_tensor(lo, src, hi.bitcast(F32), ALU.subtract).then_inc(in_lo, 1)
                if s >= 2:
                    rows_back(s - 2)
                if s >= 4:
                    pool.wait_ge(y_stored[s % 2], 16 * KS * (s // 2 - 1))
                pool.wait_ge(rows_in[s % 2], 16 * (s // 2 + 1))
                nc.gpsimd.tensor_copy(back_to[:, s % 4], xs[:, s % 2, :, D]).then_inc(ids_read, 1)
            for s in (NSLOT - 2, NSLOT - 1):
                pool.wait_ge(ids_read, s + 1)
                rows_back(s)

            for t in range(0, NT, 2):
                pool.wait_ge(y_done, NT + t + 1)
                for c in range(2):
                    pool.wait_ge(weighted, t + c + 1)
                    if c == 1:
                        pool.wait_ge(even_combined, t + 1)
                    nc.gpsimd.tensor_tensor(x_res[:, t, :], x_res[:, t, :], y_back[:, t % RING, c, :], ALU.add)\
                        .then_inc(even_combined, 1)

        @block.tensor
        def _(pe):
            def three(ps, w_hi, w_lo, m_hi, m_lo, start, stop, inc=None):
                nc.tensor.matmul(ps, w_lo, m_hi, start=start, stop=False)
                nc.tensor.matmul(ps, w_hi, m_lo, start=False, stop=False)
                return nc.tensor.matmul(ps, w_hi, m_hi, start=False, stop=stop)

            def kv(layer, k_bank, v_bank):
                w_hi, w_lo = wq[layer, "hi"], wq[layer, "lo"]
                for m in range(G):
                    for k in range(KD):
                        mm = three(k_bank[:, m * B * SC:(m + 1) * B * SC],
                                   w_hi[:, 1, k, m * P:(m + 1) * P], w_lo[:, 1, k, m * P:(m + 1) * P],
                                   ct_hi[:, k, :], ct_lo[:, k, :], k == 0, k == KD - 1)
                mm.then_inc(k_ready, 1)
                a, z = row_at[f"bv{layer}"]
                pe.wait_ge(setup_dve, 1)
                for b in range(B):
                    ps = v_bank[0:SC, b * D:(b + 1) * D]
                    for k in range(KD):
                        three(ps, ct_hi[:, k, b * SC:(b + 1) * SC], ct_lo[:, k, b * SC:(b + 1) * SC],
                              w_hi[:, 2, k, :], w_lo[:, 2, k, :], k == 0, False)
                    mm = nc.tensor.matmul(ps, ones_pair[:, 0:SC], row_pair[:, a:z], start=False, stop=True)
                mm.then_inc(v_ready, 1)

            reader = {}

            def take_work(name, *last):
                b = work_bank[name]
                if b in reader:
                    pe.wait_ge(*reader[b])
                reader[b] = last
                return bank[b]

            def x_transposed(layer, what, i, c):
                at = turn(layer, what, i)
                work = take_work(("x", layer, what, i, c), xt_lo, KD * at + c + 1)
                for j in range(TPB):
                    if c == 0:
                        pe.wait_ge(xn_ready, TPB * at + j + 1)
                    mm = nc.tensor.transpose(work[:, j * P:(j + 1) * P], xn[:, j, c * P:(c + 1) * P], ident[:])
                mm.then_inc(xt_ready, 1)

            def queries(layer, i, m):
                w_hi, w_lo = wq[layer, "hi"], wq[layer, "lo"]
                work = take_work(("q", layer, i, m), q_lo, G * (NB * layer + i) + m + 1)
                pe.wait_ge(xt_lo, KD * turn(layer, "queries", i) + KD)
                for k in range(KD):
                    mm = three(work, w_hi[:, 0, k, m * P:(m + 1) * P], w_lo[:, 0, k, m * P:(m + 1) * P],
                               xnt_hi[:, k, i * BLK:(i + 1) * BLK], xnt_lo[:, k, i * BLK:(i + 1) * BLK],
                               k == 0, k == KD - 1)
                mm.then_inc(q_ready, 1)

            def do_extras(layer, n):
                for kind, *what in extras(layer, n):
                    (x_transposed if kind == "x" else queries)(*what)

            def attention(layer, ahead):
                w_hi, w_lo = wq[layer, "hi"], wq[layer, "lo"]
                bo = row_at[f"bo{layer}"]

                def scores(n):
                    gn, i, g, b = NU * layer + n, n // UPB, n % G, n // (NU // B)
                    j = n % UPB // G
                    pe.wait_ge(q_lo, 2 * (NB * layer + i) + g + 1)
                    if gn >= 1:
                        pe.wait_ge(sub_done, gn)
                    for half in range(2):
                        ps = bank[half][:, 0:SH].rearrange("p (h c) -> p h c", c=SC)
                        heads = slice(half * HG // 2, (half + 1) * HG // 2)
                        mm = three(ps, qt_hi[:, g, j * P:(j + 1) * P], qt_lo[:, g, j * P:(j + 1) * P],
                                   kb_hi[:, g, b, heads, :], kb_lo[:, g, b, heads, :], True, True)
                    mm.then_inc(s_ready, 1)

                def probs_transposed(n):
                    gn = NU * layer + n
                    pe.wait_ge(exp_done, gn + 1)
                    for q in range(2):
                        if gn >= 1:
                            if by_pool(gn - 1, q):
                                pe.wait_ge(pt_hi_done, 2 * (gn - 1) + q + 1)
                            else:
                                pe.wait_ge(*low_parts_of(gn - 1, q))
                        for h in range(4):
                            mm = nc.tensor.transpose(bank[4 + q][0:SC, h * P:(h + 1) * P],
                                                     prob[:, n % 2, 4 * q + h, :], ident[:])
                        mm.then_inc(pt_ready, 1)

                def values(n):
                    gn, b, g = NU * layer + n, n // (NU // B), n % G
                    if g == 0 and gn >= 2:
                        pe.wait_ge(o_done, gn // 2)
                    for q in range(2):
                        pe.wait_ge(pt_hi_done, 2 * gn + q + 1)
                        pe.wait_ge(*low_parts_of(gn, q))
                        for h in range(4):
                            head = g * HG + 4 * q + h
                            ps = bank[6][:, head * VW:(head + 1) * VW]
                            hi, lo = pt_hi[:, n % 2, q, h, :], pt_lo[:, n % 2, q, h, :]
                            nc.tensor.matmul(ps, hi, vals[:, b, 2, head, :], start=True, stop=False)
                            nc.tensor.matmul(ps, hi, vals[:, b, 1, head, :], start=False, stop=False)
                            nc.tensor.matmul(ps, hi, vals[:, b, 0, head, :], start=False, stop=False)
                            nc.tensor.matmul(ps, lo, vals[:, b, 1, head, :], start=False, stop=False)
                            mm = nc.tensor.matmul(ps, lo, vals[:, b, 0, head, :], start=False, stop=True)
                    mm.then_inc(pv_ready, 1)

                def out_transposed(t):
                    gt = NT * layer + t
                    work = take_work(("o", layer, t), ot_lo_done, gt + 1)
                    pe.wait_ge(o_done, gt + 1)
                    flat = o_n[:, t % 2].rearrange("p h d -> p (h d)")
                    for c in range(KD):
                        mm = nc.tensor.transpose(work[:, c * P:(c + 1) * P], flat[:, c * P:(c + 1) * P], ident[:])
                    mm.then_inc(ot_ready, 1)

                def out_projected(t):
                    gt = NT * layer + t
                    ps = take_work(("y", layer, t), x_new, gt + 1)[:, 0:D]
                    pe.wait_ge(ot_lo_done, gt + 1)
                    for k in range(KD):
                        three(ps, ot_hi[:, t % 2, k, :], ot_lo[:, t % 2, k, :],
                              w_hi[:, 3, k, :], w_lo[:, 3, k, :], k == 0, False)
                    nc.tensor.matmul(ps, ones_pair[:], row_pair[:, bo[0]:bo[1]], start=False, stop=True)\
                        .then_inc(op_ready, 1)

                pe.wait_ge(kb_first, G * (layer + 1))
                for n in range(NU + 4):
                    i, u = n // UPB, n % UPB
                    if n == NU // B:
                        pe.wait_ge(kb_second, G * (layer + 1))
                    if n < NU:
                        scores(n)
                    if 1 <= n <= NU:
                        probs_transposed(n - 1)
                    if n == NU:
                        reader[5] = (pt_hi_done, 2 * NU * (layer + 1))
                    do_extras(layer, n)
                    if n == 2:
                        pe.wait_ge(v_done, layer + 1)
                    if 2 <= n < NU + 2:
                        values(n - 2)
                    if n % 2 == 0 and 4 <= n < NU + 4:
                        out_transposed((n - 4) // 2)
                    if n % 2 == 1 and 5 <= n:
                        out_projected((n - 5) // 2)
                    if n == NU:
                        ahead(0)
                    if n == NU + 2:
                        ahead(1)
                    if n == NU + 3:
                        ahead(2)
                        ahead(3)

            def logits(layer, tiles):
                for t in tiles:
                    if t % TPB == 0:
                        pe.wait_ge(xt_lo, KD * turn(layer, "ffn", t // TPB) + KD)
                    if t == EARLY:
                        pe.wait_ge(o_done, NT * (layer + 1))
                    for k in range(KD):
                        ps = bank[6][:, logits_at(t)]
                        nc.tensor.matmul(ps, xnt_hi[:, k, t * P:(t + 1) * P], wr_pair[:, layer, k, :],
                                         start=k == 0, stop=False)
                        mm = nc.tensor.matmul(ps[:, 0:E], xnt_lo[:, k, t * P:(t + 1) * P],
                                              wr_pair[:, layer, k, 0:E], start=False, stop=k == KD - 1)
                if t == NT - 1:
                    mm.then_inc(lg_ready, 1)

            def ffn_up(n):
                i, m = n // M0, n % M0
                if n >= 4:
                    pe.wait_ge(act_done, n - 3)
                for k in range(KD):
                    mm = three(bank[n % 4][:], w1_p["hi"][:, k, m * P:(m + 1) * P],
                               w1_p["lo"][:, k, m * P:(m + 1) * P],
                               xnt_hi[:, k, i * BLK:(i + 1) * BLK], xnt_lo[:, k, i * BLK:(i + 1) * BLK],
                               k == 0, k == KD - 1)
                mm.then_inc(up_ready, 1)

            def early_logits(layer, m):
                if m == AHEAD - 1:
                    logits(layer, range(EARLY // 2))

            def ffn_ahead(m):
                if m == 0:
                    pe.wait_ge(split_done, 2)
                    pe.wait_ge(sub_done, NU)
                    for b in (2, 3):
                        pe.wait_ge(*reader[b])
                ffn_up(m)
                early_logits(0, m)

            pe.wait_ge(kv_split, 1)
            pe.wait_ge(consts, 2)
            kv(0, bank[4], bank[6])
            for c in range(KD):
                x_transposed(0, "queries", 0, c)
            pe.wait_ge(first_split, 1)
            for m in range(G):
                queries(0, 0, m)
            attention(0, ffn_ahead)
            for i in range(NB):
                for m in range(AHEAD if i == 0 else 0, M0):
                    ffn_up(M0 * i + m)
                    if i == 0 and m in (5, 6):
                        x_transposed(0, "ffn", NB - 1, m - 5)
                if i == 0:
                    logits(0, range(EARLY // 2, NT))
                if i == KV_AFTER:
                    pe.wait_ge(split_done, 3)
                    pe.wait_ge(lg_copied, 2)
                    kv(1, bank[7], bank[6])
                    reader[7] = (k_biased, 4)
                for j in range(TPB):
                    t = TPB * i + j
                    if i == NB - 1:
                        if j < KD:
                            x_transposed(1, "queries", 0, j)
                        else:
                            queries(1, 0, j - KD)
                    if t >= 2:
                        pe.wait_ge(y_done, t - 1)
                    for k in range(M0):
                        if j == 0:
                            pe.wait_ge(lo_done, M0 * i + k + 1)
                        three(bank[4 + t % 2][:, 0:D], ht_hi[k][:, j * P:(j + 1) * P], ht_lo[k][:, j * P:(j + 1) * P],
                              w2_p["hi"][:, k, :], w2_p["lo"][:, k, :], k == 0, False)
                    a, z = row_at["b2"]
                    nc.tensor.matmul(bank[4 + t % 2][:, 0:D], ones_pair[:], row_pair[:, a:z], start=False, stop=True)\
                        .then_inc(dn_ready, 1)

            def shared_up(n):
                (w_hi, _), (w_lo, _) = expert("shared", "hi"), expert("shared", "lo")
                v, m = n // M1, n % M1
                for w in range(2):
                    if n >= 2:
                        if w == 0:
                            pe.wait_ge(act_done, NB * M0 + n - 1)
                        else:
                            pe.wait_ge(h_done, n - 1)
                    for k in range(KD):
                        mm = three(bank[2 * w + n % 2][:], w_hi[:, w, k, m * P:(m + 1) * P],
                                   w_lo[:, w, k, m * P:(m + 1) * P], xnt_hi[:, k, v * BLK:(v + 1) * BLK],
                                   xnt_lo[:, k, v * BLK:(v + 1) * BLK], k == 0, k == KD - 1)
                    mm.then_inc(up_ready, 1)

            def shared_down(v, tiles):
                (_, w_hi), (_, w_lo) = expert("shared", "hi"), expert("shared", "lo")
                for j in tiles:
                    t = TPB * v + j
                    pe.wait_ge(y_done, NT + t - 1)
                    for k in range(M1):
                        if j == 0:
                            pe.wait_ge(*parts_of(M1 * v + k))
                        at = v % 2 * M1 + k
                        mm = three(bank[4 + t % 2][:, 0:D], ht_hi[at][:, j * P:(j + 1) * P],
                                   ht_lo[at][:, j * P:(j + 1) * P], w_hi[:, k, :], w_lo[:, k, :],
                                   k == 0, k == M1 - 1)
                    mm.then_inc(dn_ready, 1)

            def shared_ahead(m):
                if m == 0:
                    pe.wait_ge(split_done, 4)
                    pe.wait_ge(sub_done, 2 * NU)
                    for b in (2, 3):
                        pe.wait_ge(*reader[b])
                shared_up(m)
                early_logits(1, m)

            pe.wait_ge(y_done, NT)
            attention(1, shared_ahead)
            for c in range(KD):
                x_transposed(1, "ffn", NB - 1, c)
            logits(1, range(EARLY // 2, NT))
            shared_down(0, range(0, 2))
            pe.wait_ge(rank_ready, 1)
            pe.wait_ge(consts, 6)
            picked = chosen[:, 2].rearrange("p t e -> p (t e)")
            nc.tensor.matmul(bank[7][:, 0:NT * E], before[:], picked, start=True, stop=True)
            nc.tensor.matmul(bank[7][:, NT * E:2 * NT * E], all_ones[:], picked, start=True, stop=True)\
                .then_inc(routed_pe, 1)
            shared_up(M1)
            shared_up(M1 + 1)
            shared_down(0, range(2, TPB))
            for v in range(1, NB - 1):
                for m in range(2 if v == 1 else 0, M1):
                    shared_up(M1 * v + m)
                shared_down(v, range(TPB))

            def rows_transposed(s):
                pe.wait_ge(rows_in[s % 2], 16 * (s // 2 + 1))
                if s >= 2:
                    pe.wait_ge(st_lo, s - 1)
                for k in range(KD):
                    for a in range(KS):
                        mm = nc.tensor.transpose(bank[6 + s % 2][:, (k * KS + a) * P:(k * KS + a + 1) * P],
                                                 xs[:, s % 2, a, k * P:(k + 1) * P], ident[:])
                mm.then_inc(st_ready, 1)

            def slot_up(s):
                (w_hi, _), (w_lo, _) = expert(s % 2, "hi"), expert(s % 2, "lo")
                pe.wait_ge(in_lo, s + 1)
                pe.wait_ge(st_lo, s + 1)
                for pair in range(2):
                    n = 2 * s + pair
                    for w in range(2):
                        if n >= 2:
                            if w == 0:
                                pe.wait_ge(s_silu, n - 1)
                            else:
                                pe.wait_ge(s_h, n - 1)
                        for c in range(2):
                            m = 2 * pair + c
                            for k in range(KD):
                                mm = three(bank[2 * w + pair][:, c * R:(c + 1) * R],
                                           w_hi[:, w, k, m * P:(m + 1) * P], w_lo[:, w, k, m * P:(m + 1) * P],
                                           xst_hi[:, s % 2, k, :], xst_lo[:, s % 2, k, :], k == 0, k == KD - 1)
                        mm.then_inc(sg_ready if w == 0 else su_ready, 1)

            def slot_down(s):
                (_, w_hi), (_, w_lo) = expert(s % 2, "hi"), expert(s % 2, "lo")
                pe.wait_ge(dn_lo, s + 1)
                if s >= 2:
                    pe.wait_ge(sy_done, s - 1)
                for a in range(KS):
                    for k in range(M1):
                        if a == 0 and k % 2 == 0:
                            pe.wait_ge(s_hlo, 2 * s + k // 2 + 1)
                        at, o = 2 * (s % 2) + k // 2, k % 2 * R + a * P
                        mm = three(bank[4 + s % 2][:, a * D:(a + 1) * D], ht_hi[at][:, o:o + P], ht_lo[at][:, o:o + P],
                                   w_hi[:, k, :], w_lo[:, k, :], k == 0, k == M1 - 1)
                mm.then_inc(sd_ready, 1)

            for m in range(M1):
                shared_up(M1 * (NB - 1) + m)
                if m >= M1 - 2:
                    rows_transposed(m - M1 + 2)
            pe.wait_ge(act_done, NB * M0 + M1 * NB)
            pe.wait_ge(h_done, M1 * NB)
            pe.wait_ge(y_done, NT + TPB * (NB - 1))
            for s in range(NSLOT):
                slot_up(s)
                if 1 <= s < NSLOT - 1:
                    rows_transposed(s + 1)
                if s >= 1:
                    slot_down(s - 1)
            slot_down(NSLOT - 1)

            pe.wait_ge(sy_done, NSLOT)
            shared_down(NB - 1, range(TPB))

        @block.scalar
        def _(act):
            def bias_keys(layer):
                kf, _, _ = key_parts(layer)
                src = bank[4] if layer == 0 else bank[7]
                act.wait_ge(k_ready, layer + 1)
                for m in range(G):
                    c = col_at[f"bk{layer}"][0] + m
                    nc.scalar.activation(kf[:, m, :], src[:, m * B * SC:(m + 1) * B * SC], ACT.Identity,
                                         bias=colp[:, c:c + 1]).then_inc(k_biased, 1)

            def norm_std(layer, group):
                a, z = norm_tiles(layer, group)
                act.wait_ge(var_done, NORM_GROUPS * layer + group + 1)
                nc.scalar.activation(std[:, a:z], std[:, a:z], ACT.Sqrt).then_inc(std_done, 1)

            def normalise(layer, what, i, j, group):
                t, at = TPB * i + j, turn(layer, what, i)
                act.wait_ge(xm_done, NORM_GROUPS * layer + group + 1)
                if at >= 1:
                    act.wait_ge(xt_ready, KD * at)
                nc.scalar.activation(xn[:, j, :], x_res[:, t, :], ACT.Identity, bias=xm[:, t:t + 1],
                                     scale=rstd[:, t:t + 1]).then_inc(xn_ready, 1)

            def xt_high(layer, what, i, c):
                act.wait_ge(xt_ready, KD * turn(layer, what, i) + c + 1)
                nc.scalar.copy(xnt_hi[:, c, i * BLK:(i + 1) * BLK], bank[work_bank["x", layer, what, i, c]])\
                    .then_inc(xt_hi, 1)

            a, z = ev_at["gates"]
            act.wait_ge(small_in, 64)
            nc.scalar.activation(gate_t[:], ev[:, a:z], ACT.Tanh).then_inc(gates_done, 1)
            norm_std(0, 0)
            for j in range(TPB):
                normalise(0, "queries", 0, j, 0)
            bias_keys(0)
            act.wait_ge(qo_in, 32)
            nc.scalar.copy(wq[0, "hi"][:, 0::3], raw_pieces(0)[:, 0::3]).then_inc(qo_hi, 1)

            def q_high(layer, i, m):
                n = 2 * (NB * layer + i) + m
                act.wait_ge(q_ready, n + 1)
                if i >= 1:
                    act.wait_ge(s_ready, NU * layer + UPB * i - 1 + m)
                c = col_at[f"bq{layer}"][0] + m
                nc.scalar.activation(qt_hi[:, m, :], bank[work_bank["q", layer, i, m]], ACT.Identity, bias=colp[:, c:c + 1])\
                    .then_inc(q_hi, 1)

            def extras_high(layer, n):
                for kind, *what in extras(layer, n):
                    (xt_high if kind == "x" else q_high)(*what)

            def attention(layer, ahead):
                for n in range(NU + 4):
                    i, u, gn = n // UPB, n % UPB, NU * layer + n
                    if 1 <= n <= NU:
                        for q in range(2):
                            act.wait_ge(pt_ready, 2 * (gn - 1) + q + 1)
                            if gn - 1 >= 2:
                                act.wait_ge(pv_ready, gn - 2)
                            if by_pool(gn - 1, q):
                                if gn - 1 > UPB:
                                    act.wait_ge(*low_parts_of(gn - 2, q))
                                nc.scalar.copy(pt_copy[:], bank[4 + q][0:SC, :])
                            nc.scalar.copy(pt_hi[:, (n - 1) % 2, q].rearrange("p h c -> p (h c)"),
                                           bank[4 + q][0:SC, :]).then_inc(pt_hi_done, 1)
                    extras_high(layer, n)
                    if n < NU:
                        act.wait_ge(sub_done, gn + 1)
                        nc.scalar.activation(prob[:, n % 2], prob[:, n % 2], ACT.Exp, scale=SCALE)\
                            .then_inc(exp_done, 1)
                    if n % 2 == 0 and 4 <= n < NU + 4:
                        t = (n - 4) // 2
                        gt = NT * layer + t
                        act.wait_ge(ot_ready, gt + 1)
                        if gt >= 2:
                            act.wait_ge(op_ready, gt - 1)
                        nc.scalar.copy(ot_hi[:, t % 2].rearrange("p k c -> p (k c)"), bank[work_bank["o", layer, t]][:, 0:D])\
                            .then_inc(ot_hi_done, 1)
                    if u in (3, 4) and i + 1 < NB:
                        for j in range(2):
                            normalise(layer, "queries", i + 1, 2 * (u - 3) + j, 1)
                    if u in (6, 7) and 1 <= i < NB:
                        for j in range(2):
                            normalise(layer, "ffn", i - 1, 2 * (u - 6) + j, 1 + i)
                    if n == 2:
                        norm_std(layer, 1)
                    if u == 5 and 1 <= i < NB:
                        norm_std(layer, 1 + i)
                    if n in (NU + 1, NU + 2):
                        ahead(n - NU - 1)
                norm_std(layer, 1 + NB)
                for j in range(TPB):
                    normalise(layer, "ffn", NB - 1, j, 1 + NB)

            def gelu(n):
                m = n % M0
                if n == 0:
                    act.wait_ge(zeroed, 16 * FILLS)
                act.wait_ge(up_ready, n + 1)
                if n >= 2:
                    act.wait_ge(lo_done, n - 1)
                c = col_at["b1"][0] + m
                nc.scalar.activation(hf[:, n % 2, :], bank[n % 4][:], ACT.Gelu_apprx_tanh, bias=colp[:, c:c + 1])\
                    .then_inc(act_done, 1)

            def silu(n):
                act.wait_ge(up_ready, NB * M0 + 2 * n + 1)
                if n >= 2:
                    act.wait_ge(*parts_of(n - 2))
                nc.scalar.activation(hf[:, n % 2, :], bank[n % 2][:], ACT.Silu).then_inc(act_done, 1)

            def pooled_high(n):
                act.wait_ge(h_done, n + 1)
                nc.scalar.copy(ht_hi[n], hf[:, n % 2, :]).then_inc(p_hi, 1)

            def pooled(n):
                silu(n)
                if n >= 1:
                    pooled_high(n - 1)

            for c in range(KD):
                xt_high(0, "queries", 0, c)
            for m in range(G):
                q_high(0, 0, m)
            attention(0, gelu)
            for n in range(2, NB * M0):
                if n == M0:
                    act.wait_ge(r_chain, 2)
                    nc.scalar.activation(rt[1][:], rt[0][:], ACT.Exp).then_inc(r_act, 1)
                if n == (KV_AFTER + 1) * M0:
                    bias_keys(1)
                gelu(n)
                if n in (5, 6):
                    xt_high(0, "ffn", NB - 1, n - 5)
                if n == (NB - 1) * M0:
                    norm_std(1, 0)
                if n == (NB - 1) * M0 + 2:
                    act.wait_ge(kb_first, 2 * G)
                    act.wait_ge(kb_second, 2 * G)
                    for j in range(TPB):
                        normalise(1, "queries", 0, j, 0)
            for c in range(KD):
                xt_high(1, "queries", 0, c)
            for m in range(G):
                q_high(1, 0, m)
            attention(1, pooled)
            for c in range(KD):
                xt_high(1, "ffn", NB - 1, c)
            for n in range(2, AHEAD):
                pooled(n)
            pooled_high(AHEAD - 1)
            for t in range(NT):
                nc.scalar.activation(xn_all[:, t, 0:D], x_res[:, t, :], ACT.Identity, bias=xm[:, t:t + 1],
                                     scale=rstd[:, t:t + 1]).then_inc(xn_all_ready, 1)
            act.wait_ge(lg_copied, 4)
            nc.scalar.activation(rt[2][:], lg[:], ACT.Sigmoid).then_inc(r_act, 1)

            def in_high(s):
                act.wait_ge(win_in[s % 2], 16 * (s // 2 + 1))
                if s >= 2:
                    act.wait_ge(su_ready, 2 * (s - 1))
                (hi, _) = expert(s % 2, "hi")
                nc.scalar.copy(hi, raw[s % 2][:, 0:WI].rearrange("p (w k n) -> p w k n", w=2, k=KD)).then_inc(in_hi, 1)

            def down_high(s):
                act.wait_ge(wdn_in[s % 2], 16 * (s // 2 + 1))
                if s >= 2:
                    act.wait_ge(sd_ready, s - 1)
                (_, hi) = expert(s % 2, "hi")
                nc.scalar.copy(hi, raw[s % 2][:, WI:WE].rearrange("p (k n) -> p k n", k=M1)).then_inc(dn_hi, 1)

            def rows_high(s):
                act.wait_ge(st_ready, s + 1)
                if s >= 2:
                    act.wait_ge(su_ready, 2 * (s - 1))
                nc.scalar.copy(xst_hi[:, s % 2].rearrange("p k r -> p (k r)"), bank[6 + s % 2][:]).then_inc(st_hi, 1)

            def slot_silu(s):
                for n in (2 * s, 2 * s + 1):
                    act.wait_ge(sg_ready, n + 1)
                    if n >= 2:
                        act.wait_ge(s_hlo, n - 1)
                    nc.scalar.activation(hf[:, n % 2, :], bank[n % 2][:], ACT.Silu).then_inc(s_silu, 1)

            def slot_out(s):
                act.wait_ge(sd_ready, s + 1)
                if s >= 2:
                    act.wait_ge(y_stored[s % 2], 16 * KS * (s // 2))
                nc.scalar.copy(y_out[:, s % 2].rearrange("p a d -> p (a d)"), bank[4 + s % 2][:]).then_inc(sy_done, 1)

            for n in range(AHEAD, M1 * NB):
                if n == M1 * (NB - 1):
                    in_high(0)
                silu(n)
                if n >= M1 * NB - 2:
                    rows_high(n - M1 * NB + 2)
            act.wait_ge(*parts_of(M1 * NB - 1))
            for s in range(NSLOT):
                if s + 1 < NSLOT:
                    in_high(s + 1)
                down_high(s)
                slot_silu(s)
                if 1 <= s < NSLOT - 1:
                    rows_high(s + 1)
                if s >= 1:
                    slot_out(s - 1)
            slot_out(NSLOT - 1)
            for t in range(0, NT, 2):
                act.wait_ge(gathered[t % RING], 16 * (t // RING + 1))
                for c in range(2):
                    nc.scalar.activation(y_back[:, t % RING, c, :], y_back[:, t % RING, c, :], ACT.Identity,
                                         scale=weight[:, c, t:t + 1]).then_inc(weighted, 1)

        @block.vector
        def _(dve):
            v = nc.vector

            v.memset(vals[:], 0.0).then_inc(vals_cleared, 1)
            dve.wait_ge(vals_cleared, 1)
            v.memset(vals[:, :, 0, :, HD:VW], 1.0).then_inc(v_chain, 1)
            v.memset(ones_pair[:].bitcast(F32), 1.0)
            dve.wait_ge(small_in, 64)
            v.tensor_copy(ct_hi[:], ct_raw[:]).then_inc(v_chain, 1)
            dve.wait_ge(kvw_in, 16)
            src = raw_pieces(0)[:, 1:3]
            v.tensor_copy(wq[0, "hi"][:, 1:3], src).then_inc(v_chain, 1)
            dve.wait_ge(v_chain, 3)
            v.tensor_tensor(ct_lo[:], ct_raw[:], ct_hi[:].bitcast(F32), ALU.subtract)
            v.tensor_tensor(wq[0, "lo"][:, 1:3], src, wq[0, "hi"][:, 1:3].bitcast(F32), ALU.subtract)\
                .then_inc(kv_split, 1)

            def tile_stats(phase, t):
                n = NT * phase + t
                v.bn_stats(stats[:, t % 2, :], x_res[:, t, :]).then_inc(stats_done, 1)
                dve.wait_ge(stats_done, n + 1)
                v.bn_aggr(mv[:, t, :], stats[:, t % 2, :]).then_inc(aggr_done, 1)

            def variance(layer, group):
                a, z = norm_tiles(layer, group)
                dve.wait_ge(aggr_done, NT * (2 * layer + (group >= 2)) + z)
                v.tensor_scalar(std[:, a:z], mv[:, a:z, 1], EPS, None, ALU.add).then_inc(var_done, 1)

            def inverse_std(layer, group):
                a, z = norm_tiles(layer, group)
                n = NORM_GROUPS * layer + group + 1
                dve.wait_ge(std_done, n)
                v.reciprocal(rstd[:, a:z], std[:, a:z]).then_inc(rstd_done, 1)
                dve.wait_ge(rstd_done, n)
                v.scalar_tensor_tensor(out=xm[:, a:z], in0=mv[:, a:z, 0], scalar=-1.0, in1=rstd[:, a:z],
                                       op0=ALU.mult, op1=ALU.mult).then_inc(xm_done, 1)

            def xt_low(layer, what, i, c):
                dve.wait_ge(xt_hi, KD * turn(layer, what, i) + c + 1)
                v.tensor_tensor(xnt_lo[:, c, i * BLK:(i + 1) * BLK], bank[work_bank["x", layer, what, i, c]],
                                xnt_hi[:, c, i * BLK:(i + 1) * BLK].bitcast(F32), ALU.subtract).then_inc(xt_lo, 1)

            def q_low(layer, i, m):
                c = col_at[f"bq{layer}"][0] + m
                dve.wait_ge(q_hi, 2 * (NB * layer + i) + m + 1)
                v.scalar_tensor_tensor(out=qt_lo[:, m, :], in0=bank[work_bank["q", layer, i, m]], scalar=colp[:, c:c + 1],
                                       in1=qt_hi[:, m, :].bitcast(F32), op0=ALU.add, op1=ALU.subtract)\
                    .then_inc(q_lo, 1)

            def extras_low(layer, n):
                for kind, *what in extras(layer, n):
                    (xt_low if kind == "x" else q_low)(*what)

            def keys(layer, between=lambda: None):
                kf, kx_hi, kx_lo = key_parts(layer)
                dve.wait_ge(k_biased, 2 * layer + 2)
                v.tensor_copy(kx_hi.bitcast(F32R), kf).then_inc(kx_done, 1)
                dve.wait_ge(kx_done, 2 * layer + 1)
                v.tensor_tensor(kx_lo.bitcast(F32R), kf, kx_hi, ALU.subtract).then_inc(kx_done, 1)
                between()
                dve.wait_ge(kx_done, 2 * layer + 2)
                dve.wait_ge(consts, 2)
                spread_keys(v, layer, 0, kb_first)
                between()

            def split_values(layer, between=lambda: None):
                ps = bank[6][0:SC, :]
                dve.wait_ge(v_ready, layer + 1)
                heads = "p (b h d) -> p b h d"
                psv = ps.rearrange(heads, b=B, h=H)
                rest = pt_copy[:].rearrange(heads, b=B, h=H)
                n = 4 * layer
                v.tensor_copy(vals[:, :, 0, :, 0:HD], psv).then_inc(vals_chain, 1)
                dve.wait_ge(vals_chain, n + 1)
                v.tensor_tensor(rest, psv, vals[:, :, 0, :, 0:HD], ALU.subtract).then_inc(vals_chain, 1)
                between()
                dve.wait_ge(vals_chain, n + 2)
                v.tensor_copy(vals[:, :, 1, :, 0:HD], rest).then_inc(vals_chain, 1)
                dve.wait_ge(vals_chain, n + 3)
                v.tensor_tensor(rest, rest, vals[:, :, 1, :, 0:HD], ALU.subtract).then_inc(vals_chain, 1)
                between()
                dve.wait_ge(vals_chain, n + 4)
                v.tensor_copy(vals[:, :, 2, :, 0:HD], rest).then_inc(v_done, 1)
                between()

            def attention(layer, ahead):
                for n in range(NU + 4):
                    i, u, gn = n // UPB, n % UPB, NU * layer + n
                    if n == 3:
                        inverse_std(layer, 1)
                    if u == 6 and 1 <= i < NB:
                        inverse_std(layer, 1 + i)
                    if n < NU:
                        dve.wait_ge(s_ready, gn + 1)
                        s = psum[:, 0:2, 0:SH].rearrange("p w (h c) -> p w h c", c=SC)
                        m = smax[:, n % 2].rearrange("p (w h) -> p w h", w=2)
                        v.tensor_reduce(m, s, AX.X, ALU.max).then_inc(max_done, 1)
                        dve.wait_ge(max_done, gn + 1)
                        if gn >= 2:
                            dve.wait_ge(pt_ready, 2 * (gn - 1))
                        ins = v.tensor_tensor(prob[:, n % 2].rearrange("p (w h) c -> p w h c", w=2), s,
                                              m.unsqueeze(3).to_broadcast([P, 2, HG // 2, SC]), ALU.subtract)
                        ins.then_inc(sub_done, 1)
                    if 1 <= n <= NU:
                        for q in range(2):
                            if by_pool(gn - 1, q):
                                continue
                            dve.wait_ge(pt_hi_done, 2 * (gn - 1) + q + 1)
                            v.tensor_tensor(pt_lo[:, (n - 1) % 2, q].rearrange("p h c -> p (h c)"),
                                            bank[4 + q][0:SC, :],
                                            pt_hi[:, (n - 1) % 2, q].rearrange("p h c -> p (h c)"),
                                            ALU.subtract).then_inc(pt_lo_done, 1)
                    extras_low(layer, n)
                    if n % 2 == 1 and 3 <= n < NU + 3:
                        t = (n - 3) // 2
                        gt = NT * layer + t
                        o = bank[6][:, 0:H * VW].rearrange("p (h d) -> p h d", h=H)
                        dve.wait_ge(pv_ready, 2 * gt + 2)
                        v.reciprocal(rsum[:, t % 2, :], o[:, :, HD]).then_inc(rsum_done, 1)
                        dve.wait_ge(rsum_done, gt + 1)
                        if gt >= 2:
                            dve.wait_ge(ot_ready, gt - 1)
                        v.tensor_tensor(o_n[:, t % 2], o[:, :, 0:HD],
                                        rsum[:, t % 2, :].unsqueeze(2).to_broadcast([P, H, HD]), ALU.mult)\
                            .then_inc(o_done, 1)
                    if n % 2 == 0 and 4 <= n < NU + 4:
                        t = (n - 4) // 2
                        gt = NT * layer + t
                        dve.wait_ge(ot_hi_done, gt + 1)
                        v.tensor_tensor(ot_lo[:, t % 2].rearrange("p k c -> p (k c)"), bank[work_bank["o", layer, t]][:, 0:D],
                                        ot_hi[:, t % 2].rearrange("p k c -> p (k c)").bitcast(F32),
                                        ALU.subtract).then_inc(ot_lo_done, 1)
                    if n % 2 == 1 and 5 <= n:
                        t = (n - 5) // 2
                        gt = NT * layer + t
                        dve.wait_ge(op_ready, gt + 1)
                        v.scalar_tensor_tensor(out=x_res[:, t, :], in0=bank[work_bank["y", layer, t]][:, 0:D],
                                               scalar=gate_t[:, layer:layer + 1], in1=x_res[:, t, :],
                                               op0=ALU.mult, op1=ALU.add).then_inc(x_new, 1)
                        dve.wait_ge(x_new, gt + 1)
                        tile_stats(2 * layer + 1, t)
                    if layer == 0 and n < NB - 1:
                        for t in range(TPB * (n + 1), TPB * (n + 2)):
                            dve.wait_ge(x_in[t // TPB], 16)
                            tile_stats(0, t)
                    if n == 2:
                        variance(layer, 1)
                    if u == 4 and 1 <= i <= NB - 1:
                        variance(layer, 1 + i)
                    if n == NU + 2:
                        ahead(0)
                variance(layer, 1 + NB)
                ahead(1)
                inverse_std(layer, 1 + NB)

            def copy_logits(layer):
                dve.wait_ge(lg_ready, layer + 1)
                for part in range(2):
                    for a, z in ((0, EARLY), (EARLY, NT)):
                        both = bank[6][:, logits_at(a).start:logits_at(z - 1).stop]
                        one = both.rearrange("p (t w e) -> p t w e", w=2, e=E)[:, :, 1 - part, :]
                        if part == 0:
                            ins = v.tensor_copy(lg[:, a:z, :], one)
                        else:
                            ins = v.tensor_tensor(lg[:, a:z, :], lg[:, a:z, :], one, ALU.add)
                    ins.then_inc(lg_copied, 1)
                    dve.wait_ge(lg_copied, 2 * layer + 1 + part)

            chain = [0]

            def link(ins):
                chain[0] += 1
                ins.then_inc(r_chain, 1)
                dve.wait_ge(r_chain, chain[0])

            dve.wait_ge(x_in[0], 16)
            for t in range(TPB):
                tile_stats(0, t)
            variance(0, 0)
            inverse_std(0, 0)
            v.tensor_copy(row_hi[:], row_raw[:]).then_inc(v_chain, 1)
            a = col_at["wr0"][0]
            wr_raw = colp[:, a:a + 2 * KD * E].rearrange("p (w k e) -> p w k e", w=2, k=KD)
            v.tensor_copy(wr_pair[:, :, :, 0:E], wr_raw).then_inc(v_chain, 1)
            dve.wait_ge(v_chain, 5)
            dve.wait_ge(low_row_done, 1)
            v.scalar_tensor_tensor(out=row_pair[:], in0=row_hi[:].bitcast(F32), scalar=low_row[:], in1=row_raw[:],
                                   op0=ALU.mult, op1=ALU.add)
            v.tensor_tensor(wr_pair[:, :, :, E:2 * E], wr_raw, wr_pair[:, :, :, 0:E].bitcast(F32), ALU.subtract)\
                .then_inc(setup_dve, 1)
            keys(0)
            for c in range(KD):
                xt_low(0, "queries", 0, c)
            split_values(0)
            for m in range(G):
                q_low(0, 0, m)
            dve.wait_ge(kb_second, G)
            dve.wait_ge(gates_done, 1)

            def split(n):
                m = n % M0
                dve.wait_ge(act_done, n + 1)
                v.tensor_copy(ht_hi[m], hf[:, n % 2, :]).then_inc(hi_done, 1)
                dve.wait_ge(hi_done, n + 1)
                v.tensor_tensor(ht_lo[m], hf[:, n % 2, :], ht_hi[m].bitcast(F32), ALU.subtract).then_inc(lo_done, 1)

            attention(0, split)
            for m in range(2, M0):
                split(m)
                if m in (5, 6):
                    xt_low(0, "ffn", NB - 1, m - 5)
            copy_logits(0)

            def over_e(a):
                return a.unsqueeze(2).to_broadcast([P, NT, E])
            link(v.tensor_reduce(rs[0][:], lg[:], AX.X, ALU.max))
            link(v.tensor_tensor(rt[0][:], lg[:], over_e(rs[0][:]), ALU.subtract))
            dve.wait_ge(r_act, 1)
            link(v.tensor_reduce(rs[0][:], rt[1][:], AX.X, ALU.add))
            link(v.reciprocal(rs[1][:], rs[0][:]))
            link(v.tensor_tensor(rt[0][:], rt[1][:], over_e(rs[1][:]), ALU.mult))
            for t in range(NT):
                ins = v.max(rt[2][:, t, :], rt[0][:, t, :])
            link(ins)
            link(v.tensor_tensor(rs[0][:], rt[2][:, :, 0], rt[2][:, :, 1], ALU.add))
            link(v.reciprocal(rs[1][:], rs[0][:]))
            link(v.tensor_tensor(rs[2][:], rt[2][:, :, 0], rs[1][:], ALU.mult))
            link(v.tensor_tensor(rs[3][:], rt[2][:, :, 1], rs[1][:], ALU.mult))
            link(v.tensor_tensor(rs[0][:], rs[2][:], rs[3][:], ALU.add))
            link(v.tensor_scalar(rs[1][:], rs[0][:], gate_t[:, 2:3], None, ALU.mult))

            done = []
            for i in range(NB):
                if i >= 1:
                    for m in range(M0):
                        if M0 * i + m in done:
                            continue
                        split(M0 * i + m)
                        if i == NB - 1 and m == 1:
                            inverse_std(1, 0)
                for j in range(TPB):
                    t = TPB * i + j
                    if i == NB - 1:
                        if j < KD:
                            xt_low(1, "queries", 0, j)
                        else:
                            q_low(1, 0, j - KD)
                    dve.wait_ge(dn_ready, t + 1)
                    v.scalar_tensor_tensor(out=x_res[:, t, :], in0=bank[4 + t % 2][:, 0:D], scalar=rs[1][:, t:t + 1],
                                           in1=x_res[:, t, :], op0=ALU.mult, op1=ALU.add).then_inc(y_done, 1)
                    dve.wait_ge(y_done, t + 1)
                    tile_stats(2, t)
                if i == KV_AFTER:
                    todo = [M0 * (i + 1) + m for m in range(M0)]

                    def next_split():
                        if todo:
                            done.append(todo.pop(0))
                            split(done[-1])

                    keys(1, next_split)
                    split_values(1, next_split)
                if i == NB - 2:
                    variance(1, 0)

            def product(n):
                dve.wait_ge(act_done, NB * M0 + n + 1)
                dve.wait_ge(up_ready, NB * M0 + 2 * n + 2)
                v.tensor_tensor(hf[:, n % 2, :], hf[:, n % 2, :], bank[2 + n % 2][:], ALU.mult).then_inc(h_done, 1)

            attention(1, product)
            for c in range(KD):
                xt_low(1, "ffn", NB - 1, c)
            for n in range(2, AHEAD):
                product(n)
            copy_logits(1)

            dve.wait_ge(split_done, 4)
            sel = rt[0][:]
            a, z = ev_at["beta"]
            link(v.tensor_tensor(sel, lg[:], ev[:, a:z].unsqueeze(1).to_broadcast([P, NT, E]), ALU.add))
            mine = sel.unsqueeze(3).to_broadcast([P, NT, E, E])
            other = sel.unsqueeze(2).to_broadcast([P, NT, E, E])
            link(v.tensor_tensor(cmp[:], other, mine, ALU.is_gt))
            link(v.tensor_tensor(rank[:], other, mine, ALU.is_equal))
            for j in range(E):
                ins = v.memset(rank[:, :, j, j:E], 0.0)
            link(ins)
            link(v.tensor_tensor(rank[:], rank[:], cmp[:], ALU.add))
            link(v.tensor_reduce(rt[1][:], rank[:], AX.X, ALU.add))
            link(v.tensor_scalar(chosen[:, 0], rt[1][:], 0.5, None, ALU.is_lt))
            v.tensor_scalar(chosen[:, 2], rt[1][:], 1.5, None, ALU.is_lt).then_inc(rank_ready, 1)
            dve.wait_ge(rank_ready, 1)
            link(v.tensor_tensor(chosen[:, 1], chosen[:, 2], chosen[:, 0], ALU.subtract))

            def add_shared(t):
                dve.wait_ge(dn_ready, NT + t + 1)
                if t == 0:
                    dve.wait_ge(xn_all_ready, NT)
                v.scalar_tensor_tensor(out=x_res[:, t, :], in0=bank[4 + t % 2][:, 0:D], scalar=gate_t[:, 3:4],
                                       in1=x_res[:, t, :], op0=ALU.mult, op1=ALU.add).then_inc(y_done, 1)

            dve.wait_ge(routed_pe, 1)
            in_tile = bank[7][:, 0:NT * E].rearrange("p (t e) -> p t e", e=E)
            tile_total = bank[7][:, NT * E:2 * NT * E].rearrange("p (t e) -> p t e", e=E)
            link(v.tensor_copy(cum[0][:], tile_total))
            a, step = 0, 1
            while step < NT:
                link(v.tensor_copy(cum[1 - a][:, 0:step, :], cum[a][:, 0:step, :]))
                link(v.tensor_tensor(cum[1 - a][:, step:NT, :], cum[a][:, step:NT, :], cum[a][:, 0:NT - step, :], ALU.add))
                a, step = 1 - a, 2 * step
            count = cum[a][:, NT - 1, :]
            link(v.tensor_tensor(filled[:], count.unsqueeze(2).to_broadcast([P, E, MAX_PER_EXPERT]), slot_limit[:],
                                 ALU.is_gt))
            link(v.tensor_reduce(es[0][:], filled[:], AX.X, ALU.add))
            link(v.tensor_copy(es[1][:], es[0][:]))
            b, step = 1, 1
            while step < E:
                link(v.tensor_copy(es[3 - b][:, 0:step], es[b][:, 0:step]))
                link(v.tensor_tensor(es[3 - b][:, step:E], es[b][:, step:E], es[b][:, 0:E - step], ALU.add))
                b, step = 3 - b, 2 * step
            link(v.tensor_tensor(es[3][:], es[b][:], es[0][:], ALU.subtract))
            link(v.tensor_scalar(es[3][:], es[3][:], float(R), None, ALU.mult))
            link(v.tensor_tensor(cum[1 - a][:], cum[a][:], tile_total, ALU.subtract))
            link(v.tensor_tensor(cum[a][:], cum[1 - a][:], in_tile, ALU.add))
            link(v.tensor_tensor(cum[1 - a][:], cum[a][:], es[3][:].unsqueeze(1).to_broadcast([P, NT, E]), ALU.add))
            for c in range(2):
                link(v.tensor_tensor(rt[c][:], chosen[:, c], cum[1 - a][:], ALU.mult))
                link(v.tensor_reduce(dest_f[:, c, :], rt[c][:], AX.X, ALU.add))
            link(v.tensor_copy(dest[:], dest_f[:]))
            link(v.tensor_tensor(slot_cmp[:], es[b][0:1, :].unsqueeze(1).to_broadcast([1, NSLOT, E]), slot_id[:],
                                 ALU.is_le))
            link(v.tensor_reduce(slot_e[:], slot_cmp[:], AX.X, ALU.add))
            link(v.tensor_scalar(slot_e[:], slot_e[:], float(E - 1), None, ALU.min))
            v.tensor_copy(slot_expert[:], slot_e[:]).then_inc(route_done, 1)
            add_shared(0)
            add_shared(1)
            dve.wait_ge(r_act, 2)
            for c in range(2):
                link(v.tensor_tensor(rt[0][:], chosen[:, c], rt[2][:], ALU.mult))
                link(v.tensor_reduce(rs[c][:], rt[0][:], AX.X, ALU.add))
                v.tensor_scalar(weight[:, c, :], rs[c][:], gate_t[:, 3:4], None, ALU.mult).then_inc(weights_done, 1)
                dve.wait_ge(weights_done, c + 1)

            def shared_chunk(n):
                at, k = n % M0, n - AHEAD
                product(n)
                dve.wait_ge(h_done, n + 1)
                v.tensor_copy(ht_hi[at], hf[:, n % 2, :]).then_inc(hi_done, 1)
                dve.wait_ge(hi_done, NB * M0 + k + 1)
                v.tensor_tensor(ht_lo[at], hf[:, n % 2, :], ht_hi[at].bitcast(F32), ALU.subtract).then_inc(lo_done, 1)

            for u in range(1, NB - 1):
                for m in range(M1):
                    shared_chunk(M1 * u + m)
                    if u == 1 and m == 1:
                        add_shared(2)
                        add_shared(3)
                for j in range(TPB):
                    add_shared(TPB * u + j)

            def rows_low(s):
                dve.wait_ge(st_hi, s + 1)
                v.tensor_tensor(xst_lo[:, s % 2].rearrange("p k r -> p (k r)"), bank[6 + s % 2][:],
                                xst_hi[:, s % 2].rearrange("p k r -> p (k r)").bitcast(F32), ALU.subtract)\
                    .then_inc(st_lo, 1)

            def down_low(s):
                dve.wait_ge(dn_hi, s + 1)
                (_, hi), (_, lo) = expert(s % 2, "hi"), expert(s % 2, "lo")
                v.tensor_tensor(lo, raw[s % 2][:, WI:WE].rearrange("p (k n) -> p k n", k=M1), hi.bitcast(F32),
                                ALU.subtract).then_inc(dn_lo, 1)

            def slot_pair(s, pair):
                n, at = 2 * s + pair, 2 * (s % 2) + pair
                dve.wait_ge(s_silu, n + 1)
                dve.wait_ge(su_ready, n + 1)
                v.tensor_tensor(hf[:, n % 2, :], hf[:, n % 2, :], bank[2 + pair][:], ALU.mult).then_inc(s_h, 1)
                dve.wait_ge(s_h, n + 1)
                v.tensor_copy(ht_hi[at], hf[:, n % 2, :]).then_inc(s_hhi, 1)
                dve.wait_ge(s_hhi, n + 1)
                v.tensor_tensor(ht_lo[at], hf[:, n % 2, :], ht_hi[at].bitcast(F32), ALU.subtract)\
                    .then_inc(s_hlo, 1)

            for m in range(M1):
                shared_chunk(M1 * (NB - 1) + m)
                if m >= M1 - 2:
                    rows_low(m - M1 + 2)
            for s in range(NSLOT):
                down_low(s)
                slot_pair(s, 0)
                slot_pair(s, 1)
                if 1 <= s < NSLOT - 1:
                    rows_low(s + 1)

            def combine(t):
                dve.wait_ge(y_done, NT + t + 1)
                dve.wait_ge(gathered[t % RING], 16 * (t // RING + 1))
                for c in range(2):
                    if c == 1:
                        dve.wait_ge(odd_combined, t)
                    v.scalar_tensor_tensor(out=x_res[:, t, :], in0=y_back[:, t % RING, c, :],
                                           scalar=weight[:, c, t:t + 1], in1=x_res[:, t, :],
                                           op0=ALU.mult, op1=ALU.add).then_inc(odd_combined, 1)

            for j in range(TPB):
                add_shared(TPB * (NB - 1) + j)
            for t in range(1, NT, 2):
                combine(t)


def kernel(**inputs):
    import numpy as np
    import concourse.bacc as bacc
    from concourse.bass_utils import run_bass_kernel_spmd

    i = {k: np.asarray(v) for k, v in inputs.items()}

    def per_partition(a):
        return a.reshape(-1, P).T

    def rows_per_partition(a):
        return a.reshape(KD, P, -1).transpose(1, 0, 2).reshape(P, -1)

    def pack(gate, up, down):
        def chunks(w):
            e, rows, n = w.shape
            return w.reshape(e, rows // P, P, n).transpose(0, 2, 1, 3).reshape(e, P, -1)
        return np.concatenate([chunks(gate), chunks(up), chunks(down)], axis=2)

    arrays = {
        "x": i["x"].reshape(T, D),
        "ctx_t": i["ctx_1024"].reshape(B * SC, D).T,
        "cols": np.concatenate([
            per_partition(i["L0_xattn_bq"]), per_partition(i["L0_xattn_bk"]), per_partition(i["L0_ffn_b1"]),
            per_partition(i["L1_xattn_bq"]), per_partition(i["L1_xattn_bk"]),
            rows_per_partition(i["L0_ffn_router_w"]), rows_per_partition(i["L1_ffn_gate_w"].T)], axis=1),
        "rows": np.concatenate([i["L0_xattn_bv"], i["L0_xattn_bo"], i["L0_ffn_b2"], i["L1_xattn_bv"],
                                i["L1_xattn_bo"]]),
        "every": np.concatenate([i["g_xattn"], i["g_ffn"], i["L1_ffn_beta"]]),
        "wa0": np.stack([i["L0_xattn_Wq"], i["L0_xattn_Wk"], i["L0_xattn_Wv"], i["L0_xattn_Wo"]]),
        "w1": i["L0_ffn_w1"],
        "w2": i["L0_ffn_w2"],
        "wa1": np.stack([i["L1_xattn_wq"].T, i["L1_xattn_wk"].T, i["L1_xattn_wv"].T, i["L1_xattn_wo"].T]),
        "w_shared": pack(i["L1_ffn_shared_gate_w"], i["L1_ffn_shared_up_w"], i["L1_ffn_shared_down_w"])[0],
        "w_experts": pack(i["L1_ffn_gate_proj_w"], i["L1_ffn_up_proj_w"], i["L1_ffn_down_proj_w"]),
    }
    arrays = {k: np.ascontiguousarray(a) for k, a in arrays.items()}
    nc = bacc.Bacc("TRN2", target_bir_lowering=False, num_devices=1)
    aps = [nc.dram_tensor("in_" + k, a.shape, F32, kind="ExternalInput").ap() for k, a in arrays.items()]
    out = nc.dram_tensor("out_x", (T, D), F32, kind="ExternalOutput").ap()
    flamingo(nc, *aps, out)
    r = run_bass_kernel_spmd(nc, [{"in_" + k: a for k, a in arrays.items()}], core_ids=[0])
    return r.results[0]["out_x"].reshape(B, SEQ, D)
```
